# Optimizing a Trainium2 kernel written in Bass

```python
import numpy as np
import jax
import jax.numpy as jnp

def _softmax(x, axis=-1):
    return jax.nn.softmax(x, axis=axis)

def _gelu(x):
    return jax.nn.gelu(x, approximate=True)

def _silu(x):
    return jax.nn.silu(x)

def _sigmoid(x):
    return jax.nn.sigmoid(x)

def _layernorm(x, axis=-1, eps=1e-05):
    m = jnp.mean(x, axis=axis, keepdims=True)
    v = jnp.var(x, axis=axis, keepdims=True)
    return (x - m) / jnp.sqrt(v + eps)

def _scatter_add(tgt, idx, src, axis=0):
    return tgt.at[idx].add(src)

def _segment_sum(src, seg, n):
    return jax.ops.segment_sum(src, seg, n)
kernel_name = 'mk_decoder_postln_d2_seqx_r4_3d7e81'

def setup_inputs(seed: int=0):
    np.random.seed(seed)
    _w = jnp.asarray

    def _rec_inputs():
        import jax
        import jax.numpy as jnp
        _rk = jax.random.key(seed)
        x = -0.0002928 + 1 * jax.random.normal(jax.random.fold_in(_rk, 1), (8, 256, 256), jnp.float32)
        _lenS = 256 - jax.random.randint(jax.random.fold_in(_rk, 7), (8,), 0, max(1, 256 // 4) + 1, jnp.int32)
        _lenS2 = 77 - jax.random.randint(jax.random.fold_in(_rk, 8), (8,), 0, max(1, 77 // 4) + 1, jnp.int32)
        _ctx_1024P = jax.random.normal(jax.random.fold_in(_rk, 11), (8, 16, 256), jnp.float32)
        _ctx_1024c = jax.random.dirichlet(jax.random.fold_in(_rk, 511), 0.3 * jnp.ones((16,), jnp.float32), (8, 77))
        _ctx_1024t = jnp.einsum('bsk,bkd->bsd', _ctx_1024c, _ctx_1024P)
        _ctx_1024t = _ctx_1024t * jax.lax.rsqrt(jnp.mean(jnp.square(_ctx_1024t)) + 1e-12) * 0.953939
        ctx_1024 = 2.81802e-05 + 1.00001 * (_ctx_1024t + 0.3 * jax.random.normal(jax.random.fold_in(_rk, 611), (8, 77, 256), jnp.float32))
        _validS = jnp.arange(256)[None, :] < _lenS[:, None]
        _validS2 = jnp.arange(77)[None, :] < _lenS2[:, None]
        _causal = jnp.tril(jnp.ones((256, 256), dtype=bool))
        mask_BxS2_bk0 = jnp.logical_not(jnp.broadcast_to(_validS2[:, :], (8, 77)))
        mask_Bx1xSxS2_fk0 = jnp.where(jnp.broadcast_to(_validS2[:, None, None, :], (8, 1, 256, 77)), 0.0, 1.0).astype(jnp.float32)
        return (x, ctx_1024, mask_BxS2_bk0, mask_Bx1xSxS2_fk0)
    x, ctx_1024, mask_BxS2_bk0, mask_Bx1xSxS2_fk0 = _rec_inputs()

    def _L0_attn_setup():
        import jax, jax.numpy as jnp
        import numpy as np
        N_HEAD = 16
        HEAD_SIZE = 256
        EMBED = 256
        MULTI_HEAD_SIZE = HEAD_SIZE // N_HEAD
        B, S = (4, 512)
        key = jax.random.key(seed)
        k1, k2, k3, k4 = jax.random.split(key, 4)
        x = jax.random.normal(k1, (B, S, EMBED), dtype=jnp.float32)
        w_qkv = jax.random.normal(k2, (3 * HEAD_SIZE, EMBED), dtype=jnp.float32) * 0.02
        w_proj = jax.random.normal(k3, (EMBED, HEAD_SIZE), dtype=jnp.float32) * 0.02
        b_proj = jax.random.normal(k4, (EMBED,), dtype=jnp.float32) * 0.02
        return {'x': x, 'w_qkv': w_qkv, 'w_proj': w_proj, 'b_proj': b_proj}
    _L0_attn_all = _L0_attn_setup()
    _L0_attn_in = {k: v for k, v in _L0_attn_all.items() if k in ('w_qkv', 'w_proj', 'b_proj')}
    del _L0_attn_all

    def _L0_xattn_setup():
        import jax, jax.numpy as jnp
        import numpy as np
        NUM_HEADS = 16
        key = jax.random.key(seed)
        ks = jax.random.split(key, 7)
        B, Nq, Nkv, D = (4, 256, 1024, 256)
        q = jax.random.normal(ks[0], (B, Nq, D), dtype=jnp.float32)
        kv = jax.random.normal(ks[1], (B, Nkv, D), dtype=jnp.float32)
        mask = jax.random.randint(ks[2], (B, Nkv), 0, 2) > 0
        mask = mask.at[:, 0].set(False)
        s = D ** (-0.5)
        Wq = jax.random.normal(ks[3], (D, D), dtype=jnp.float32) * s
        Wkv = jax.random.normal(ks[4], (D, 2 * D), dtype=jnp.float32) * s
        Wproj = jax.random.normal(ks[5], (D, D), dtype=jnp.float32) * s
        bproj = jnp.zeros((D,), dtype=jnp.float32)
        return {'q': q, 'kv': kv, 'key_padding_mask': mask, 'Wq': Wq, 'Wkv': Wkv, 'Wproj': Wproj, 'bproj': bproj}
    _L0_xattn_all = _L0_xattn_setup()
    _L0_xattn_in = {k: v for k, v in _L0_xattn_all.items() if k in ('Wq', 'Wkv', 'Wproj', 'bproj')}
    del _L0_xattn_all

    def _L0_ffn_setup():
        import jax, jax.numpy as jnp
        import numpy as np
        MANT_BITS = 8
        _PWL_X = jnp.linspace(-4.0, 4.0, 33, dtype=jnp.float32)
        _PWL_Y = 0.5 * _PWL_X * (1.0 + jax.lax.erf(_PWL_X / jnp.sqrt(jnp.float32(2.0))))

        def float2fix(x, mantissa_bits):
            s = jnp.float32(2.0 ** mantissa_bits)
            q = jnp.round(x * s) / s
            return x + jax.lax.stop_gradient(q - x)

        def pwlin_gelu_basic(x, mantissa_bits_in, mantissa_bits_out):
            xq = float2fix(x, mantissa_bits_in)
            y = jnp.interp(xq, _PWL_X, _PWL_Y)
            y = jnp.where(xq > 4.0, xq, jnp.where(xq < -4.0, jnp.float32(0.0), y))
            return float2fix(y, mantissa_bits_out)
        key = jax.random.key(seed)
        k_x, k_w1, k_b1, k_w2, k_b2 = jax.random.split(key, 5)
        dim, ff_dim = (256, 1024)
        B, S = (32, 128)
        sc1 = 1.0 / np.sqrt(dim)
        sc2 = 1.0 / np.sqrt(ff_dim)
        return {'x': jax.random.normal(k_x, (B, S, dim), dtype=jnp.float32), 'w1': jax.random.uniform(k_w1, (dim, ff_dim), jnp.float32, -sc1, sc1), 'b1': jax.random.uniform(k_b1, (ff_dim,), jnp.float32, -sc1, sc1), 'w2': jax.random.uniform(k_w2, (ff_dim, dim), jnp.float32, -sc2, sc2), 'b2': jax.random.uniform(k_b2, (dim,), jnp.float32, -sc2, sc2)}
    _L0_ffn_all = _L0_ffn_setup()
    _L0_ffn_in = {k: v for k, v in _L0_ffn_all.items() if k in ('w1', 'b1', 'w2', 'b2')}
    del _L0_ffn_all

    def _L1_attn_setup():
        import jax, jax.numpy as jnp
        import numpy as np
        B, N, D = (4, 512, 256)
        H = 8
        DK = D // H
        DV = D // H
        DF = 2 * DK
        CHUNK = 64
        RMS_EPS = 1e-05

        def _hedgehog(x, w, b):
            y = jnp.einsum('bhnd,ed->bhne', x, w) + b
            return jnp.concatenate([jnp.exp(y), jnp.exp(-y)], axis=-1)

        def _fused_chunk_linear_attn(q, k, v):
            b, h, n, df = q.shape
            dv = v.shape[-1]
            nc = n // CHUNK

            def to_chunks(t):
                d = t.shape[-1]
                return t.reshape(b, h, nc, CHUNK, d).transpose(2, 0, 1, 3, 4)
            qc, kc, vc = (to_chunks(q), to_chunks(k), to_chunks(v))
            mask = jnp.tril(jnp.ones((CHUNK, CHUNK), dtype=bool))

            def step(S, inp):
                qi, ki, vi = inp
                attn = jnp.einsum('bhcd,bhed->bhce', qi, ki)
                attn = jnp.where(mask, attn, 0.0)
                intra = jnp.einsum('bhce,bhev->bhcv', attn, vi)
                inter = jnp.einsum('bhcd,bhdv->bhcv', qi, S)
                S = S + jnp.einsum('bhcd,bhcv->bhdv', ki, vi)
                return (S, intra + inter)
            S0 = jnp.zeros((b, h, df, dv), dtype=q.dtype)
            _, oc = jax.lax.scan(step, S0, (qc, kc, vc))
            return oc.transpose(1, 2, 0, 3, 4).reshape(b, h, n, dv)
        key = jax.random.key(seed)
        ks = jax.random.split(key, 10)
        s = D ** (-0.5)
        x = jax.random.normal(ks[0], (B, N, D), dtype=jnp.float32)
        Wq = jax.random.normal(ks[1], (D, D), dtype=jnp.float32) * s
        Wk = jax.random.normal(ks[2], (D, D), dtype=jnp.float32) * s
        Wv = jax.random.normal(ks[3], (D, D), dtype=jnp.float32) * s
        Wo = jax.random.normal(ks[4], (D, D), dtype=jnp.float32) * s
        eye = jnp.eye(DK, dtype=jnp.float32)
        fmq_w = eye + 0.02 * jax.random.normal(ks[5], (DK, DK), dtype=jnp.float32)
        fmq_b = 0.02 * jax.random.normal(ks[6], (DK,), dtype=jnp.float32)
        fmk_w = eye + 0.02 * jax.random.normal(ks[7], (DK, DK), dtype=jnp.float32)
        fmk_b = 0.02 * jax.random.normal(ks[8], (DK,), dtype=jnp.float32)
        rms_w = 1.0 + 0.1 * jax.random.normal(ks[9], (DV,), dtype=jnp.float32)
        return {'x': x, 'Wq': Wq, 'Wk': Wk, 'Wv': Wv, 'Wo': Wo, 'fmq_w': fmq_w, 'fmq_b': fmq_b, 'fmk_w': fmk_w, 'fmk_b': fmk_b, 'rms_w': rms_w}
    _L1_attn_all = _L1_attn_setup()
    _L1_attn_in = {k: v for k, v in _L1_attn_all.items() if k in ('Wq', 'Wk', 'Wv', 'Wo', 'fmq_w', 'fmq_b', 'fmk_w', 'fmk_b', 'rms_w')}
    del _L1_attn_all

    def _L1_xattn_setup():
        import jax, jax.numpy as jnp
        import numpy as np
        D_MODEL = 256
        NUM_HEADS = 16
        DEPTH = D_MODEL // NUM_HEADS
        B, S = (4, 512)

        def _split(t):
            b, s, _ = t.shape
            return t.reshape(b, s, NUM_HEADS, DEPTH).transpose(0, 2, 1, 3)
        key = jax.random.key(seed)
        ks = jax.random.split(key, 13)
        sd = 1.0 / np.sqrt(D_MODEL)
        inp = {'q_in': jax.random.normal(ks[0], (B, S, D_MODEL), jnp.float32), 'k_in': jax.random.normal(ks[1], (B, S, D_MODEL), jnp.float32), 'v_in': jax.random.normal(ks[2], (B, S, D_MODEL), jnp.float32), 'm_in': (jax.random.uniform(ks[3], (B, 1, S, S)) < 0.1).astype(jnp.float32), 'Wq': jax.random.normal(ks[4], (D_MODEL, D_MODEL), jnp.float32) * sd, 'bq': jax.random.normal(ks[5], (D_MODEL,), jnp.float32) * 0.01, 'Wk': jax.random.normal(ks[6], (D_MODEL, D_MODEL), jnp.float32) * sd, 'bk': jax.random.normal(ks[7], (D_MODEL,), jnp.float32) * 0.01, 'Wv': jax.random.normal(ks[8], (D_MODEL, D_MODEL), jnp.float32) * sd, 'bv': jax.random.normal(ks[9], (D_MODEL,), jnp.float32) * 0.01, 'Wo': jax.random.normal(ks[10], (D_MODEL, D_MODEL), jnp.float32) * sd, 'bo': jax.random.normal(ks[11], (D_MODEL,), jnp.float32) * 0.01}
        return inp
    _L1_xattn_all = _L1_xattn_setup()
    _L1_xattn_in = {k: v for k, v in _L1_xattn_all.items() if k in ('Wq', 'bq', 'Wk', 'bk', 'Wv', 'bv', 'Wo', 'bo')}
    del _L1_xattn_all

    def _L1_ffn_setup():
        import jax, jax.numpy as jnp
        import numpy as np
        EPS = 1e-05

        def _layernorm(x, w, b):
            mu = jnp.mean(x, axis=-1, keepdims=True)
            var = jnp.mean((x - mu) ** 2, axis=-1, keepdims=True)
            return (x - mu) * jax.lax.rsqrt(var + EPS) * w + b

        def _rope_tables(T, D, base=10000.0):
            inv_freq = 1.0 / base ** (jnp.arange(0, D, 2, dtype=jnp.float32) / D)
            t = jnp.arange(T, dtype=jnp.float32)
            freqs = jnp.einsum('i,j->ij', t, inv_freq)
            emb = jnp.concatenate([freqs, freqs], axis=-1)
            return (jnp.cos(emb), jnp.sin(emb))

        def _rotate_half(x):
            x1, x2 = (x[..., :x.shape[-1] // 2], x[..., x.shape[-1] // 2:])
            return jnp.concatenate([-x2, x1], axis=-1)

        def _attn(x, ln_w, ln_b, conv_w, attn_w, proj_w, n_head):
            B, T, C = x.shape
            D = C // n_head
            h = _layernorm(x, ln_w, ln_b)
            hc = jnp.transpose(h, (0, 2, 1))
            hc = jnp.pad(hc, ((0, 0), (0, 0), (2, 0)))
            hc = jax.lax.conv_general_dilated(hc, conv_w, window_strides=(1,), padding='VALID', dimension_numbers=('NCH', 'OIH', 'NCH'), feature_group_count=C)
            h = jnp.transpose(hc, (0, 2, 1))
            qkv = h @ attn_w
            q, k, v = jnp.split(qkv, 3, axis=-1)
            q = q.reshape(B, T, n_head, D)
            k = k.reshape(B, T, n_head, D)
            v = v.reshape(B, T, n_head, D)
            cos, sin = _rope_tables(T, D)
            cos = cos[None, :, None, :]
            sin = sin[None, :, None, :]
            q = q * cos + _rotate_half(q) * sin
            k = k * cos + _rotate_half(k) * sin
            scores = jnp.einsum('bqhd,bkhd->bhqk', q, k) / jnp.sqrt(jnp.float32(D))
            causal = jnp.tril(jnp.ones((T, T), dtype=bool))
            scores = jnp.where(causal, scores, jnp.float32(-1e+30))
            p = jax.nn.softmax(scores, axis=-1)
            y = jnp.einsum('bhqk,bkhd->bqhd', p, v).reshape(B, T, C)
            return y @ proj_w

        def _moe(x, ln_w, ln_b, router_w, expert_wv, expert_proj):
            h = _layernorm(x, ln_w, ln_b)
            logits = h @ router_w
            expert_idx = jnp.argmax(logits, axis=-1)
            E = router_w.shape[-1]
            out = jnp.zeros_like(x)
            for e in range(E):
                gv = h @ expert_wv[e]
                gate_raw, value = jnp.split(gv, 2, axis=-1)
                y = gate_raw * jax.nn.sigmoid(gate_raw) * value @ expert_proj[e]
                out = out + jnp.where((expert_idx == e)[..., None], y, 0.0)
            return out
        C, H, E, B, T = (256, 16, 4, 4, 256)
        Dff = 4 * C
        key = jax.random.key(seed)
        ks = jax.random.split(key, 8)
        s = 0.02
        return {'x': jax.random.normal(ks[0], (B, T, C), dtype=jnp.float32), 'ln1_w': jnp.ones((C,), jnp.float32), 'ln1_b': jnp.zeros((C,), jnp.float32), 'ln2_w': jnp.ones((C,), jnp.float32), 'ln2_b': jnp.zeros((C,), jnp.float32), 'conv_w': jax.random.normal(ks[1], (C, 1, 3), dtype=jnp.float32) * 0.1, 'attn_w': jax.random.normal(ks[2], (C, 3 * C), dtype=jnp.float32) * s, 'proj_w': jax.random.normal(ks[3], (C, C), dtype=jnp.float32) * s, 'router_w': jax.random.normal(ks[4], (C, E), dtype=jnp.float32) * s, 'expert_wv': jax.random.normal(ks[5], (E, C, 2 * Dff), dtype=jnp.float32) * s, 'expert_proj': jax.random.normal(ks[6], (E, Dff, C), dtype=jnp.float32) * s}
    _L1_ffn_all = _L1_ffn_setup()
    _L1_ffn_in = {k: v for k, v in _L1_ffn_all.items() if k in ('ln1_w', 'ln1_b', 'ln2_w', 'ln2_b', 'conv_w', 'attn_w', 'proj_w', 'router_w', 'expert_wv', 'expert_proj')}
    del _L1_ffn_all
    return {'x': x, 'ctx_1024': ctx_1024, 'mask_BxS2_bk0': mask_BxS2_bk0, 'mask_Bx1xSxS2_fk0': mask_Bx1xSxS2_fk0, 'L0_attn_w_qkv': _L0_attn_in['w_qkv'], 'L0_attn_w_proj': _L0_attn_in['w_proj'], 'L0_attn_b_proj': _L0_attn_in['b_proj'], 'L0_xattn_Wq': _L0_xattn_in['Wq'], 'L0_xattn_Wkv': _L0_xattn_in['Wkv'], 'L0_xattn_Wproj': _L0_xattn_in['Wproj'], 'L0_xattn_bproj': _L0_xattn_in['bproj'], 'L0_ffn_w1': _L0_ffn_in['w1'], 'L0_ffn_b1': _L0_ffn_in['b1'], 'L0_ffn_w2': _L0_ffn_in['w2'], 'L0_ffn_b2': _L0_ffn_in['b2'], 'L1_attn_Wq': _L1_attn_in['Wq'], 'L1_attn_Wk': _L1_attn_in['Wk'], 'L1_attn_Wv': _L1_attn_in['Wv'], 'L1_attn_Wo': _L1_attn_in['Wo'], 'L1_attn_fmq_w': _L1_attn_in['fmq_w'], 'L1_attn_fmq_b': _L1_attn_in['fmq_b'], 'L1_attn_fmk_w': _L1_attn_in['fmk_w'], 'L1_attn_fmk_b': _L1_attn_in['fmk_b'], 'L1_attn_rms_w': _L1_attn_in['rms_w'], 'L1_xattn_Wq': _L1_xattn_in['Wq'], 'L1_xattn_bq': _L1_xattn_in['bq'], 'L1_xattn_Wk': _L1_xattn_in['Wk'], 'L1_xattn_bk': _L1_xattn_in['bk'], 'L1_xattn_Wv': _L1_xattn_in['Wv'], 'L1_xattn_bv': _L1_xattn_in['bv'], 'L1_xattn_Wo': _L1_xattn_in['Wo'], 'L1_xattn_bo': _L1_xattn_in['bo'], 'L1_ffn_ln1_w': _L1_ffn_in['ln1_w'], 'L1_ffn_ln1_b': _L1_ffn_in['ln1_b'], 'L1_ffn_ln2_w': _L1_ffn_in['ln2_w'], 'L1_ffn_ln2_b': _L1_ffn_in['ln2_b'], 'L1_ffn_conv_w': _L1_ffn_in['conv_w'], 'L1_ffn_attn_w': _L1_ffn_in['attn_w'], 'L1_ffn_proj_w': _L1_ffn_in['proj_w'], 'L1_ffn_router_w': _L1_ffn_in['router_w'], 'L1_ffn_expert_wv': _L1_ffn_in['expert_wv'], 'L1_ffn_expert_proj': _L1_ffn_in['expert_proj']}

def reference(x, ctx_1024, mask_BxS2_bk0, mask_Bx1xSxS2_fk0, L0_attn_w_qkv, L0_attn_w_proj, L0_attn_b_proj, L0_xattn_Wq, L0_xattn_Wkv, L0_xattn_Wproj, L0_xattn_bproj, L0_ffn_w1, L0_ffn_b1, L0_ffn_w2, L0_ffn_b2, L1_attn_Wq, L1_attn_Wk, L1_attn_Wv, L1_attn_Wo, L1_attn_fmq_w, L1_attn_fmq_b, L1_attn_fmk_w, L1_attn_fmk_b, L1_attn_rms_w, L1_xattn_Wq, L1_xattn_bq, L1_xattn_Wk, L1_xattn_bk, L1_xattn_Wv, L1_xattn_bv, L1_xattn_Wo, L1_xattn_bo, L1_ffn_ln1_w, L1_ffn_ln1_b, L1_ffn_ln2_w, L1_ffn_ln2_b, L1_ffn_conv_w, L1_ffn_attn_w, L1_ffn_proj_w, L1_ffn_router_w, L1_ffn_expert_wv, L1_ffn_expert_proj):
    import jax
    import jax.numpy as jnp

    def _L0_attn_ref(x, w_qkv, w_proj, b_proj):
        import jax, jax.numpy as jnp
        import numpy as np
        N_HEAD = 16
        HEAD_SIZE = 256
        EMBED = 256
        MULTI_HEAD_SIZE = HEAD_SIZE // N_HEAD
        B, S = (4, 512)
        qkv = jnp.einsum('bse,he->bsh', x, w_qkv)
        q, k, v = jnp.split(qkv, 3, axis=-1)
        scale = 1.0 / np.sqrt(MULTI_HEAD_SIZE).astype(np.float32)
        scores = jnp.einsum('bqh,bkh->bqk', q, k) * scale
        probs = jax.nn.softmax(scores, axis=-1)
        out = jnp.einsum('bqk,bkh->bqh', probs, v)
        Bn, Sn, H = out.shape
        out = jnp.swapaxes(out, 1, 2).reshape(Bn, Sn, H)
        out = jnp.einsum('bsh,eh->bse', out, w_proj) + b_proj
        return out

    def _L0_xattn_ref(q, kv, key_padding_mask, Wq, Wkv, Wproj, bproj):
        import jax, jax.numpy as jnp
        import numpy as np
        NUM_HEADS = 16
        B, Nq, D = q.shape
        Nkv = kv.shape[1]
        H = NUM_HEADS
        hd = D // H
        scale = hd ** (-0.5)
        qp = (q @ Wq).reshape(B, Nq, H, hd).transpose(0, 2, 1, 3) * scale
        kvp = kv @ Wkv
        k = kvp[..., :D].reshape(B, Nkv, H, hd).transpose(0, 2, 1, 3)
        v = kvp[..., D:].reshape(B, Nkv, H, hd).transpose(0, 2, 1, 3)
        attn = jnp.einsum('bhqd,bhkd->bhqk', qp, k)
        neg_inf = jnp.finfo(attn.dtype).min
        attn = jnp.where(key_padding_mask[:, None, None, :], neg_inf, attn)
        attn = jax.nn.softmax(attn, axis=-1)
        x = jnp.einsum('bhqk,bhkd->bhqd', attn, v)
        x = x.transpose(0, 2, 1, 3).reshape(B, Nq, D)
        return x @ Wproj + bproj

    def _L0_ffn_ref(x, w1, b1, w2, b2):
        import jax, jax.numpy as jnp
        import numpy as np
        MANT_BITS = 8
        _PWL_X = jnp.linspace(-4.0, 4.0, 33, dtype=jnp.float32)
        _PWL_Y = 0.5 * _PWL_X * (1.0 + jax.lax.erf(_PWL_X / jnp.sqrt(jnp.float32(2.0))))

        def float2fix(x, mantissa_bits):
            s = jnp.float32(2.0 ** mantissa_bits)
            q = jnp.round(x * s) / s
            return x + jax.lax.stop_gradient(q - x)

        def pwlin_gelu_basic(x, mantissa_bits_in, mantissa_bits_out):
            xq = float2fix(x, mantissa_bits_in)
            y = jnp.interp(xq, _PWL_X, _PWL_Y)
            y = jnp.where(xq > 4.0, xq, jnp.where(xq < -4.0, jnp.float32(0.0), y))
            return float2fix(y, mantissa_bits_out)
        h = jnp.einsum('bsd,df->bsf', x, w1) + b1
        h = float2fix(h, MANT_BITS)
        h = pwlin_gelu_basic(h, MANT_BITS, MANT_BITS)
        h = float2fix(h, MANT_BITS)
        out = jnp.einsum('bsf,fd->bsd', h, w2) + b2
        return float2fix(out, MANT_BITS)

    def _L1_attn_ref(x, Wq, Wk, Wv, Wo, fmq_w, fmq_b, fmk_w, fmk_b, rms_w):
        import jax, jax.numpy as jnp
        import numpy as np
        B, N, D = (4, 512, 256)
        H = 8
        DK = D // H
        DV = D // H
        DF = 2 * DK
        CHUNK = 64
        RMS_EPS = 1e-05

        def _hedgehog(x, w, b):
            y = jnp.einsum('bhnd,ed->bhne', x, w) + b
            return jnp.concatenate([jnp.exp(y), jnp.exp(-y)], axis=-1)

        def _fused_chunk_linear_attn(q, k, v):
            b, h, n, df = q.shape
            dv = v.shape[-1]
            nc = n // CHUNK

            def to_chunks(t):
                d = t.shape[-1]
                return t.reshape(b, h, nc, CHUNK, d).transpose(2, 0, 1, 3, 4)
            qc, kc, vc = (to_chunks(q), to_chunks(k), to_chunks(v))
            mask = jnp.tril(jnp.ones((CHUNK, CHUNK), dtype=bool))

            def step(S, inp):
                qi, ki, vi = inp
                attn = jnp.einsum('bhcd,bhed->bhce', qi, ki)
                attn = jnp.where(mask, attn, 0.0)
                intra = jnp.einsum('bhce,bhev->bhcv', attn, vi)
                inter = jnp.einsum('bhcd,bhdv->bhcv', qi, S)
                S = S + jnp.einsum('bhcd,bhcv->bhdv', ki, vi)
                return (S, intra + inter)
            S0 = jnp.zeros((b, h, df, dv), dtype=q.dtype)
            _, oc = jax.lax.scan(step, S0, (qc, kc, vc))
            return oc.transpose(1, 2, 0, 3, 4).reshape(b, h, n, dv)
        b, n, d = x.shape
        split = lambda t: t.reshape(b, n, H, -1).transpose(0, 2, 1, 3)
        q = split(x @ Wq.T)
        k = split(x @ Wk.T)
        v = split(x @ Wv.T)
        q = _hedgehog(q, fmq_w, fmq_b)
        k = _hedgehog(k, fmk_w, fmk_b)
        scale = q.shape[-1] ** (-0.5)
        o = _fused_chunk_linear_attn(q * scale, k, v)
        o = o * jax.lax.rsqrt(jnp.mean(o * o, axis=-1, keepdims=True) + RMS_EPS) * rms_w
        o = o.transpose(0, 2, 1, 3).reshape(b, n, H * DV)
        return o @ Wo.T

    def _L1_xattn_ref(q_in, k_in, v_in, m_in, Wq, bq, Wk, bk, Wv, bv, Wo, bo):
        import jax, jax.numpy as jnp
        import numpy as np
        D_MODEL = 256
        NUM_HEADS = 16
        DEPTH = D_MODEL // NUM_HEADS
        B, S = (4, 512)

        def _split(t):
            b, s, _ = t.shape
            return t.reshape(b, s, NUM_HEADS, DEPTH).transpose(0, 2, 1, 3)
        q = _split(q_in @ Wq.T + bq)
        k = _split(k_in @ Wk.T + bk)
        v = _split(v_in @ Wv.T + bv)
        scale = jnp.sqrt(jnp.asarray(DEPTH, jnp.float32))
        scores = jnp.einsum('bhqd,bhkd->bhqk', q, k) / scale
        scores = scores - m_in * 1000000.0
        attn = jax.nn.softmax(scores, axis=-1)
        out = jnp.einsum('bhqk,bhkd->bhqd', attn, v)
        out = out.transpose(0, 2, 1, 3).reshape(q_in.shape[0], -1, D_MODEL)
        return out @ Wo.T + bo

    def _L1_ffn_ref(x, ln1_w, ln1_b, ln2_w, ln2_b, conv_w, attn_w, proj_w, router_w, expert_wv, expert_proj):
        import jax, jax.numpy as jnp
        import numpy as np
        EPS = 1e-05

        def _layernorm(x, w, b):
            mu = jnp.mean(x, axis=-1, keepdims=True)
            var = jnp.mean((x - mu) ** 2, axis=-1, keepdims=True)
            return (x - mu) * jax.lax.rsqrt(var + EPS) * w + b

        def _rope_tables(T, D, base=10000.0):
            inv_freq = 1.0 / base ** (jnp.arange(0, D, 2, dtype=jnp.float32) / D)
            t = jnp.arange(T, dtype=jnp.float32)
            freqs = jnp.einsum('i,j->ij', t, inv_freq)
            emb = jnp.concatenate([freqs, freqs], axis=-1)
            return (jnp.cos(emb), jnp.sin(emb))

        def _rotate_half(x):
            x1, x2 = (x[..., :x.shape[-1] // 2], x[..., x.shape[-1] // 2:])
            return jnp.concatenate([-x2, x1], axis=-1)

        def _attn(x, ln_w, ln_b, conv_w, attn_w, proj_w, n_head):
            B, T, C = x.shape
            D = C // n_head
            h = _layernorm(x, ln_w, ln_b)
            hc = jnp.transpose(h, (0, 2, 1))
            hc = jnp.pad(hc, ((0, 0), (0, 0), (2, 0)))
            hc = jax.lax.conv_general_dilated(hc, conv_w, window_strides=(1,), padding='VALID', dimension_numbers=('NCH', 'OIH', 'NCH'), feature_group_count=C)
            h = jnp.transpose(hc, (0, 2, 1))
            qkv = h @ attn_w
            q, k, v = jnp.split(qkv, 3, axis=-1)
            q = q.reshape(B, T, n_head, D)
            k = k.reshape(B, T, n_head, D)
            v = v.reshape(B, T, n_head, D)
            cos, sin = _rope_tables(T, D)
            cos = cos[None, :, None, :]
            sin = sin[None, :, None, :]
            q = q * cos + _rotate_half(q) * sin
            k = k * cos + _rotate_half(k) * sin
            scores = jnp.einsum('bqhd,bkhd->bhqk', q, k) / jnp.sqrt(jnp.float32(D))
            causal = jnp.tril(jnp.ones((T, T), dtype=bool))
            scores = jnp.where(causal, scores, jnp.float32(-1e+30))
            p = jax.nn.softmax(scores, axis=-1)
            y = jnp.einsum('bhqk,bkhd->bqhd', p, v).reshape(B, T, C)
            return y @ proj_w

        def _moe(x, ln_w, ln_b, router_w, expert_wv, expert_proj):
            h = _layernorm(x, ln_w, ln_b)
            logits = h @ router_w
            expert_idx = jnp.argmax(logits, axis=-1)
            E = router_w.shape[-1]
            out = jnp.zeros_like(x)
            for e in range(E):
                gv = h @ expert_wv[e]
                gate_raw, value = jnp.split(gv, 2, axis=-1)
                y = gate_raw * jax.nn.sigmoid(gate_raw) * value @ expert_proj[e]
                out = out + jnp.where((expert_idx == e)[..., None], y, 0.0)
            return out
        n_head = 16
        x = x + _attn(x, ln1_w, ln1_b, conv_w, attn_w, proj_w, n_head)
        x = x + _moe(x, ln2_w, ln2_b, router_w, expert_wv, expert_proj)
        return x
    x = _layernorm(x + _L0_attn_ref(x, L0_attn_w_qkv, L0_attn_w_proj, L0_attn_b_proj), axis=-1)
    x = _layernorm(x + _L0_xattn_ref(x, ctx_1024, mask_BxS2_bk0, L0_xattn_Wq, L0_xattn_Wkv, L0_xattn_Wproj, L0_xattn_bproj), axis=-1)
    x = _layernorm(x + _L0_ffn_ref(x, L0_ffn_w1, L0_ffn_b1, L0_ffn_w2, L0_ffn_b2), axis=-1)
    x = _layernorm(x + _L1_attn_ref(x, L1_attn_Wq, L1_attn_Wk, L1_attn_Wv, L1_attn_Wo, L1_attn_fmq_w, L1_attn_fmq_b, L1_attn_fmk_w, L1_attn_fmk_b, L1_attn_rms_w), axis=-1)
    x = _layernorm(x + _L1_xattn_ref(x, ctx_1024, ctx_1024, mask_Bx1xSxS2_fk0, L1_xattn_Wq, L1_xattn_bq, L1_xattn_Wk, L1_xattn_bk, L1_xattn_Wv, L1_xattn_bv, L1_xattn_Wo, L1_xattn_bo), axis=-1)
    x = _layernorm(x + _L1_ffn_ref(x, L1_ffn_ln1_w, L1_ffn_ln1_b, L1_ffn_ln2_w, L1_ffn_ln2_b, L1_ffn_conv_w, L1_ffn_attn_w, L1_ffn_proj_w, L1_ffn_router_w, L1_ffn_expert_wv, L1_ffn_expert_proj), axis=-1)
    return x

_drawn_inputs = setup_inputs


def setup_inputs(seed=0):
    import zlib

    import numpy as np

    out = dict(_drawn_inputs(seed))
    spreads = {'L0_xattn_bproj': (0.0, 0.1),
     'L1_ffn_ln1_w': (1.0, 0.6),
     'L1_ffn_ln1_b': (0.0, 0.8),
     'L1_ffn_ln2_w': (1.0, 0.6),
     'L1_ffn_ln2_b': (0.0, 0.8)}
    factors = {'L0_attn_w_qkv': 8.0,
     'L0_attn_w_proj': 8.0,
     'L0_ffn_b1': 3.315,
     'L1_attn_fmq_b': 8.0,
     'L1_attn_fmk_b': 8.0,
     'L1_xattn_bq': 8.0,
     'L1_xattn_bk': 8.0,
     'L1_xattn_bv': 6.038,
     'L1_xattn_bo': 6.359,
     'L1_ffn_conv_w': 6.905,
     'L1_ffn_attn_w': 7.007,
     'L1_ffn_proj_w': 7.293,
     'L1_ffn_router_w': 3.768,
     'L1_ffn_expert_wv': 3.18,
     'L1_ffn_expert_proj': 3.151}
    for name, (base, spread) in spreads.items():
        noise = np.random.default_rng([zlib.crc32(name.encode()), seed]).standard_normal(out[name].shape)
        drawn = base * np.exp(spread * noise) if base else spread * noise
        out[name] = jnp.asarray(drawn.astype(out[name].dtype))
    for name, factor in factors.items():
        out[name] = (out[name] * factor).astype(out[name].dtype)
    return out
```

```python
from contextlib import ExitStack

import numpy as np

import concourse.bass as bass
from concourse import mybir

F32 = mybir.dt.float32
BF16 = mybir.dt.bfloat16
I32 = mybir.dt.int32
U8 = mybir.dt.uint8
ALU = mybir.AluOpType
ACT = mybir.ActivationFunctionType
AX = mybir.AxisListType.X

P = 128
B, S, D, C = 8, 256, 256, 77
KT = D // P
TT = S // P
H, HD = 16, 16
H1, HD1 = 8, 32
FF0 = 1024
E, FFE = 4, 1024
N = B * S
NT = N // P
TILES = NT + E - 1
ROWS = TILES * P
PARTS = 6
KS = PARTS * HD
W = KS + 2
EPS = 1e-5
DVE_LINKS = 94
MAGIC = 1.5 * 2.0 ** 23
NEG = -3.3895313892515355e38
FLT_MAX = 3.4028234663852886e38

CF = {}
_o = 0
for _n, _w in (("ident", P), ("allow", S), ("upper", P), ("ones", P), ("block", P), ("onesexp", 64),
               ("cos", TT * HD), ("sin", TT * HD), ("pm", 1), ("half", 4), ("kth", NT), ("tile", TILES),
               ("token", NT), ("quarter", 1)):
    CF[_n] = (_o, _w)
    _o += _w
CF_N = _o
CB = {"ident": (0, P), "neg_qk": (P, S), "neg_kq": (P + S, S), "sel": (P + 2 * S, H * P)}
CB_N = P + 2 * S + H * P


NORMS = ("a0", "x0", "f", "l", "x1", "n1", "n2")
SOFTMAX = ("x0", "x1", "m")
TURNS = {"moments": NORMS, "variance": NORMS, "rstd": NORMS, "normed": NORMS[:5], "residual": ("a0", "x0", "x1"),
         "y": ("a0", "x0", "f", "l", "x1", "m"), "transposed": ("a0", "x0", "f", "l", "m"),
         "xT": ("start", "a0", "x0", "f", "l"), "qkv": ("a0", "x0", "x1", "m"), "oT": ("x0", "l", "x1", "m"),
         "scores0": ("x0", "l", "x1", "m"), "scores1": ("x0", "l", "x1", "m")}
for _n in ("q32 k32 q_part1 k_part1 v q_rest k_rest q_part2 k_part2 q_stack k_stack q_copies k_copies q_transposed "
           "k_transposed qT_act qT_dve kT_act kT_dve minus_max max_transposed mT pv scores_t0 scores_t1 max0 max1 "
           "exp0 exp1").split():
    TURNS[_n] = SOFTMAX


def turn_of(name):
    stage, _, thing = name.partition("_")
    if thing in TURNS and stage in TURNS[thing]:
        return thing, TURNS[thing].index(stage), len(TURNS[thing])
    return name, 0, 1


def settler(sem):
    def settled_wait(engine, signal, value):
        engine.wait_ge(signal, value)
        engine.sem_inc(sem("passed"), 1)
    return settled_wait


class Count:

    def __init__(self, engine, i):
        self.bases = {n: engine.snap(2 * n * i) for n in (1, 3, 4, 5, 6, 7)}
        self.j = 0

    def slot(self, j):
        other = Count.__new__(Count)
        other.bases, other.j = self.bases, j
        return other

    def __call__(self, name):
        _, k, n = turn_of(name)
        return self.bases[n] + (2 * k + self.j + 1)


def shape_constants():
    f = np.zeros((P, CF_N), np.float32)

    def put(name, value):
        o, w = CF[name]
        f[:, o:o + w] = value

    r, c = np.arange(P)[:, None], np.arange(P)[None, :]
    put("ident", r == c)
    put("allow", np.where(r <= np.arange(S)[None, :], (2 * HD1) ** -0.5, 0.0))
    put("upper", r < c)
    put("ones", 1.0)
    put("block", r // HD1 == c // HD1)
    put("onesexp", np.concatenate([np.arange(32) < 16, np.arange(32) >= 16])[None, :])
    inv = (1.0 / np.float32(10000.0) ** (np.arange(0, HD, 2, dtype=np.float32) / np.float32(HD))).astype(np.float32)
    ang = (np.arange(S, dtype=np.float32)[:, None] * inv[None, :]).astype(np.float32)
    cos, sin = np.cos(ang), np.sin(ang)
    tiled = lambda a: a.reshape(TT, P, HD).transpose(1, 0, 2).reshape(P, TT * HD)
    put("cos", tiled(np.concatenate([cos, cos], 1)))
    put("sin", tiled(np.concatenate([-sin, sin], 1)))
    put("pm", np.where(r // HD1 % 2 == 0, 1.0, -1.0))
    put("half", -0.5)
    put("kth", np.arange(NT)[None, :] * float(P))
    put("tile", np.arange(TILES)[None, :])
    put("token", np.arange(NT)[None, :] * P + r)
    put("quarter", 0.25)
    b = np.zeros((P, CB_N), np.float32)
    b[:, 0:P] = r == c
    b[:, P + P:P + S] = np.where(c > r, -1e30, 0.0)
    b[:, P + S:P + S + P] = np.where(r > c, -1e30, 0.0)
    sel = np.zeros((P, H, P), np.float32)
    for part in range(2):
        for h in range(H):
            sel[part * H + h, h, :] = 1.0
    b[:, P + 2 * S:] = sel.reshape(P, H * P)
    return f, b.astype(mybir.dt.np(BF16))


def decoder(nc, a, out):
    ctx = ExitStack()
    with ctx:
        def sb(name, shape, dt=F32, stack=ctx):
            return stack.enter_context(nc.sbuf_tensor(name, shape, dt))

        sems = {}

        def sem(name):
            name = turn_of(name)[0]
            if name not in sems:
                sems[name] = ctx.enter_context(nc.semaphore(name))
            return sems[name]

        residual_dram = nc.dram_tensor("residual_rows", (N, D), F32, kind="Internal").ap()
        h2_dram = nc.dram_tensor("h2_rows", (N, D), F32, kind="Internal").ap()
        token_dram = nc.dram_tensor("token_of_row", (ROWS, 1), I32, kind="Internal").ap()

        cf = sb("cf", [P, CF_N])
        cb = sb("cb", [P, CB_N], BF16)
        logits = sb("logits", [P, NT, E])

        def const(name, rows=P):
            o, w = CF[name]
            return cf[0:rows, o:o + w]

        identb = cb[:, 0:P]
        neg_qk = cb[:, P:P + S]
        neg_kq = cb[:, P + S:P + 2 * S]
        selh = cb[:, P + 2 * S:].rearrange("p (h k) -> p h k", h=H)
        ident = const("ident")

        ps = [ctx.enter_context(nc.psum_tensor(f"ps{j}", [P, 2048], F32)) for j in range(2)]
        psb = [t[:, :].bitcast(BF16) for t in ps]

        part_one(nc, a, ctx, sb, sem, ps, psb, const, identb, neg_qk, neg_kq, selh, ident, cf, cb,
                 logits, residual_dram, h2_dram)
        part_two(nc, a, ctx, sb, sem, ps, const, ident, logits, residual_dram, h2_dram, token_dram, out)


def part_one(nc, a, ctx, sb0, sem, ps, psb, const, identb, neg_qk, neg_kq, selh, ident, cf, cb,
             logits, residual_dram, h2_dram):
    with ExitStack() as one:
        def sb(name, shape, dt=F32):
            return sb0(name, shape, dt, one)

        wt = {}
        for name, rows, cols in (("a0_qkv", D, 3 * D), ("a0_proj", D, D), ("x0_q", D, D), ("x0_kv", D, 2 * D),
                                 ("x0_proj", D, D), ("f_w1", D, FF0), ("f_w2", FF0, D),
                                 ("a1_v", D, D), ("a1_o", D, D), ("x1_q", D, D), ("x1_k", D, D), ("x1_v", D, D),
                                 ("x1_o", D, D), ("m_qkv", D, 3 * D), ("m_proj", D, D)):
            wt[name] = sb("w_" + name, [P, rows // P, cols])
        wf = {s: sb(f"wf_{s}", [P, KT, 2 * D]) for s in "qk"}
        rows_of = {}
        for name in ("a0_b", "x0_b", "f_b2", "x1_bq", "x1_bk", "x1_bv", "x1_bo", "m_ln2_w", "m_ln2_b"):
            rows_of[name] = sb("r_" + name, [P, D])
        f_b1 = sb("f_b1", [P, FF0 // P])
        fmb = {s: sb(f"fmb_{s}", [P, 1]) for s in "qk"}
        rmsw = sb("rmsw", [P, 1])
        ln1w = sb("ln1w", [P, KT])
        ln1b = sb("ln1b", [P, KT])
        convw = sb("convw", [P, KT, 3])
        routw = sb("routw", [P, E, D])

        two = range(2)
        xin = [sb(f"xin{j}", [P, TT, D]) for j in two]
        cin = [sb(f"cin{j}", [C, D]) for j in two]
        bkin = [sb(f"bkin{j}", [C, 1], U8) for j in two]
        fkin = [sb(f"fkin{j}", [P, TT, C]) for j in two]
        ctxT = [sb(f"ctxT{j}", [P, KT, C]) for j in two]
        bkneg = [sb(f"bkneg{j}", [C, 1]) for j in two]
        fk4 = [sb(f"fk4{j}", [P, TT, C]) for j in two]
        fk4T = [sb(f"fk4T{j}", [C, S]) for j in two]
        x = [sb(f"x{j}", [P, TT, D]) for j in two]
        xb = [sb(f"xb{j}", [P, TT, D]) for j in two]
        r = [sb(f"r{j}", [P, TT, D]) for j in two]
        xT = [sb(f"xT{j}", [P, KT, S]) for j in two]
        bn = [sb(f"bn{j}", [P, TT, 6]) for j in two]
        mv = [sb(f"mv{j}", [P, TT, 2]) for j in two]
        rstd = [sb(f"rstd{j}", [P, TT]) for j in two]
        mx = [sb(f"mx{j}", [P, TT, H]) for j in two]
        mn = [sb(f"mn{j}", [P, TT, P], BF16) for j in two]
        mT = [sb(f"mT{j}", [P, S], BF16) for j in two]
        oT = [sb(f"oT{j}", [P, 512]) for j in two]
        rden = [t[:, :, :].rearrange("p t n -> p (t n)") for t in r]
        vexp = [sb(f"vexp{j}", [P, TT, H * 32]) for j in two]
        big = [sb(f"big{j}", [P, 6144]) for j in two]
        qkT = [sb(f"qkT{j}", [P, 2, H, S], BF16) for j in two]
        lg = [sb(f"lg{j}", [P, TT * E]) for j in two]
        setup_dma = sem("weights_loaded")
        settled_wait = settler(sem)

        loads = []

        def queue(dst, src):
            loads.append((dst, src))

        queue(cf[:, :], a["cf"])
        queue(cb[:, :], a["cb"])
        for name, t in wt.items():
            queue(t[:, :, :], a[name].rearrange("(t p) n -> p t n", p=P))
        for name, t in rows_of.items():
            queue(t[:, :], a[name].rearrange("(o n) -> o n", o=1).broadcast_to([P, D]))
        queue(f_b1[:, :], a["f_b1"])
        queue(ln1w[:, :], a["m_ln1_w"])
        queue(ln1b[:, :], a["m_ln1_b"])
        queue(convw[:, :, :], a["m_conv"])
        for e in range(E):
            queue(routw[:, e, :], a["m_router"][e:e + 1, :].broadcast_to([P, D]))
        raw_w = {s: big[0][:, 512 * i:512 * i + 512].rearrange("p (t n) -> p t n", t=KT) for i, s in enumerate("qk")}
        diag = {s: big[0][:, 1024 + P * i:1024 + P * i + P] for i, s in enumerate("qk")}
        for s in "qk":
            queue(raw_w[s], a[f"a1_{s}"].rearrange("(t p) n -> p t n", p=P))
            for g in range(4):
                queue(fmb[s][32 * g:32 * g + 32, :], a[f"a1_fm{s}_b"].rearrange("(n o) -> n o", o=1))
        for g in range(4):
            queue(rmsw[32 * g:32 * g + 32, :], a["a1_rms"].rearrange("(n o) -> n o", o=1))
        diag_loads = [(diag[s][32 * g:32 * g + 32, 32 * g:32 * g + 32], a[f"a1_fm{s}T"])
                      for s in "qk" for g in range(4)]
        LOADED = 16 * (len(loads) + len(diag_loads))

        block = one.enter_context(nc.Block())

        def tiles2(ap, n):
            return ap.rearrange("p (t n) -> p t n", n=n)

        def stack_view(j, which):
            o = which * 3136
            t = big[j][:, o // 2:o // 2 + TT * H * W // 2].bitcast(BF16)
            g = t.rearrange("p (g w) -> p g w", w=W)
            return g, g[:, :, 0:KS].rearrange("p g (a d) -> p g a d", d=HD)

        def qk32(j, which):
            o = 3136 + 512 * which
            return big[j][:, o:o + 512]

        def qk32_both(j):
            return big[j][:, 3136:3136 + 1024]

        def rope_tmp(j, i):
            o = 5184 if i == 0 else 4160
            return big[j][:, o:o + 512]

        def rem(j, which):
            o = 4160 + 512 * which
            return big[j][:, o:o + 512]

        def probs(j, kb):
            if kb == 0:
                return big[j][:, 0:4096].rearrange("p (h q) -> p h q", h=H)
            return big[j][:, 4096:6144].rearrange("p (h q) -> p h q", h=H)

        vview = [t[:, :, :].rearrange("p t (g w) -> p t g w", w=64) for t in vexp]
        onesexp = const("onesexp").rearrange("p (a w) -> p a w", a=2)

        ffn = [[big[j][:, 2048 * i:2048 * i + 2048] for i in range(3)]
               + [qkT[j][:, i, :, :].rearrange("p h s -> p (h s)").bitcast(F32) for i in range(2)] for j in two]
        qF = [big[j][:, 0:1024].rearrange("p (m s) -> p m s", m=4) for j in two]
        kF = [big[j][:, 1024:3072].rearrange("p (m a s) -> p m a s", m=4, a=2) for j in two]
        aT = [[big[j][:, 3072:5120].rearrange("p (h q) -> p h q", h=H1),
               big[j][:, 5120:6144].rearrange("p (h q) -> p h q", h=H1)] for j in two]
        v1 = [qkT[j][:, 0, :, :].rearrange("p h s -> p (h s)").bitcast(F32)[:, 0:512] for j in two]
        sq1 = [qkT[j][:, 0, :, :].rearrange("p h s -> p (h s)").bitcast(F32)[:, 512:1024] for j in two]
        qT0 = [big[j][:, 0:512].rearrange("p (t s) -> p t s", t=KT) for j in two]
        kT0 = [big[j][:, 512:1024].rearrange("p (t s) -> p t s", t=KT) for j in two]
        v0 = [big[j][:, 1024:1536].rearrange("p (t s) -> p t s", t=TT) for j in two]
        p0 = [big[j][:, 1536:2048].rearrange("p (t s) -> p t s", t=TT) for j in two]
        p0T = [big[j][:, 2048:2560].rearrange("p (t s) -> p t s", t=TT) for j in two]
        o0 = [big[j][:, 2560:3072].rearrange("p (t s) -> p t s", t=TT) for j in two]
        sm0 = [big[j][:, 3072:3080] for j in two]
        ms = [big[j][:, 0:H * C].rearrange("p (a b c) -> p a b c", a=4, b=4) for j in two]
        hpad = [big[j][:, 0:2 * (S + 2)].rearrange("p (t s) -> p t s", t=KT) for j in two]
        h1n = [big[j][:, 1024:1536].rearrange("p (t s) -> p t s", t=TT) for j in two]

        @block.tensor
        def _(pe):
            pe.wait_ge(setup_dma, LOADED)
            for i, s in enumerate("qk"):
                for t in range(KT):
                    for g in range(KT):
                        mm = pe.matmul(ps[0][:, 512 * i + 256 * t + P * g:512 * i + 256 * t + P * g + P],
                                       raw_w[s][:, g, P * t:P * t + P], diag[s], start=True, stop=True)
            mm.then_inc(sem("folded_maps"), 1)
            pe.wait_ge(sem("setup_act"), 1)
            pe.wait_ge(sem("setup_pool"), 1)

            def transposed(src, dst, signal):
                for kt in range(KT):
                    for tt in range(TT):
                        mm = pe.transpose(dst[:, kt * S + tt * P:kt * S + tt * P + P],
                                          src[:, tt, kt * P:kt * P + P], ident)
                mm.then_inc(signal, 1)

            def rows_product(dst, lhs, weight, cols, signal=None):
                n = cols.stop - cols.start
                for tt in range(TT):
                    for kt in range(KT):
                        mm = pe.matmul(dst[:, tt * n:tt * n + n], lhs[:, kt, tt * P:tt * P + P],
                                       weight[:, kt, cols], start=kt == 0, stop=kt == KT - 1)
                if signal is not None:
                    mm.then_inc(signal, 1)

            def start(j, n, it):
                pe.wait_ge(sem(f"inputs_loaded{j}"), it)
                transposed(xin[j], ps[j], sem("x_transposed"))
                for kt in range(KT):
                    mm = pe.transpose(ps[j][:, 512 + kt * C:512 + kt * C + C], cin[j][:, kt * P:kt * P + P],
                                      ident[0:C, 0:C])
                pe.wait_ge(sem("fk4"), n("fk4"))
                for tt in range(TT):
                    mm = pe.transpose(ps[j][0:C, 1024 + tt * P:1024 + tt * P + P], fk4[j][:, tt, :], ident)
                mm.then_inc(sem("ctx_transposed"), 1)

            def a0_qkv(j, n):
                pe.wait_ge(sem("start_xT"), n("start_xT"))
                pe.wait_ge(sem("start_ctxT"), n("start_ctxT"))
                w = wt["a0_qkv"]
                for i in range(2):
                    for m in range(KT):
                        for kt in range(KT):
                            mm = pe.matmul(ps[j][:, 512 * i + S * m:512 * i + S * m + S],
                                           w[:, kt, D * i + P * m:D * i + P * m + P], xT[j][:, kt, :],
                                           start=kt == 0, stop=kt == KT - 1)
                rows_product(ps[j][:, 1024:1536], xT[j], w, slice(2 * D, 3 * D), sem("a0_qkv"))

            def a0_scores(j, n):
                pe.wait_ge(sem("a0_qT"), n("a0_qT"))
                pe.wait_ge(sem("a0_kT_v"), n("a0_kT_v"))
                for tt in range(TT):
                    for kt in range(KT):
                        mm = pe.matmul(ps[j][:, tt * S:tt * S + S], qT0[j][:, kt, tt * P:tt * P + P],
                                       kT0[j][:, kt, :], start=kt == 0, stop=kt == KT - 1)
                mm.then_inc(sem("a0_scores"), 1)

            def a0_pT(j, n):
                pe.wait_ge(sem("a0_exp"), n("a0_exp"))
                transposed(p0[j], ps[j], sem("a0_p_transposed"))

            def a0_pv(j, n):
                pe.wait_ge(sem("a0_pT"), n("a0_pT"))
                rows_product(ps[j][:, 0:512], p0T[j], v0[j], slice(0, D), sem("a0_pv"))

            def a0_proj(j, n):
                pe.wait_ge(sem("a0_o"), n("a0_o"))
                rows_product(ps[j][:, 0:512], o0[j], wt["a0_proj"], slice(0, D), sem("a0_y"))

            def x_transposes(s):
                def step(j, n):
                    pe.wait_ge(sem(f"{s}_normed"), n(f"{s}_normed"))
                    transposed(x[j], ps[j], sem(f"{s}_transposed"))
                return step

            def cross_qkv(s, wq, wk, wv, prev):
                def step(j, n):
                    pe.wait_ge(sem(f"{prev}_xT"), n(f"{prev}_xT"))
                    rows_product(ps[j][:, 0:512], xT[j], wq, slice(0, D))
                    for i, w in enumerate((wk, wv)):
                        for kt in range(KT):
                            mm = pe.matmul(ps[j][0:C, 512 + 512 * i:512 + 512 * i + D], ctxT[j][:, kt, :],
                                           w[:, kt, 0:D], start=kt == 0, stop=kt == KT - 1)
                    mm.then_inc(sem(f"{s}_qkv"), 1)
                return step

            def causal_qkv(j, n):
                pe.wait_ge(sem("m_conv"), n("m_conv"))
                rows_product(ps[j][:, 0:1024], xT[j], wt["m_qkv"], slice(0, 2 * D))
                rows_product(ps[j][:, 1024:1536], xT[j], wt["m_qkv"], slice(2 * D, 3 * D), sem("m_qkv"))

            def q_transposes(s, rows):
                def step(j, n):
                    pe.wait_ge(sem(f"{s}_q_stack"), n(f"{s}_q_stack"))
                    pe.wait_ge(sem(f"{s}_q_copies"), n(f"{s}_q_copies"))
                    pe.wait_ge(sem(f"{s}_v"), n(f"{s}_v"))
                    pe.wait_ge(sem(f"{s}_k_stack"), n(f"{s}_k_stack"))
                    g, _ = stack_view(j, 0)
                    for h in range(H):
                        for tt in range(TT):
                            mm = pe.transpose(psb[j][0:rows, h * S + tt * P:h * S + tt * P + P],
                                              g[:, tt * H + h, 0:rows], identb)
                    mm.then_inc(sem(f"{s}_q_transposed"), 1)
                return step

            def k_transposes(s, rows, cross):
                def step(j, n):
                    pe.wait_ge(sem(f"{s}_k_copies"), n(f"{s}_k_copies"))
                    pe.wait_ge(sem(f"{s}_qT_act"), n(f"{s}_qT_act"))
                    pe.wait_ge(sem(f"{s}_qT_dve"), n(f"{s}_qT_dve"))
                    g, _ = stack_view(j, 1)
                    for h in range(H):
                        if cross:
                            mm = pe.transpose(psb[j][0:rows, h * S:h * S + C], g[0:C, h, 0:rows],
                                              identb[0:C, 0:C])
                        else:
                            for tt in range(TT):
                                mm = pe.transpose(psb[j][0:rows, h * S + tt * P:h * S + tt * P + P],
                                                  g[:, tt * H + h, 0:rows], identb)
                    mm.then_inc(sem(f"{s}_k_transposed"), 1)
                return step

            def cross_scores(s, rows, tt):
                def step(j, n):
                    if tt == 0:
                        pe.wait_ge(sem(f"{s}_kT_act"), n(f"{s}_kT_act"))
                        pe.wait_ge(sem(f"{s}_kT_dve"), n(f"{s}_kT_dve"))
                    else:
                        pe.wait_ge(sem(f"{s}_max0"), n(f"{s}_max0"))
                    for h in range(H):
                        o = 512 * (h // 4) + C * (h % 4)
                        mm = pe.matmul(ps[j][:, o:o + C], qkT[j][0:rows, 0, h, tt * P:tt * P + P],
                                       qkT[j][0:rows, 1, h, 0:C], start=True, stop=True)
                    mm.then_inc(sem(f"{s}_scores{tt}"), 1)
                return step

            def causal_scores(part):
                def step(j, n):
                    if part == 0:
                        pe.wait_ge(sem("m_kT_act"), n("m_kT_act"))
                        pe.wait_ge(sem("m_kT_dve"), n("m_kT_dve"))
                    else:
                        pe.wait_ge(sem(f"m_max{part - 1}"), n(f"m_max{part - 1}"))
                    heads, tt, nk = (8, 1, S) if part < 2 else (16, 0, P)
                    per = 512 // nk
                    neg = neg_qk if part < 2 else neg_qk[:, P:S]
                    for bank in range(4):
                        bk = ps[j][:, 512 * bank:512 * bank + 512]
                        pe.matmul(bk.rearrange("p (a k) -> p a k", a=per), identb,
                                  neg.unsqueeze(1).broadcast_to([P, per, nk]), start=True, stop=False)
                        for i in range(per):
                            h = (8 * part if part < 2 else 0) + bank * per + i
                            mm = pe.matmul(bk[:, nk * i:nk * i + nk], qkT[j][0:KS, 0, h, tt * P:tt * P + P],
                                           qkT[j][0:KS, 1, h, 0:nk], start=False, stop=i == per - 1)
                    mm.then_inc(sem(f"m_scores{part}"), 1)
                return step

            def max_transposes(s):
                def step(j, n):
                    pe.wait_ge(sem(f"{s}_minus_max"), n(f"{s}_minus_max"))
                    for tt in range(TT):
                        mm = pe.transpose(psb[j][:, tt * P:tt * P + P], mn[j][:, tt, :], identb)
                    mm.then_inc(sem(f"{s}_max_transposed"), 1)
                return step

            def cross_scores_t(s, rows, part):
                def step(j, n):
                    pe.wait_ge(sem(f"{s}_mT" if part == 0 else f"{s}_exp0"), n(f"{s}_mT" if part == 0 else f"{s}_exp0"))
                    for i in range(8):
                        h = 8 * part + i
                        pe.matmul(ps[j][0:C, S * i:S * i + S], qkT[j][0:rows, 1, h, 0:C],
                                  qkT[j][0:rows, 0, h, :], start=True, stop=False)
                        mm = pe.matmul(ps[j][0:C, S * i:S * i + S], selh[:, h, 0:C], mT[j][:, :],
                                       start=False, stop=True)
                    mm.then_inc(sem(f"{s}_scores_t{part}"), 1)
                return step

            def causal_scores_t(part):
                def step(j, n):
                    pe.wait_ge(sem("m_mT" if part == 0 else f"m_exp{part - 1}"), n("m_mT" if part == 0 else f"m_exp{part - 1}"))
                    kb, q0 = (0, 0) if part < 2 else (1, P)
                    nq = S - q0
                    per = 512 // nq
                    for bank in range(4):
                        bk = ps[j][:, 512 * bank:512 * bank + 512]
                        pe.matmul(bk.rearrange("p (a k) -> p a k", a=per), identb,
                                  neg_kq[:, 0:nq].unsqueeze(1).broadcast_to([P, per, nq]), start=True, stop=False)
                        for i in range(per):
                            h = (8 * part if part < 2 else 0) + bank * per + i
                            o = bk[:, nq * i:nq * i + nq]
                            pe.matmul(o, qkT[j][0:KS, 1, h, kb * P:kb * P + P], qkT[j][0:KS, 0, h, q0:S],
                                      start=False, stop=False)
                            mm = pe.matmul(o, selh[:, h, :], mT[j][:, q0:S], start=False, stop=i == per - 1)
                    mm.then_inc(sem(f"m_scores_t{part}"), 1)
                return step

            def weigh_values(s, cross):
                def step(j, n):
                    pe.wait_ge(sem(f"{s}_exp{1 if cross else 2}"), n(f"{s}_exp{1 if cross else 2}"))
                    kbs = ((0, 0, C),) if cross else ((0, 0, P), (1, P, P))
                    for bank in range(2):
                        for half in range(2):
                            todo = [(par, kb) for kb in kbs for par in range(2)]
                            for i, (par, (kb, q0, nk)) in enumerate(todo):
                                for strip in range(4):
                                    h = 8 * half + 2 * strip + par
                                    lhs = (vexp[j][0:nk, kb, 32 * h:32 * h + 32] if bank == 0
                                           else onesexp[0:nk, par, :])
                                    mm = pe.matmul(
                                        ps[j][32 * strip:32 * strip + 32,
                                              512 * bank + S * half + q0:512 * bank + S * half + S],
                                        lhs, probs(j, kb)[0:nk, h, :], start=i == 0, stop=i == len(todo) - 1)
                    mm.then_inc(sem(f"{s}_pv"), 1)
                return step

            def out_proj(s, w):
                def step(j, n):
                    pe.wait_ge(sem(f"{s}_oT"), n(f"{s}_oT"))
                    rows_product(ps[j][:, 0:512], oT[j][:, :].rearrange("p (t s) -> p t s", t=2), w,
                                 slice(0, D), sem(f"{s}_y"))
                return step

            def f_up(j, n):
                pe.wait_ge(sem("x0_xT"), n("x0_xT"))
                for m in range(FF0 // P):
                    for kt in range(KT):
                        mm = pe.matmul(ps[j][:, S * m:S * m + S], wt["f_w1"][:, kt, P * m:P * m + P],
                                       xT[j][:, kt, :], start=kt == 0, stop=kt == KT - 1)
                mm.then_inc(sem("f_h"), 1)

            def f_down(j, n):
                pe.wait_ge(sem("f_hT"), n("f_hT"))
                h = ffn[j][0].rearrange("p (m s) -> p m s", s=S)
                for tt in range(TT):
                    for m in range(FF0 // P):
                        mm = pe.matmul(ps[j][:, tt * D:tt * D + D], h[:, m, tt * P:tt * P + P],
                                       wt["f_w2"][:, m, :], start=m == 0, stop=m == FF0 // P - 1)
                mm.then_inc(sem("f_y"), 1)

            def l_features(j, n):
                pe.wait_ge(sem("f_xT"), n("f_xT"))
                for i, s in enumerate("qk"):
                    for m in range(4):
                        for kt in range(KT):
                            mm = pe.matmul(ps[j][:, 1024 * i + S * m:1024 * i + S * m + S],
                                           wf[s][:, kt, P * m:P * m + P], xT[j][:, kt, :],
                                           start=kt == 0, stop=kt == KT - 1)
                mm.then_inc(sem("l_maps"), 1)

            def l_scores0(j, n):
                pe.wait_ge(sem("l_features"), n("l_features"))
                for h in range(H1):
                    mm = pe.matmul(ps[j][:, S * h:S * h + S], kF[j][:, h // 2, h % 2, 0:P],
                                   qF[j][:, h // 2, :], start=True, stop=True)
                mm.then_inc(sem("l_scores0"), 1)

            def l_scores1(j, n):
                pe.wait_ge(sem("l_masked0"), n("l_masked0"))
                for h in range(H1):
                    mm = pe.matmul(ps[j][:, P * h:P * h + P], kF[j][:, h // 2, h % 2, P:S],
                                   qF[j][:, h // 2, P:S], start=True, stop=True)
                mm.then_inc(sem("l_scores1"), 1)
                rows_product(ps[j][:, 1024:1536], xT[j], wt["a1_v"], slice(0, D), sem("l_v_product"))

            def l_values(j, n):
                pe.wait_ge(sem("l_masked1"), n("l_masked1"))
                pe.wait_ge(sem("l_v"), n("l_v"))
                for half in range(2):
                    for kb, q0 in ((0, 0), (1, P)):
                        for strip in range(4):
                            h = 4 * half + strip
                            mm = pe.matmul(ps[j][32 * strip:32 * strip + 32, S * half + q0:S * half + S],
                                           v1[j][:, kb * D + 32 * h:kb * D + 32 * h + 32],
                                           aT[j][kb][:, h, :], start=kb == 0, stop=kb == 1)
                mm.then_inc(sem("l_o"), 1)

            def l_squares(j, n):
                pe.wait_ge(sem("l_squared"), n("l_squared"))
                pe.matmul(ps[j][:, 512:1024], const("block"), sq1[j], start=True, stop=True)\
                    .then_inc(sem("l_square_sums"), 1)

            def m_transposes(j, n):
                pe.wait_ge(sem("m_h"), n("m_h"))
                transposed(h1n[j], ps[j], sem("m_transposed"))

            with pe.Fori(0, B // 2) as i:
                counts = Count(pe, i)
                ns = [counts.slot(j) for j in two]
                it = pe.snap(64 * i + 64)
                for j in two:
                    start(j, ns[j], it)
                steps = [a0_qkv, a0_scores, a0_pT, a0_pv, a0_proj, x_transposes("a0")]
                steps += [cross_qkv("x0", wt["x0_q"], wt["x0_kv"], wt["x0_kv"][:, :, D:2 * D], "a0"),
                          q_transposes("x0", KS + 1), k_transposes("x0", KS + 1, True),
                          cross_scores("x0", KS + 1, 0), cross_scores("x0", KS + 1, 1), max_transposes("x0"),
                          cross_scores_t("x0", KS + 1, 0), cross_scores_t("x0", KS + 1, 1),
                          weigh_values("x0", True), out_proj("x0", wt["x0_proj"]), x_transposes("x0")]
                steps += [f_up, f_down, x_transposes("f")]
                steps += [l_features, l_scores0, l_scores1, l_values, l_squares,
                          out_proj("l", wt["a1_o"]), x_transposes("l")]
                steps += [cross_qkv("x1", wt["x1_q"], wt["x1_k"], wt["x1_v"], "l"),
                          q_transposes("x1", KS), k_transposes("x1", KS, True),
                          cross_scores("x1", KS, 0), cross_scores("x1", KS, 1), max_transposes("x1"),
                          cross_scores_t("x1", KS, 0), cross_scores_t("x1", KS, 1),
                          weigh_values("x1", True), out_proj("x1", wt["x1_o"])]
                steps += [m_transposes, causal_qkv, q_transposes("m", KS), k_transposes("m", KS, False),
                          causal_scores(0), causal_scores(1), causal_scores(2), max_transposes("m"),
                          causal_scores_t(0), causal_scores_t(1), causal_scores_t(2),
                          weigh_values("m", False), out_proj("m", wt["m_proj"])]
                for step in steps:
                    for j in two:
                        step(j, ns[j])
                for j in two:
                    pe.wait_ge(sem("m_x"), ns[j]("m_x"))

        @block.scalar
        def _(act):
            act.wait_ge(sem("folded_maps"), 1)
            for i, s in enumerate("qk"):
                for t in range(KT):
                    for dup in range(2):
                        src = ps[0][:, 512 * i + 256 * t:512 * i + 256 * t + 256].rearrange("p (h e) -> p h e", e=32)
                        dst = wf[s][:, t, :].rearrange("p (h a e) -> p h a e", a=2, e=32)[:, :, dup, :]
                        last = act.activation(dst, src, ACT.Copy)
            last.then_inc(sem("setup_act"), 1)
            act.wait_ge(sem("setup_pool"), 1)

            def copy_xT(s, signal):
                def step(j, n):
                    act.wait_ge(sem(f"{s}_transposed"), n(f"{s}_transposed"))
                    act.activation(xT[j][:, :, :].rearrange("p t s -> p (t s)"), ps[j][:, 0:512], ACT.Copy)\
                        .then_inc(sem(signal), 1)
                return step

            def a0_qT(j, n):
                act.wait_ge(sem("a0_qkv"), n("a0_qkv"))
                act.activation(big[j][:, 0:512], ps[j][:, 0:512], ACT.Copy).then_inc(sem("a0_qT"), 1)

            def a0_exp(j, n):
                act.wait_ge(sem("a0_minus_max"), n("a0_minus_max"))
                for tt in range(TT):
                    last = act.activation(p0[j][:, tt, :], ps[j][:, tt * S:tt * S + S], ACT.Exp,
                                          bias=sm0[j][:, tt:tt + 1], scale=HD ** -0.5,
                                          accum_out=sm0[j][:, 2 + tt:3 + tt])
                last.then_inc(sem("a0_exp"), 1)

            def a0_pT(j, n):
                act.wait_ge(sem("a0_p_transposed"), n("a0_p_transposed"))
                act.activation(big[j][:, 2048:2560], ps[j][:, 0:512], ACT.Copy).then_inc(sem("a0_pT"), 1)

            def stacks(s, cross):
                def step(j, n):
                    for which, c in ((0, "q"), (1, "k")):
                        rows = C if cross and which else P
                        g = H if cross and which else TT * H
                        _, st = stack_view(j, which)
                        first, second = (0, 2) if which == 0 else (0, 1)
                        src = qk32(j, which).rearrange("p (g d) -> p g d", d=HD)
                        act.wait_ge(sem(f"{s}_{c}32"), n(f"{s}_{c}32"))
                        act.activation(st[0:rows, 0:g, first, :], src[0:rows, 0:g, :], ACT.Copy)\
                            .then_inc(sem(f"{s}_{c}_part1"), 1)
                    act.wait_ge(sem(f"{s}_qkv"), n(f"{s}_qkv"))
                    rows = C if cross else P
                    nt = 1 if cross else TT
                    vp = ps[j][0:rows, 1024:1024 + nt * D].rearrange("p (t g a d) -> p t g a d", t=nt, a=2, d=HD)
                    if s == "x1":
                        act.wait_ge(sem("x1_v32"), n("x1_v32"))
                        vp = rden[j][0:rows, 0:D].rearrange("p (t g a d) -> p t g a d", t=nt, a=2, d=HD)
                    for t in range(nt):
                        act.activation(vview[j][0:rows, t, :, 0:16], vp[:, t, :, 0, :], ACT.Copy)
                        last = act.activation(vview[j][0:rows, t, :, 48:64], vp[:, t, :, 1, :], ACT.Copy)
                    last.then_inc(sem(f"{s}_v"), 1)
                    for which, c in ((0, "q"), (1, "k")):
                        rows = C if cross and which else P
                        g = H if cross and which else TT * H
                        _, st = stack_view(j, which)
                        second = 2 if which == 0 else 1
                        act.wait_ge(sem(f"{s}_{c}_rest"), n(f"{s}_{c}_rest"))
                        src = rem(j, which).rearrange("p (g d) -> p g d", d=HD)
                        act.activation(st[0:rows, 0:g, second, :], src[0:rows, 0:g, :], ACT.Copy)\
                            .then_inc(sem(f"{s}_{c}_part2"), 1)
                return step

            def qT_copy(s, rows):
                def step(j, n):
                    act.wait_ge(sem(f"{s}_q_transposed"), n(f"{s}_q_transposed"))
                    act.activation(qkT[j][0:rows, 0, 0:8, :].rearrange("p h s -> p (h s)"),
                                   psb[j][0:rows, 0:2048], ACT.Copy).then_inc(sem(f"{s}_qT_act"), 1)
                return step

            def kT_copy(s, rows, cross):
                def step(j, n):
                    act.wait_ge(sem(f"{s}_k_transposed"), n(f"{s}_k_transposed"))
                    nk = C if cross else S
                    act.activation(qkT[j][0:rows, 1, 0:8, 0:nk],
                                   psb[j][0:rows, 0:2048].rearrange("p (h s) -> p h s", s=S)[:, :, 0:nk],
                                   ACT.Copy).then_inc(sem(f"{s}_kT_act"), 1)
                return step

            def x0_exp(part):
                def step(j, n):
                    act.wait_ge(sem(f"x0_scores_t{part}"), n(f"x0_scores_t{part}"))
                    act.activation(probs(j, 0)[0:C, 8 * part:8 * part + 8, :].rearrange("p h q -> p (h q)"),
                                   ps[j][0:C, :], ACT.Exp, scale=HD ** -0.5).then_inc(sem(f"x0_exp{part}"), 1)
                return step

            def x1_exp(part):
                def step(j, n):
                    act.wait_ge(sem(f"x1_masked_t{part}"), n(f"x1_masked_t{part}"))
                    p = probs(j, 0)[0:C, 8 * part:8 * part + 8, :].rearrange("p h q -> p (h q)")
                    act.activation(p, p, ACT.Exp, scale=HD ** -0.5).then_inc(sem(f"x1_exp{part}"), 1)
                return step

            def m_exp(part):
                def step(j, n):
                    act.wait_ge(sem(f"m_scores_t{part}"), n(f"m_scores_t{part}"))
                    act.activation(big[j][:, 2048 * part:2048 * part + 2048], ps[j][:, :], ACT.Exp,
                                   scale=HD ** -0.5).then_inc(sem(f"m_exp{part}"), 1)
                return step

            def f_bias(j, n):
                act.wait_ge(sem("f_h"), n("f_h"))
                for m in range(FF0 // P):
                    last = act.activation(ffn[j][0][:, S * m:S * m + S], ps[j][:, S * m:S * m + S],
                                          ACT.Identity, bias=f_b1[:, m:m + 1], scale=256.0)
                last.then_inc(sem("f_h256"), 1)

            def f_gelu(j, n):
                act.wait_ge(sem("f_index"), n("f_index"))
                act.activation(ffn[j][3], ffn[j][1], ACT.Gelu, scale=0.25).then_inc(sem("f_left"), 1)
                act.activation(ffn[j][4], ffn[j][1], ACT.Gelu, bias=const("quarter"), scale=0.25)\
                    .then_inc(sem("f_right"), 1)

            def l_features(j, n):
                act.wait_ge(sem("l_maps"), n("l_maps"))
                act.activation(big[j][:, 0:1024], ps[j][:, 0:1024], ACT.Exp, bias=fmb["q"][:, :],
                               scale=const("pm"))
                act.wait_ge(sem("l_zeros"), n("l_zeros"))
                for s in range(2):
                    rows = slice(64 * s, 64 * s + 64)
                    last = act.activation(kF[j][rows, :, s, :],
                                          ps[j][rows, 1024:2048].rearrange("p (m s) -> p m s", s=S), ACT.Exp,
                                          bias=fmb["k"][rows, :], scale=const("pm")[rows, :])
                last.then_inc(sem("l_features"), 1)

            def l_v(j, n):
                act.wait_ge(sem("l_v_product"), n("l_v_product"))
                act.activation(v1[j], ps[j][:, 1024:1536], ACT.Copy).then_inc(sem("l_v"), 1)

            def l_square(j, n):
                act.wait_ge(sem("l_o"), n("l_o"))
                act.activation(sq1[j], ps[j][:, 0:512], ACT.Square).then_inc(sem("l_squared"), 1)

            def l_rms(j, n):
                act.wait_ge(sem("l_mean_square"), n("l_mean_square"))
                act.activation(rden[j][:, :], rden[j][:, :], ACT.Ln).then_inc(sem("l_ln"), 1)
                act.wait_ge(sem("l_ln"), n("l_ln"))
                act.activation(rden[j][:, :], rden[j][:, :], ACT.Exp, scale=-0.5).then_inc(sem("l_rms"), 1)

            def m_affine(j, n):
                act.wait_ge(sem("m_transposed"), n("m_transposed"))
                act.wait_ge(sem("m_pad"), n("m_pad"))
                for kt in range(KT):
                    last = act.activation(hpad[j][:, kt, 2:S + 2], ps[j][:, kt * S:kt * S + S], ACT.Identity,
                                          bias=ln1b[:, kt:kt + 1], scale=ln1w[:, kt:kt + 1])
                last.then_inc(sem("m_affine"), 1)

            def start_ctx(j, n):
                act.wait_ge(sem("x_transposed"), n("x_transposed"))
                act.activation(xT[j][:, :, :].rearrange("p t s -> p (t s)"), ps[j][:, 0:512], ACT.Copy)\
                    .then_inc(sem("start_xT"), 1)
                act.wait_ge(sem("ctx_transposed"), n("ctx_transposed"))
                act.activation(ctxT[j][:, :, :].rearrange("p t s -> p (t s)"), ps[j][:, 512:512 + KT * C], ACT.Copy)
                act.activation(fk4T[j][:, :], ps[j][0:C, 1024:1024 + S], ACT.Copy)\
                    .then_inc(sem("start_ctxT"), 1)

            with act.Fori(0, B // 2) as i:
                counts = Count(act, i)
                ns = [counts.slot(j) for j in two]
                steps = [start_ctx, a0_qT, a0_exp, a0_pT, copy_xT("a0", "a0_xT"),
                         stacks("x0", True), qT_copy("x0", KS + 1), kT_copy("x0", KS + 1, True),
                         x0_exp(0), x0_exp(1), copy_xT("x0", "x0_xT"),
                         f_bias, f_gelu, copy_xT("f", "f_xT"),
                         l_features, l_v, l_square, l_rms, copy_xT("l", "l_xT"),
                         stacks("x1", True), qT_copy("x1", KS), kT_copy("x1", KS, True), x1_exp(0), x1_exp(1),
                         m_affine, stacks("m", False), qT_copy("m", KS), kT_copy("m", KS, False),
                         m_exp(0), m_exp(1), m_exp(2)]
                for step in steps:
                    for j in two:
                        step(j, ns[j])

        @block.vector
        def _(dve):
            dve.wait_ge(setup_dma, LOADED)
            for j in two:
                dve.memset(vexp[j][:, :, :], 0.0)
                dve.memset(mn[j][:, :, :], 0.0)
            dve.tensor_scalar(f_b1[:, :], f_b1[:, :], 256.0, None, ALU.mult)
            for s in "qk":
                dve.tensor_scalar(fmb[s][:, :], fmb[s][:, :], const("pm"), None, ALU.mult)
            dve.tensor_scalar(rows_of["f_b2"][:, :], rows_of["f_b2"][:, :], 256.0, None, ALU.mult)\
                .then_inc(sem("setup_dve"), 1)
            dve.wait_ge(sem("setup_dve"), 1)
            dve.wait_ge(sem("setup_act"), 1)
            dve.wait_ge(sem("setup_pool"), 1)

            chain = {"base": None, "n": 0}

            def link(ins, held=False):
                chain["n"] += 1
                ins.then_inc(sem("dve_chain"), 1)
                if held:
                    settled_wait(dve, sem("dve_chain"), chain["base"] + chain["n"])
                else:
                    dve.wait_ge(sem("dve_chain"), chain["base"] + chain["n"])

            def moments(s, j):
                for tt in range(TT):
                    ins = dve.bn_stats(bn[j][:, tt, :], r[j][:, tt, :])
                link(ins, True)
                for tt in range(TT):
                    ins = dve.bn_aggr(mv[j][:, tt, :], bn[j][:, tt, :])
                ins.then_inc(sem(f"{s}_moments"), 1)

            def normalised(s, j, n, dst, signal):
                dve.wait_ge(sem(f"{s}_rstd"), n(f"{s}_rstd"))
                for tt in range(TT):
                    ins = dve.tensor_scalar(dst[:, tt, :], r[j][:, tt, :], mv[j][:, tt, 0:1], rstd[j][:, tt:tt + 1],
                                            ALU.subtract, ALU.mult)
                ins.then_inc(sem(signal), 1)

            def flat(t):
                return t[:, :, :].rearrange("p t n -> p (t n)")

            def add_norm(s, residual_signal, residual):
                def step(j, n):
                    dve.wait_ge(sem(f"{s}_y"), n(f"{s}_y"))
                    if residual_signal:
                        dve.wait_ge(sem(residual_signal), n(residual_signal))
                    link(dve.tensor_tensor(flat(r[j]), ps[j][:, 0:512], flat(residual[j]), ALU.add))
                    moments(s, j)
                    normalised(s, j, n, x[j], f"{s}_normed")
                return step

            def a0_kv(j, n):
                dve.wait_ge(sem("a0_qkv"), n("a0_qkv"))
                dve.tensor_copy(big[j][:, 512:1536], ps[j][:, 512:1536]).then_inc(sem("a0_kT_v"), 1)

            def a0_max(j, n):
                dve.wait_ge(sem("a0_scores"), n("a0_scores"))
                link(dve.tensor_reduce(sm0[j][:, 4:6], tiles2(ps[j][:, 0:512], S), AX, ALU.max))
                dve.tensor_scalar(sm0[j][:, 0:2], sm0[j][:, 4:6], -HD ** -0.5, None, ALU.mult)\
                    .then_inc(sem("a0_minus_max"), 1)

            def a0_o(j, n):
                dve.wait_ge(sem("a0_pv"), n("a0_pv"))
                link(dve.reciprocal(sm0[j][:, 6:8], sm0[j][:, 2:4]))
                for tt in range(TT):
                    ins = dve.tensor_scalar(o0[j][:, tt, :], ps[j][:, tt * S:tt * S + S], sm0[j][:, 6 + tt:7 + tt],
                                            None, ALU.mult)
                ins.then_inc(sem("a0_o"), 1)

            def cross_qk32(s):
                def step(j, n):
                    dve.wait_ge(sem(f"{s}_qkv"), n(f"{s}_qkv"))
                    if s == "x0":
                        dve.tensor_copy(qk32(j, 0), ps[j][:, 0:512]).then_inc(sem("x0_q32"), 1)
                        dve.tensor_copy(qk32(j, 1)[0:C, 0:D], ps[j][0:C, 512:512 + D]).then_inc(sem("x0_k32"), 1)
                    else:
                        bq = rows_of["x1_bq"][:, :].unsqueeze(1).broadcast_to([P, TT, D])
                        dve.tensor_tensor(tiles2(qk32(j, 0), D), tiles2(ps[j][:, 0:512], D), bq, ALU.add)\
                            .then_inc(sem("x1_q32"), 1)
                        dve.tensor_tensor(qk32(j, 1)[0:C, 0:D], ps[j][0:C, 512:512 + D],
                                          rows_of["x1_bk"][0:C, :], ALU.add).then_inc(sem("x1_k32"), 1)
                        dve.tensor_tensor(rden[j][0:C, 0:D], ps[j][0:C, 1024:1024 + D],
                                          rows_of["x1_bv"][0:C, :], ALU.add).then_inc(sem("x1_v32"), 1)
                return step

            def rope(j, n):
                dve.wait_ge(sem("m_qkv"), n("m_qkv"))
                co = const("cos").rearrange("p (t d) -> p t d", t=TT).unsqueeze(2).broadcast_to([P, TT, H, HD])
                si = const("sin").rearrange("p (t d) -> p t d", t=TT).unsqueeze(2).broadcast_to([P, TT, H, HD])
                hd = HD // 2
                heads = lambda t: t.rearrange("p (t g d) -> p t g d", t=TT, d=HD)
                for which, c in ((0, "q"), (1, "k")):
                    src = ps[j][:, 0:1024].rearrange("p (t w g d) -> p t w g d", t=TT, w=2, d=HD)[:, :, which]
                    straight, turned = heads(rope_tmp(j, which)), heads((oT, rden)[which][j][:, :])
                    dve.tensor_tensor(straight, src, co, ALU.mult)
                    dve.tensor_tensor(turned[:, :, :, 0:hd], src[:, :, :, hd:HD], si[:, :, :, 0:hd], ALU.mult)
                    link(dve.tensor_tensor(turned[:, :, :, hd:HD], src[:, :, :, 0:hd], si[:, :, :, hd:HD], ALU.mult))
                    dve.tensor_tensor(heads(qk32(j, which)), straight, turned, ALU.add)\
                        .then_inc(sem(f"m_{c}32"), 1)

            def rests(s, cross):
                def step(j, n):
                    for which, c in ((0, "q"), (1, "k")):
                        rows = C if cross and which else P
                        g = H if cross and which else TT * H
                        _, st = stack_view(j, which)
                        src = qk32(j, which).rearrange("p (g d) -> p g d", d=HD)[0:rows, 0:g, :]
                        rest = rem(j, which).rearrange("p (g d) -> p g d", d=HD)[0:rows, 0:g, :]
                        dve.wait_ge(sem(f"{s}_{c}_part1"), n(f"{s}_{c}_part1"))
                        dve.tensor_tensor(rest, src, st[0:rows, 0:g, 0, :], ALU.subtract)\
                            .then_inc(sem(f"{s}_{c}_rest"), 1)
                    for which, c in ((0, "q"), (1, "k")):
                        rows = C if cross and which else P
                        g = H if cross and which else TT * H
                        _, st = stack_view(j, which)
                        rest = rem(j, which).rearrange("p (g d) -> p g d", d=HD)[0:rows, 0:g, :]
                        second, third = (2, 5) if which == 0 else (1, 4)
                        dve.wait_ge(sem(f"{s}_{c}_part2"), n(f"{s}_{c}_part2"))
                        dve.tensor_tensor(st[0:rows, 0:g, third, :], rest, st[0:rows, 0:g, second, :],
                                          ALU.subtract).then_inc(sem(f"{s}_{c}_stack"), 1)
                return step

            def qT_copy(s, rows):
                def step(j, n):
                    dve.wait_ge(sem(f"{s}_q_transposed"), n(f"{s}_q_transposed"))
                    dve.tensor_copy(qkT[j][0:rows, 0, 8:16, :].rearrange("p h s -> p (h s)"),
                                    psb[j][0:rows, 2048:4096]).then_inc(sem(f"{s}_qT_dve"), 1)
                return step

            def kT_copy(s, rows, cross):
                def step(j, n):
                    dve.wait_ge(sem(f"{s}_k_transposed"), n(f"{s}_k_transposed"))
                    nk = C if cross else S
                    dve.tensor_copy(qkT[j][0:rows, 1, 8:16, 0:nk],
                                    psb[j][0:rows, 2048:4096].rearrange("p (h s) -> p h s", s=S)[:, :, 0:nk])\
                        .then_inc(sem(f"{s}_kT_dve"), 1)
                return step

            def minus_max(s, j, n):
                dve.wait_ge(sem(f"{s}_max{1 if s != 'm' else 2}"), n(f"{s}_max{1 if s != 'm' else 2}"))
                link(dve.tensor_scalar(mn[j][:, :, 0:H], mx[j][:, :, :], -1.0, None, ALU.mult))
                dve.scalar_tensor_tensor(out=mn[j][:, :, H:2 * H], in0=mx[j][:, :, :], scalar=-1.0,
                                         in1=mn[j][:, :, 0:H], op0=ALU.mult, op1=ALU.subtract)\
                    .then_inc(sem(f"{s}_minus_max"), 1)

            def cross_max(s, tt):
                def step(j, n):
                    dve.wait_ge(sem(f"{s}_scores{tt}"), n(f"{s}_scores{tt}"))
                    sc = ps[j][:, :].rearrange("p (a k) -> p a k", a=4)[:, :, 0:4 * C]\
                        .rearrange("p a (b c) -> p a b c", c=C)
                    if s == "x1":
                        mask = fk4[j][:, tt, :].unsqueeze(1).unsqueeze(1).broadcast_to([P, 4, 4, C])
                        link(dve.tensor_tensor(ms[j], sc, mask, ALU.add))
                        sc = ms[j]
                    dve.tensor_reduce(mx[j][:, tt, :].rearrange("p (a b) -> p a b", a=4), sc, AX, ALU.max)\
                        .then_inc(sem(f"{s}_max{tt}"), 1)
                    if tt == 1:
                        minus_max(s, j, n)
                return step

            def causal_max(part):
                def step(j, n):
                    dve.wait_ge(sem(f"m_scores{part}"), n(f"m_scores{part}"))
                    dst = mx[j][:, 1, 8 * part:8 * part + 8] if part < 2 else mx[j][:, 0, :]
                    dve.tensor_reduce(dst, tiles2(ps[j][:, :], S if part < 2 else P), AX, ALU.max)\
                        .then_inc(sem(f"m_max{part}"), 1)
                    if part == 2:
                        minus_max("m", j, n)
                return step

            def mT_copy(s):
                def step(j, n):
                    dve.wait_ge(sem(f"{s}_max_transposed"), n(f"{s}_max_transposed"))
                    dve.tensor_copy(mT[j][:, :], psb[j][:, 0:S]).then_inc(sem(f"{s}_mT"), 1)
                return step

            def x1_mask(part):
                def step(j, n):
                    dve.wait_ge(sem(f"x1_scores_t{part}"), n(f"x1_scores_t{part}"))
                    mask = fk4T[j][:, :].unsqueeze(1).broadcast_to([C, 8, S])
                    dve.tensor_tensor(probs(j, 0)[0:C, 8 * part:8 * part + 8, :],
                                      ps[j][0:C, :].rearrange("p (h q) -> p h q", q=S), mask, ALU.add)\
                        .then_inc(sem(f"x1_masked_t{part}"), 1)
                return step

            def divided(s):
                def step(j, n):
                    dve.wait_ge(sem(f"{s}_pv"), n(f"{s}_pv"))
                    link(dve.reciprocal(rden[j][:, :], ps[j][:, 512:1024]))
                    dve.tensor_tensor(oT[j][:, :], ps[j][:, 0:512], rden[j][:, :], ALU.mult)\
                        .then_inc(sem(f"{s}_oT"), 1)
                return step

            def f_round(j, n):
                k, idx, t = ffn[j][0], ffn[j][1], ffn[j][2]
                dve.wait_ge(sem("f_h256"), n("f_h256"))
                link(dve.tensor_scalar(k, k, MAGIC, MAGIC, ALU.add, ALU.subtract))
                link(dve.tensor_scalar(t, k, -1024.0, 1024.0, ALU.max, ALU.min))
                link(dve.tensor_scalar(idx, t, 1.0 / 64, -63.0 / 128, ALU.mult, ALU.add))
                dve.tensor_scalar(idx, idx, MAGIC, MAGIC, ALU.add, ALU.subtract).then_inc(sem("f_index"), 1)

            def f_interpolate(j, n):
                k, idx, t, left, right = ffn[j]
                dve.wait_ge(sem("f_index"), n("f_index"))
                link(dve.scalar_tensor_tensor(out=t, in0=t, scalar=1.0 / 64, in1=idx, op0=ALU.mult, op1=ALU.subtract))
                dve.wait_ge(sem("f_right"), n("f_right"))
                link(dve.tensor_tensor(right, right, left, ALU.subtract))
                link(dve.tensor_tensor(right, right, t, ALU.mult))
                link(dve.tensor_tensor(right, right, left, ALU.add))
                link(dve.tensor_scalar(right, right, 256.0, MAGIC, ALU.mult, ALU.add))
                link(dve.tensor_scalar(k, k, 1024.0, 0.0, ALU.subtract, ALU.max))
                dve.scalar_tensor_tensor(out=k, in0=right, scalar=MAGIC, in1=k, op0=ALU.subtract, op1=ALU.add)\
                    .then_inc(sem("f_hT"), 1)

            def f_norm(j, n):
                dve.wait_ge(sem("f_y"), n("f_y"))
                b2 = rows_of["f_b2"][:, :].unsqueeze(1).broadcast_to([P, TT, D])
                link(dve.tensor_tensor(r[j][:, :, :], tiles2(ps[j][:, 0:512], D), b2, ALU.add))
                link(dve.tensor_scalar(flat(r[j]), flat(r[j]), MAGIC, MAGIC, ALU.add, ALU.subtract))
                link(dve.scalar_tensor_tensor(out=flat(r[j]), in0=flat(r[j]), scalar=1.0 / 256, in1=flat(x[j]),
                                              op0=ALU.mult, op1=ALU.add))
                moments("f", j)
                normalised("f", j, n, x[j], "f_normed")

            def l_mask(kb):
                def step(j, n):
                    dve.wait_ge(sem(f"l_scores{kb}"), n(f"l_scores{kb}"))
                    nq = S if kb == 0 else P
                    allow = const("allow")[:, 0:nq].unsqueeze(1).broadcast_to([P, H1, nq])
                    src = ps[j][:, 0:H1 * nq].rearrange("p (h q) -> p h q", q=nq)
                    dve.scalar_tensor_tensor(out=aT[j][kb], in0=src, scalar=FLT_MAX, in1=allow, op0=ALU.min,
                                             op1=ALU.mult).then_inc(sem(f"l_masked{kb}"), 1)
                return step

            def l_mean(j, n):
                dve.wait_ge(sem("l_square_sums"), n("l_square_sums"))
                dve.tensor_scalar(rden[j][:, :], ps[j][:, 512:1024], 1.0 / HD1, EPS, ALU.mult, ALU.add)\
                    .then_inc(sem("l_mean_square"), 1)

            def l_scale(j, n):
                dve.wait_ge(sem("l_rms"), n("l_rms"))
                dve.scalar_tensor_tensor(out=oT[j][:, :], in0=ps[j][:, 0:512], scalar=rmsw[:, :], in1=rden[j][:, :],
                                         op0=ALU.mult, op1=ALU.mult).then_inc(sem("l_oT"), 1)

            def m_norm1(j, n):
                dve.wait_ge(sem("x1_normed"), n("x1_normed"))
                for tt in range(TT):
                    ins = dve.bn_stats(bn[j][:, tt, :], x[j][:, tt, :])
                link(ins, True)
                for tt in range(TT):
                    ins = dve.bn_aggr(mv[j][:, tt, :], bn[j][:, tt, :])
                ins.then_inc(sem("n1_moments"), 1)
                dve.wait_ge(sem("n1_rstd"), n("n1_rstd"))
                for tt in range(TT):
                    ins = dve.tensor_scalar(h1n[j][:, tt, :], x[j][:, tt, :], mv[j][:, tt, 0:1],
                                            rstd[j][:, tt:tt + 1], ALU.subtract, ALU.mult)
                ins.then_inc(sem("m_h"), 1)

            def m_conv(j, n):
                dve.wait_ge(sem("m_affine"), n("m_affine"))
                for kt in range(KT):
                    ins = dve.tensor_scalar(xT[j][:, kt, :], hpad[j][:, kt, 2:S + 2], convw[:, kt, 2:3], None, ALU.mult)
                link(ins)
                for tap in (1, 0):
                    for kt in range(KT):
                        ins = dve.scalar_tensor_tensor(out=xT[j][:, kt, :], in0=hpad[j][:, kt, tap:S + tap],
                                                       scalar=convw[:, kt, tap:tap + 1], in1=xT[j][:, kt, :],
                                                       op0=ALU.mult, op1=ALU.add)
                    if tap:
                        link(ins)
                ins.then_inc(sem("m_conv"), 1)

            def m_router(j, n, tile):
                dve.wait_ge(sem("m_y"), n("m_y"))
                dve.tensor_tensor(flat(r[j]), ps[j][:, 0:512], flat(x[j]), ALU.add).then_inc(sem("m_x"), 1)
                dve.wait_ge(sem("m_x"), n("m_x"))
                moments("n2", j)
                dve.wait_ge(sem("n2_rstd"), n("n2_rstd"))
                for tt in range(TT):
                    ins = dve.tensor_scalar(xb[j][:, tt, :], r[j][:, tt, :], mv[j][:, tt, 0:1],
                                            rstd[j][:, tt:tt + 1], ALU.subtract, ALU.mult)
                link(ins)
                w = rows_of["m_ln2_w"][:, :].unsqueeze(1).broadcast_to([P, TT, D])
                b = rows_of["m_ln2_b"][:, :].unsqueeze(1).broadcast_to([P, TT, D])
                link(dve.tensor_tensor(xb[j][:, :, :], xb[j][:, :, :], w, ALU.mult))
                dve.tensor_tensor(xb[j][:, :, :], xb[j][:, :, :], b, ALU.add).then_inc(sem("m_h2"), 1)
                dve.wait_ge(sem("m_h2"), n("m_h2"))
                for tt in range(TT):
                    for e in range(E):
                        ins = dve.tensor_tensor_reduce(
                            out=oT[j][:, 0:D], in0=xb[j][:, tt, :], in1=routw[:, e, :], scale=1.0, scalar=0.0,
                            op0=ALU.mult, op1=ALU.add, accum_out=lg[j][:, tt * E + e:tt * E + e + 1])
                        link(ins)
                dve.tensor_copy(logits[:, bass.ds(tile, TT), :], lg[j][:, :].rearrange("p (t e) -> p t e", e=E))\
                    .then_inc(sem("m_logits"), 1)

            with dve.Fori(0, B // 2) as i:
                counts = Count(dve, i)
                ns = [counts.slot(j) for j in two]
                chain["base"] = dve.snap(i * DVE_LINKS)
                chain["stored"] = dve.snap(i * 32 + 32)
                steps = [a0_kv, a0_max, a0_o, add_norm("a0", "a0_residual", xb),
                         cross_qk32("x0"), rests("x0", True), qT_copy("x0", KS + 1), kT_copy("x0", KS + 1, True),
                         cross_max("x0", 0), cross_max("x0", 1), mT_copy("x0"), divided("x0"),
                         add_norm("x0", "x0_residual", xb),
                         f_round, f_interpolate, f_norm,
                         l_mask(0), l_mask(1), l_mean, l_scale, add_norm("l", None, x),
                         cross_qk32("x1"), rests("x1", True), qT_copy("x1", KS), kT_copy("x1", KS, True),
                         cross_max("x1", 0), cross_max("x1", 1), mT_copy("x1"), x1_mask(0), x1_mask(1),
                         divided("x1"), add_norm("x1", "x1_residual", xb), m_norm1, m_conv,
                         rope, rests("m", False), qT_copy("m", KS), kT_copy("m", KS, False),
                         causal_max(0), causal_max(1), causal_max(2), mT_copy("m"), divided("m")]
                for step in steps:
                    for j in two:
                        step(j, ns[j])
                for j in two:
                    m_router(j, ns[j], 2 * TT * i + TT * j)
                for j in two:
                    dve.wait_ge(sem(f"rows_stored{j}"), chain["stored"])
            assert chain["n"] == DVE_LINKS, chain["n"]

        @block.gpsimd
        def _(pool):
            for s in "qk":
                last = pool.memset(diag[s], 0.0)
            last.then_inc(sem("diag_zero"), 1)
            pool.wait_ge(setup_dma, LOADED)
            pool.wait_ge(sem("setup_act"), 1)
            pool.wait_ge(sem("setup_dve"), 1)
            pool.engine_nop().then_inc(sem("setup_pool"), 1)

            def start(j, n, it):
                settled_wait(pool, sem(f"inputs_loaded{j}"), it)
                pool.tensor_scalar(fk4[j][:, :, :], fkin[j][:, :, :], -4e6, None, ALU.mult).then_inc(sem("fk4"), 1)
                pool.tensor_scalar(bkneg[j][:, :], bkin[j][:, :], NEG, None, ALU.mult)
                ab = rows_of["a0_b"][:, :].unsqueeze(1).broadcast_to([P, TT, D])
                pool.tensor_tensor(xb[j][:, :, :], xin[j][:, :, :], ab, ALU.add).then_inc(sem("a0_residual"), 1)

            def rstd_of(s):
                def step(j, n):
                    settled_wait(pool, sem(f"{s}_moments"), n(f"{s}_moments"))
                    pool.tensor_scalar(rstd[j][:, :], mv[j][:, :, 1], EPS, None, ALU.add)\
                        .then_inc(sem(f"{s}_variance"), 1)
                    pool.wait_ge(sem(f"{s}_variance"), n(f"{s}_variance"))
                    pool.tensor_tensor(rstd[j][:, :], rstd[j][:, :], const("half")[:, 0:TT], ALU.pow)\
                        .then_inc(sem(f"{s}_rstd"), 1)
                return step

            def residual(s, prev, bias):
                def step(j, n):
                    settled_wait(pool, sem(f"{prev}_normed"), n(f"{prev}_normed"))
                    bb = rows_of[bias][:, :].unsqueeze(1).broadcast_to([P, TT, D])
                    pool.tensor_tensor(xb[j][:, :, :], x[j][:, :, :], bb, ALU.add).then_inc(sem(f"{s}_residual"), 1)
                return step

            def copies(s, cross):
                def step(j, n):
                    for which, c, first, second, firsts, seconds in ((0, "q", 0, 2, (1, 4), (3,)),
                                                                     (1, "k", 0, 1, (2, 5), (3,))):
                        rows = C if cross and which else P
                        g = H if cross and which else TT * H
                        gv, st = stack_view(j, which)
                        settled_wait(pool, sem(f"{s}_{c}_part1"), n(f"{s}_{c}_part1"))
                        for d in firsts:
                            pool.tensor_scalar(st[0:rows, 0:g, d, :], st[0:rows, 0:g, first, :], 1.0, None, ALU.mult)
                        if s == "x0":
                            row = gv[0:rows, 0:g, KS:KS + 1]
                            if which == 0:
                                pool.memset(row, 1.0)
                            else:
                                pool.tensor_scalar(row, cf[0:C, CF["ones"][0]:CF["ones"][0] + H].unsqueeze(2),
                                                   bkneg[j][:, :], None, ALU.mult)
                    for which, c, first, second, firsts, seconds in ((0, "q", 0, 2, (1, 4), (3,)),
                                                                     (1, "k", 0, 1, (2, 5), (3,))):
                        rows = C if cross and which else P
                        g = H if cross and which else TT * H
                        gv, st = stack_view(j, which)
                        settled_wait(pool, sem(f"{s}_{c}_part2"), n(f"{s}_{c}_part2"))
                        for d in seconds:
                            ins = pool.tensor_scalar(st[0:rows, 0:g, d, :], st[0:rows, 0:g, second, :], 1.0, None,
                                                     ALU.mult)
                        ins.then_inc(sem(f"{s}_{c}_copies"), 1)
                return step

            def l_zeros(j, n):
                settled_wait(pool, sem("f_normed"), n("f_normed"))
                pool.memset(kF[j], 0.0).then_inc(sem("l_zeros"), 1)

            def m_residual(j, n):
                pool.wait_ge(sem("m_x"), n("m_x"))
                pool.tensor_tensor(x[j][:, :, :], x[j][:, :, :], r[j][:, :, :], ALU.add)\
                    .then_inc(sem("m_residual"), 1)
                rstd_of("n2")(j, n)

            def m_pad(j, n):
                settled_wait(pool, sem("x1_normed"), n("x1_normed"))
                pool.memset(hpad[j][:, :, 0:2], 0.0).then_inc(sem("m_pad"), 1)

            with pool.Fori(0, B // 2) as i:
                counts = Count(pool, i)
                ns = [counts.slot(j) for j in two]
                it = pool.snap(64 * i + 64)
                for j in two:
                    start(j, ns[j], it)
                steps = [rstd_of("a0"), residual("x0", "a0", "x0_b"), copies("x0", True), rstd_of("x0"),
                         rstd_of("f"), l_zeros, rstd_of("l"), residual("x1", "l", "x1_bo"),
                         copies("x1", True), rstd_of("x1"), m_pad, rstd_of("n1"), copies("m", False), m_residual]
                for step in steps:
                    for j in two:
                        step(j, ns[j])
                stored = pool.snap(32 * i + 32)
                for j in two:
                    settled_wait(pool, sem(f"rows_stored{j}"), stored)
                    settled_wait(pool, sem("m_logits"), ns[j]("m_logits"))

        @block.sync
        def _(sp):
            for dst, src in loads:
                sp.dma_start(dst, src).then_inc(setup_dma, 16)
            sp.wait_ge(sem("diag_zero"), 1)
            for dst, src in diag_loads:
                sp.dma_start(dst, src).then_inc(setup_dma, 16)

            mask_bytes = a["bk"].bitcast(U8).rearrange("(b p) -> b p", p=C)

            def load(j, b):
                q = sem(f"inputs_loaded{j}")
                sp.dma_start(xin[j][:, :, :], a["x"][bass.ds(b, 1)].rearrange("b (t p) n -> p (b t) n", p=P))\
                    .then_inc(q, 16)
                sp.dma_start(cin[j][:, :], a["ctx"][bass.ds(b, 1)].rearrange("b p n -> p (b n)")).then_inc(q, 16)
                sp.dma_start(bkin[j][:, :], mask_bytes[bass.ds(b, 1)].rearrange("b p -> p b")).then_inc(q, 16)
                sp.dma_start(fkin[j][:, :, :], a["fk"][bass.ds(b, 1)].rearrange("b o (t p) n -> p (b o t) n", p=P))\
                    .then_inc(q, 16)

            def store(j, n, b):
                q = sem(f"rows_stored{j}")
                rows = bass.ds(S * b, S)
                sp.wait_ge(sem("m_residual"), n("m_residual"))
                sp.dma_start(residual_dram[rows, :].rearrange("(t p) n -> p t n", p=P), x[j][:, :, :]).then_inc(q, 16)
                sp.wait_ge(sem("m_h2"), n("m_h2"))
                sp.dma_start(h2_dram[rows, :].rearrange("(t p) n -> p t n", p=P), xb[j][:, :, :]).then_inc(q, 16)

            for j in two:
                load(j, j)
            with sp.Fori(0, B // 2 - 1) as i:
                counts = Count(sp, i)
                ns = [counts.slot(j) for j in two]
                for j in two:
                    settled_wait(sp, sem("ctx_transposed"), ns[j]("ctx_transposed"))
                    settled_wait(sp, sem("a0_residual"), ns[j]("a0_residual"))
                    load(j, 2 * i + 2 + j)
                for j in two:
                    store(j, ns[j], 2 * i + j)
            for j in two:
                store(j, lambda name, j=j: B - 1 + j, B - 2 + j)


def part_two(nc, a, ctx, sb, sem, ps, const, ident, logits, residual_dram, h2_dram, token_dram, out):
    w_up = sb("w_up", [P, KT, E * 2 * FFE])
    w_down = sb("w_down", [P, FFE // P, E * D])
    top = sb("top", [P, NT])
    oh = sb("oh", [P, NT, E])
    free = sb("free", [P, NT])
    before = sb("before", [P, NT + 1, E])
    fills = sb("fills", [P, E, NT])
    ntile = sb("ntile", [P, E])
    base = sb("base", [P, E])
    place = sb("place", [P, NT, E])
    row = sb("row", [P, NT])
    row_i = sb("row_i", [P, NT], I32)
    token_i = sb("token_i", [P, NT], I32)
    nobody = sb("nobody", [P, TILES], I32)
    expert = sb("expert", [P, TILES])
    expert_i = sb("expert_i", [P, TILES], I32)
    tokens_i = sb("tokens_i", [TILES, P], I32)
    tokens = sb("tokens", [TILES, P])
    target = sb("target", [P, TILES], I32)
    source = sb("source", [P, TILES], I32)
    idx_h = sb("idx_h", [P, 1], I32)
    idx_x = sb("idx_x", [P, 1], I32)
    idx_o = sb("idx_o", [P, 1], I32)
    hg = sb("hg", [P, D])
    xg = sb("xg", [P, D])
    hT = sb("hT", [P, KT, P])
    silu = sb("silu", [P, FFE])
    hid = sb("hid", [P, FFE])
    hidT = sb("hidT", [P, FFE])
    total = sb("total", [P, D])
    bn2 = sb("bn2", [P, 6])
    mv2 = sb("mv2", [P, 2])
    rs2 = sb("rs2", [P, 1])
    result = sb("result", [P, D])

    settled_wait = settler(sem)
    block = ctx.enter_context(nc.Block())

    @block.sync
    def _(sp):
        for e in range(0, E, 2):
            c = 2 * FFE
            sp.dma_start(w_up[:, :, e * c:e * c + c], a["e_up"][e].rearrange("(t p) n -> p t n", p=P))\
                .then_inc(sem("up_loaded"), 16)
            sp.dma_start(w_down[:, :, e * D:e * D + D], a["e_down"][e].rearrange("(t p) n -> p t n", p=P))\
                .then_inc(sem("down_loaded"), 16)

    @block.tensor
    def _(pe):
        pe.wait_ge(sem("one_expert"), 1)
        flat = oh[:, :, :].rearrange("p t e -> p (t e)")
        pe.matmul(ps[0][:, 0:NT * E], const("upper"), flat, start=True, stop=True)
        pe.matmul(ps[1][:, 0:NT * E], const("ones"), flat, start=True, stop=True).then_inc(sem("counts"), 1)
        pe.wait_ge(sem("rows_known"), 1)
        pe.wait_ge(sem("tokens_float"), 1)
        pe.transpose(ps[0][:, 0:TILES], tokens[:, :], ident[0:TILES, 0:TILES]).then_inc(sem("tokens_by_tile"), 1)
        pe.wait_ge(sem("sources"), 1)
        pe.wait_ge(sem("up_loaded"), 16 * E)
        pe.wait_ge(sem("down_loaded"), 16 * E)
        experts = {}

        def turn(n16):
            pe.wait_ge(sem("h_gathered"), n16)
            for kt in range(KT):
                mm = pe.transpose(ps[1][:, P * kt:P * kt + P], hg[:, P * kt:P * kt + P], ident)
            mm.then_inc(sem("h_turned"), 1)

        def turn_hidden(n):
            pe.wait_ge(sem("hidden"), n)
            for m in range(FFE // P):
                mm = pe.transpose(ps[1][:, 512 + P * m:512 + P * m + P], hid[:, P * m:P * m + P], ident)
            mm.then_inc(sem("hidden_turned"), 1)

        def up(n, e):
            pe.wait_ge(sem("hT"), n)
            for c in range(4):
                for kt in range(KT):
                    mm = pe.matmul(ps[0][:, 512 * c:512 * c + 512], hT[:, kt, :],
                                   w_up[:, kt, bass.ds(e * (2 * FFE) + 512 * c, 512)],
                                   start=kt == 0, stop=kt == KT - 1)
            mm.then_inc(sem("up"), 1)

        def down(n, e):
            pe.wait_ge(sem("hidT_act"), n)
            pe.wait_ge(sem("hidT_dve"), n)
            for m in range(FFE // P):
                mm = pe.matmul(ps[1][:, 1536:1536 + D], hidT[:, P * m:P * m + P],
                               w_down[:, m, bass.ds(e * D, D)], start=m == 0, stop=m == FFE // P - 1)
            mm.then_inc(sem("expert_y"), 1)

        def expert_of(t):
            return pe.value_load(expert_i[0:1, t], min_val=0, max_val=E - 1)

        turn(16)
        up(1, expert_of(slice(0, 1)))
        with pe.Fori(1, TILES) as t:
            n, prev = pe.snap(t + 1), t
            turn(pe.snap(16 * t + 16))
            turn_hidden(prev)
            up(n, expert_of(bass.ds(t, 1)))
            down(prev, expert_of(bass.ds(t - 1, 1)))
        turn_hidden(TILES)
        down(TILES, expert_of(slice(TILES - 1, TILES)))

    @block.scalar
    def _(act):
        for e in range(1, E, 2):
            c = 2 * FFE
            act.dma_start(w_up[:, :, e * c:e * c + c], a["e_up"][e].rearrange("(t p) n -> p t n", p=P))\
                .then_inc(sem("up_loaded"), 16)
            act.dma_start(w_down[:, :, e * D:e * D + D], a["e_down"][e].rearrange("(t p) n -> p t n", p=P))\
                .then_inc(sem("down_loaded"), 16)

        def copy_hT(n):
            act.wait_ge(sem("h_turned"), n)
            act.activation(hT[:, :, :].rearrange("p t s -> p (t s)"), ps[1][:, 0:D], ACT.Copy)\
                .then_inc(sem("hT"), 1)

        def copy_hidT(n):
            act.wait_ge(sem("hidden_turned"), n)
            act.activation(hidT[:, 0:512], ps[1][:, 512:1024], ACT.Copy).then_inc(sem("hidT_act"), 1)

        def gate(n):
            act.wait_ge(sem("up"), n)
            act.activation(silu[:, :], ps[0][:, 0:FFE], ACT.Silu).then_inc(sem("silu"), 1)

        copy_hT(1)
        gate(1)
        with act.Fori(1, TILES) as t:
            n = act.snap(t + 1)
            copy_hT(n)
            copy_hidT(t)
            gate(n)
        copy_hidT(TILES)

    @block.vector
    def _(dve):
        done = {"n": 0}

        def link(ins):
            done["n"] += 1
            ins.then_inc(sem("routing_chain"), 1)
            dve.wait_ge(sem("routing_chain"), done["n"])

        link(dve.tensor_reduce(top[:, :], logits[:, :, :], AX, ALU.max))
        link(dve.tensor_tensor(oh[:, :, :], logits[:, :, :], top[:, :].unsqueeze(2).broadcast_to([P, NT, E]),
                               ALU.is_ge))
        link(dve.tensor_scalar(free[:, :], oh[:, :, 0], -1.0, 1.0, ALU.mult, ALU.add))
        for e in range(1, E - 1):
            link(dve.tensor_tensor(oh[:, :, e], oh[:, :, e], free[:, :], ALU.mult))
            link(dve.tensor_tensor(free[:, :], free[:, :], oh[:, :, e], ALU.subtract))
        dve.tensor_copy(oh[:, :, E - 1], free[:, :]).then_inc(sem("one_expert"), 1)
        dve.tensor_copy(token_i[:, :], const("token"))
        dve.memset(nobody[:, :], N).then_inc(sem("ids"), 1)
        dve.memset(before[:, 0, :], 0.0)
        link(dve.memset(base[:, :], 0.0))
        dve.wait_ge(sem("counts"), 1)
        tot = ps[1][:, 0:NT * E].rearrange("p (t e) -> p t e", e=E)
        for t in range(NT):
            link(dve.tensor_tensor(before[:, t + 1, :], tot[:, t, :], before[:, t, :], ALU.add))
        link(dve.tensor_tensor(fills[:, :, :], before[:, NT, :].unsqueeze(2).broadcast_to([P, E, NT]),
                               const("kth").unsqueeze(1).broadcast_to([P, E, NT]), ALU.is_gt))
        link(dve.tensor_reduce(ntile[:, :], fills[:, :, :], AX, ALU.add))
        for e in range(1, E):
            link(dve.tensor_tensor(base[:, e:e + 1], base[:, e - 1:e], ntile[:, e - 1:e], ALU.add))
        link(dve.tensor_tensor(place[:, :, :], ps[0][:, 0:NT * E].rearrange("p (t e) -> p t e", e=E),
                               before[:, 0:NT, :], ALU.add))
        link(dve.scalar_tensor_tensor(out=place[:, :, :], in0=base[:, :].unsqueeze(1).broadcast_to([P, NT, E]),
                                      scalar=float(P), in1=place[:, :, :], op0=ALU.mult, op1=ALU.add))
        link(dve.tensor_tensor(place[:, :, :], place[:, :, :], oh[:, :, :], ALU.mult))
        link(dve.tensor_reduce(row[:, :], place[:, :, :], AX, ALU.add))
        dve.tensor_copy(row_i[:, :], row[:, :]).then_inc(sem("row_of_token"), 1)
        link(dve.tensor_scalar(expert[:, :], const("tile"), base[:, 1:2], None, ALU.is_ge))
        for e in range(2, E):
            link(dve.scalar_tensor_tensor(out=expert[:, :], in0=const("tile"), scalar=base[:, e:e + 1],
                                          in1=expert[:, :], op0=ALU.is_ge, op1=ALU.add))
        dve.tensor_copy(expert_i[:, :], expert[:, :]).then_inc(sem("rows_known"), 1)
        dve.wait_ge(sem("tokens_read"), 16)
        dve.tensor_copy(tokens[:, :], tokens_i[:, :]).then_inc(sem("tokens_float"), 1)
        dve.wait_ge(sem("tokens_by_tile"), 1)
        dve.tensor_copy(target[:, :], ps[0][:, 0:TILES])
        dve.tensor_scalar(source[:, :], ps[0][:, 0:TILES], float(N - 1), None, ALU.min).then_inc(sem("sources"), 1)

        def copy_hidT(n):
            dve.wait_ge(sem("hidden_turned"), n)
            dve.tensor_copy(hidT[:, 512:1024], ps[1][:, 1024:1536]).then_inc(sem("hidT_dve"), 1)

        def gated(n, prev):
            dve.wait_ge(sem("silu"), n)
            if prev is not None:
                dve.wait_ge(sem("hidden_turned"), prev)
            dve.tensor_tensor(hid[:, :], ps[0][:, FFE:2 * FFE], silu[:, :], ALU.mult).then_inc(sem("hidden"), 1)

        def finish(n, n16):
            dve.wait_ge(sem("expert_y"), n)
            dve.wait_ge(sem("x_gathered"), n16)
            dve.tensor_tensor(total[:, :], ps[1][:, 1536:1536 + D], xg[:, :], ALU.add).then_inc(sem("total"), 1)
            dve.wait_ge(sem("total"), n)
            dve.bn_stats(bn2[:, :], total[:, :]).then_inc(sem("stats"), 1)
            settled_wait(dve, sem("stats"), n)
            dve.bn_aggr(mv2[:, :], bn2[:, :]).then_inc(sem("last_moments"), 1)
            dve.wait_ge(sem("last_rstd"), n)

        def write_result(scattered):
            if scattered is not None:
                dve.wait_ge(sem("scattered"), scattered)
            dve.tensor_scalar(result[:, :], total[:, :], mv2[:, 0:1], rs2[:, 0:1], ALU.subtract, ALU.mult)\
                .then_inc(sem("result"), 1)

        gated(1, None)
        copy_hidT(1)
        gated(2, 1)
        finish(1, 16)
        write_result(None)
        with dve.Fori(2, TILES) as t:
            n, n16 = dve.snap(t + 1), dve.snap(16 * t)
            copy_hidT(t)
            gated(n, t)
            finish(t, n16)
            write_result(dve.snap(16 * t - 16))
        copy_hidT(TILES)
        finish(TILES, 16 * TILES)
        write_result(16 * TILES - 16)

    @block.gpsimd
    def _(pool):
        pool.wait_ge(sem("ids"), 1)
        pool.dma_start(token_dram.rearrange("(p t) o -> p (t o)", p=P), nobody[:, :]).then_inc(sem("cleared"), 16)
        pool.wait_ge(sem("cleared"), 16)
        pool.wait_ge(sem("row_of_token"), 1)
        for t in range(NT):
            pool.indirect_dma_start(out=token_dram, out_offset=bass.IndirectOffsetOnAxis(ap=row_i[:, t:t + 1], axis=0),
                                    in_=token_i[:, t:t + 1], in_offset=None, bounds_check=ROWS - 1,
                                    oob_is_err=True).then_inc(sem("tokens_written"), 16)
        pool.wait_ge(sem("tokens_written"), 16 * NT)
        pool.dma_start(tokens_i[:, :], token_dram.rearrange("(t p) o -> t (p o)", p=P)).then_inc(sem("tokens_read"), 16)
        pool.wait_ge(sem("sources"), 1)

        def gather(dst, table, idx, t, signal, copied, n):
            pool.tensor_copy(idx[:, :], source[:, t]).then_inc(sem(copied), 1)
            settled_wait(pool, sem(copied), n)
            pool.indirect_dma_start(out=dst[:, :], out_offset=None, in_=table,
                                    in_offset=bass.IndirectOffsetOnAxis(ap=idx[:, :], axis=0),
                                    bounds_check=N - 1, oob_is_err=True).then_inc(sem(signal), 16)

        def rstd(n):
            settled_wait(pool, sem("last_moments"), n)
            pool.tensor_scalar(rs2[:, :], mv2[:, 1:2], EPS, None, ALU.add).then_inc(sem("last_variance"), 1)
            pool.wait_ge(sem("last_variance"), n)
            pool.tensor_tensor(rs2[:, :], rs2[:, :], const("half")[:, 0:1], ALU.pow).then_inc(sem("last_rstd"), 1)

        def scatter(t, n):
            pool.tensor_copy(idx_o[:, :], target[:, t]).then_inc(sem("o_index"), 1)
            pool.wait_ge(sem("o_index"), n)
            settled_wait(pool, sem("result"), n)
            pool.indirect_dma_start(out=out, out_offset=bass.IndirectOffsetOnAxis(ap=idx_o[:, :], axis=0),
                                    in_=result[:, :], in_offset=None, bounds_check=N - 1, oob_is_err=False)\
                .then_inc(sem("scattered"), 16)

        gather(hg, h2_dram, idx_h, slice(0, 1), "h_gathered", "h_index", 1)
        gather(xg, residual_dram, idx_x, slice(0, 1), "x_gathered", "x_index", 1)
        pool.wait_ge(sem("h_turned"), 1)
        gather(hg, h2_dram, idx_h, slice(1, 2), "h_gathered", "h_index", 2)
        rstd(1)
        scatter(slice(0, 1), 1)
        gather(xg, residual_dram, idx_x, slice(1, 2), "x_gathered", "x_index", 2)
        with pool.Fori(2, TILES) as t:
            n = pool.snap(t + 1)
            settled_wait(pool, sem("h_turned"), t)
            gather(hg, h2_dram, idx_h, bass.ds(t, 1), "h_gathered", "h_index", n)
            rstd(t)
            settled_wait(pool, sem("scattered"), 16 * t - 16)
            scatter(bass.ds(t - 1, 1), t)
            gather(xg, residual_dram, idx_x, bass.ds(t, 1), "x_gathered", "x_index", n)
        rstd(TILES)
        pool.wait_ge(sem("scattered"), 16 * TILES - 16)
        scatter(slice(TILES - 1, TILES), TILES)
        pool.wait_ge(sem("scattered"), 16 * TILES)


def kernel(**inputs):
    import numpy as _np
    import concourse.bacc as _bacc
    from concourse import mybir as _mybir
    from concourse.bass_utils import run_bass_kernel_spmd as _run

    g = {k: _np.asarray(v) for k, v in inputs.items()}
    cf, cb = shape_constants()
    host = {
        "x": g["x"], "ctx": g["ctx_1024"], "bk": _np.ascontiguousarray(g["mask_BxS2_bk0"]).reshape(-1).view(_np.int32), "fk": g["mask_Bx1xSxS2_fk0"],
        "cf": cf, "cb": cb,
        "a0_qkv": g["L0_attn_w_qkv"].T, "a0_proj": g["L0_attn_w_proj"].T, "a0_b": g["L0_attn_b_proj"],
        "x0_q": g["L0_xattn_Wq"], "x0_kv": g["L0_xattn_Wkv"], "x0_proj": g["L0_xattn_Wproj"],
        "x0_b": g["L0_xattn_bproj"],
        "f_w1": g["L0_ffn_w1"], "f_b1": g["L0_ffn_b1"].reshape(FF0 // P, P).T, "f_w2": g["L0_ffn_w2"], "f_b2": g["L0_ffn_b2"],
        "a1_q": g["L1_attn_Wq"], "a1_k": g["L1_attn_Wk"], "a1_v": g["L1_attn_Wv"].T, "a1_o": g["L1_attn_Wo"].T,
        "a1_fmqT": g["L1_attn_fmq_w"].T, "a1_fmq_b": g["L1_attn_fmq_b"],
        "a1_fmkT": g["L1_attn_fmk_w"].T, "a1_fmk_b": g["L1_attn_fmk_b"], "a1_rms": g["L1_attn_rms_w"],
        "x1_q": g["L1_xattn_Wq"].T, "x1_bq": g["L1_xattn_bq"], "x1_k": g["L1_xattn_Wk"].T,
        "x1_bk": g["L1_xattn_bk"], "x1_v": g["L1_xattn_Wv"].T, "x1_bv": g["L1_xattn_bv"],
        "x1_o": g["L1_xattn_Wo"].T, "x1_bo": g["L1_xattn_bo"],
        "m_ln1_w": g["L1_ffn_ln1_w"].reshape(KT, P).T, "m_ln1_b": g["L1_ffn_ln1_b"].reshape(KT, P).T, "m_ln2_w": g["L1_ffn_ln2_w"],
        "m_ln2_b": g["L1_ffn_ln2_b"], "m_conv": g["L1_ffn_conv_w"].reshape(KT, P, 3).transpose(1, 0, 2), "m_qkv": g["L1_ffn_attn_w"],
        "m_proj": g["L1_ffn_proj_w"], "m_router": g["L1_ffn_router_w"].T,
        "e_up": g["L1_ffn_expert_wv"], "e_down": g["L1_ffn_expert_proj"],
    }
    nc = _bacc.Bacc("TRN2", target_bir_lowering=False, num_devices=1)
    arrays, aps = {}, {}
    for name, v in host.items():
        v = _np.ascontiguousarray(v)
        arrays[f"in_{name}"] = v
        aps[name] = nc.dram_tensor(f"in_{name}", v.shape, _mybir.dt.from_np(v.dtype), kind="ExternalInput").ap()
    out = nc.dram_tensor("out_rows", (N, D), F32, kind="ExternalOutput").ap()
    decoder(nc, aps, out)
    r = _run(nc, [arrays], core_ids=[0])
    return r.results[0]["out_rows"].reshape(B, S, D)
```

```python
from contextlib import ExitStack

import numpy as np

import concourse.bass as bass
from concourse import mybir

F32 = mybir.dt.float32
BF16 = mybir.dt.bfloat16
I32 = mybir.dt.int32
U8 = mybir.dt.uint8
ALU = mybir.AluOpType
ACT = mybir.ActivationFunctionType
AX = mybir.AxisListType.X

P = 128
B, S, D, C = 8, 256, 256, 77
KT = D // P
TT = S // P
H, HD = 16, 16
H1, HD1 = 8, 32
FF0 = 1024
E, FFE = 4, 1024
N = B * S
NT = N // P
TILES = NT + E - 1
ROWS = TILES * P
PARTS = 6
KS = PARTS * HD
W = KS + 2
SECOND, THIRD = (3, 1), (5, 2)
FIRST_AGAIN = ((1, 2), (3, 5))
EPS = 1e-5
DVE_LINKS = 62
ROUNDS = B // 2
A0, X0, F, L, X1, M = 0, 7, 18, 21, 28, 38
LENGTHS = (4, 8, 4, 3, 4, 6, 3) + (14, 5, 3, 3, 3, 1, 5, 5, 8, 7) + (3, 28, 9, 3) \
    + (10, 5, 5, 3, 6, 7, 3) + (14, 5, 3, 4, 4, 1, 7, 7, 8, 10) + (6, 18, 6, 5, 5, 5, 5, 1, 6, 6, 6, 9, 12, 3)
LAG = 0.5
MAGIC = 1.5 * 2.0 ** 23
MAGIC64 = 64 * MAGIC
NEG = -3.3895313892515355e38
FLT_MAX = 3.4028234663852886e38

CF = {}
_o = 0
for _n, _w in (("ident", P), ("allow", S), ("upper", P), ("ones", P), ("block", P), ("onesexp", 64),
               ("cos", TT * HD), ("sin", TT * HD), ("pm", 1), ("half", 4), ("kth", NT), ("tile", TILES),
               ("token", NT), ("left", 1), ("right", 1)):
    CF[_n] = (_o, _w)
    _o += _w
CF_N = _o
CB = {"ident": (0, P), "neg_qk": (P, S), "neg_kq": (P + S, S), "sel": (P + 2 * S, H * P)}
CB_N = P + 2 * S + H * P


SOFTMAX = ("x0", "x1", "m")
NORMS = ("a0", "x0", "f", "l", "x1", "n1", "n2")


def _in_turn(text):
    names, stage = [], None
    for word in text.split():
        if word.endswith(":"):
            stage = word[:-1]
        else:
            names.append(f"{stage}_{word}" if stage else word)
    return names


TURNS = {
    "projected": _in_turn("a0: qkv x0: qkv f: h0 h1 l: maps v_product x1: qkv m: qkv"),
    "transposed": _in_turn("x: transposed ctx: transposed a0: p_transposed transposed fk4: transposed x0: q_transposed k_transposed "
                           "max_transposed transposed f: transposed l: transposed x1: q_transposed k_transposed "
                           "max_transposed m: transposed q_transposed k_transposed max_transposed"),
    "scored": _in_turn("a0: scores x0: scores0 scores1 scores_t0 scores_t1 l: scores0 scores1 "
                       "x1: scores0 scores1 scores_t0 scores_t1 m: scores0 scores1 scores2 scores_t0 scores_t1 "
                       "scores_t2"),
    "weighed": _in_turn("a0: pv x0: pv l: o square_sums x1: pv m: pv"),
    "y": _in_turn("a0: y x0: y f: y l: y x1: y m: y"),
    "act_copied": _in_turn("start: xT ctxT a0: qT pT xT fk4: T x0: qT_act kT_act xT f: xT l: v xT x1: qT_act kT_act "
                           "m: qT_act kT_act"),
    "parts": [f"{s}_{t}" for s in SOFTMAX for t in ("q_part1", "k_part1", "v", "q_part2", "k_part2")],
    "exp": _in_turn("a0: exp x0: exp0 exp1 x1: exp0 exp1 m: exp0 exp1 exp2"),
    "mapped": _in_turn("x0: ln inverse f: h256 left right l: features squared ln rms x1: ln inverse m: affine ln "
                       "inverse"),
    "dve_copied": _in_turn("a0: kT_v x0: qT_dve kT_dve mT x1: qT_dve kT_dve mT m: qT_dve kT_dve mT"),
    "split": _in_turn("x0: q32 k32 q_rest k_rest q_stack k_stack x1: q32 k32 v32 q_rest k_rest q_stack k_stack "
                      "m: q32 k32 q_rest q_stack k_stack"),
    "max": _in_turn("a0: minus_max x0: max0 max1 minus_max x1: max0 max1 minus_max m: max0 max1 max2 minus_max"),
    "masked": _in_turn("l: masked0 masked1 mean_square x1: masked_t0 masked_t1"),
    "output": _in_turn("a0: o x0: oT l: oT x1: oT m: oT"),
    "hidden": _in_turn("f: k clipped index fraction "
                        "slope0 rise0 value0 rounded0 hT0 slope1 rise1 value1 rounded1 hT1"),
    "moments": [f"{s}_moments" for s in NORMS],
    "normed": _in_turn("a0: normed x0: normed f: normed l: normed x1: normed m: h conv x h2 logits"),
    "filled": _in_turn("fk4 x0: rows f: over l: zeros m: pad k_rest k_part3"),
    "residual": _in_turn("a0: residual x0: residual x1: residual m: residual"),
    "variance": [f"{s}_variance" for s in NORMS],
    "rstd": [f"{s}_rstd" for s in NORMS],
}
PLACE = {product: (name, k, len(products)) for name, products in TURNS.items() for k, product in enumerate(products)}


def settler(sem):
    def settled_wait(engine, signal, value):
        engine.wait_ge(signal, value)
        if not isinstance(value, int):
            engine.sem_inc(sem("passed"), 1)
    return settled_wait


class Count:

    def __init__(self, engine, i, j=0, later=0, bases=None):
        self.engine, self.i, self.j, self.later = engine, i, j, later
        self.bases = {} if bases is None else bases

    def at(self, j, later=0):
        return Count(self.engine, self.i, j, later, self.bases)

    def of(self, n, plus):
        if n not in self.bases:
            self.bases[n] = n * self.i if isinstance(self.i, int) else self.engine.snap(n * self.i)
        return self.bases[n] + (n * self.later + plus)

    def __call__(self, product):
        _, k, n = PLACE[product]
        return self.of(n, k + 1)

    def loaded(self):
        return self.of(64, 64)

    def stored(self):
        return self.of(32, 32)


def when(tick):
    whole = int(tick)
    return sum(LENGTHS[:whole]) + (tick - whole) * LENGTHS[whole]


class Schedule:

    def __init__(self, steps):
        self.steps = [(when(tick), step) for tick, step in steps]

    def first(self, counts):
        for time, step in sorted(self.steps, key=lambda s: s[0]):
            if time < LAG:
                step(0, counts.at(0))

    def round(self, counts, last=False):
        turns = [(time, 0, 0, step) for time, step in self.steps if time >= LAG]
        turns += [(time + LAG, 1, 0, step) for time, step in self.steps]
        if not last:
            turns += [(time + sum(LENGTHS), 0, 1, step) for time, step in self.steps if time < LAG]
        for _, j, later, step in sorted(turns, key=lambda t: t[:2]):
            step(j, counts.at(j, later))


def shape_constants():
    f = np.zeros((P, CF_N), np.float32)

    def put(name, value):
        o, w = CF[name]
        f[:, o:o + w] = value

    r, c = np.arange(P)[:, None], np.arange(P)[None, :]
    put("ident", r == c)
    put("allow", np.where(r <= np.arange(S)[None, :], (2 * HD1) ** -0.5, 0.0))
    put("upper", r < c)
    put("ones", 1.0)
    put("block", r // HD1 == c // HD1)
    put("onesexp", np.concatenate([np.arange(32) < 16, np.arange(32) >= 16])[None, :])
    inv = (1.0 / np.float32(10000.0) ** (np.arange(0, HD, 2, dtype=np.float32) / np.float32(HD))).astype(np.float32)
    ang = (np.arange(S, dtype=np.float32)[:, None] * inv[None, :]).astype(np.float32)
    cos, sin = np.cos(ang), np.sin(ang)
    tiled = lambda a: a.reshape(TT, P, HD).transpose(1, 0, 2).reshape(P, TT * HD)
    put("cos", tiled(np.concatenate([cos, cos], 1)))
    put("sin", tiled(np.concatenate([-sin, sin], 1)))
    put("pm", np.where(r // HD1 % 2 == 0, 1.0, -1.0))
    put("half", -0.5)
    put("kth", np.arange(NT)[None, :] * float(P))
    put("tile", np.arange(TILES)[None, :])
    put("token", np.arange(NT)[None, :] * P + r)
    put("left", -MAGIC64 / 256)
    put("right", -MAGIC64 / 256 + 0.25)
    b = np.zeros((P, CB_N), np.float32)
    b[:, 0:P] = r == c
    b[:, P + P:P + S] = np.where(c > r, -1e30, 0.0)
    b[:, P + S:P + S + P] = np.where(r > c, -1e30, 0.0)
    sel = np.zeros((P, H, P), np.float32)
    for part in range(2):
        for h in range(H):
            sel[part * H + h, h, :] = 1.0
    b[:, P + 2 * S:] = sel.reshape(P, H * P)
    return f, b.astype(mybir.dt.np(BF16))


def decoder(nc, a, out):
    ctx = ExitStack()
    with ctx:
        def sb(name, shape, dt=F32, stack=ctx):
            return stack.enter_context(nc.sbuf_tensor(name, shape, dt))

        sems = {}

        def sem(name, j=None):
            if j is not None:
                name = f"{PLACE[name][0]}_{j}"
            if name not in sems:
                sems[name] = ctx.enter_context(nc.semaphore(name))
            return sems[name]

        residual_dram = nc.dram_tensor("residual_rows", (N, D), F32, kind="Internal").ap()
        h2_dram = nc.dram_tensor("h2_rows", (N, D), F32, kind="Internal").ap()
        token_dram = nc.dram_tensor("token_of_row", (ROWS, 1), I32, kind="Internal").ap()

        cf = sb("cf", [P, CF_N])
        cb = sb("cb", [P, CB_N], BF16)
        logits = sb("logits", [P, NT, E])
        w_up = sb("w_up", [P, KT, E * 2 * FFE])

        def const(name, rows=P):
            o, w = CF[name]
            return cf[0:rows, o:o + w]

        identb = cb[:, 0:P]
        neg_qk = cb[:, P:P + S]
        neg_kq = cb[:, P + S:P + 2 * S]
        selh = cb[:, P + 2 * S:].rearrange("p (h k) -> p h k", h=H)
        ident = const("ident")

        ps = [ctx.enter_context(nc.psum_tensor(f"ps{j}", [P, 2048], F32)) for j in range(2)]
        psb = [t[:, :].bitcast(BF16) for t in ps]

        part_one(nc, a, ctx, sb, sem, ps, psb, const, identb, neg_qk, neg_kq, selh, ident, cf, cb, w_up,
                 logits, residual_dram, h2_dram)
        part_two(nc, a, ctx, sb, sem, ps, w_up, const, ident, logits, residual_dram, h2_dram, token_dram, out)


def part_one(nc, a, ctx, sb0, sem, ps, psb, const, identb, neg_qk, neg_kq, selh, ident, cf, cb, w_up,
             logits, residual_dram, h2_dram):
    with ExitStack() as one:
        def sb(name, shape, dt=F32):
            return sb0(name, shape, dt, one)

        wt, used = {}, [0, 0]
        for name, rows, cols in (("a0_qkv", D, 3 * D), ("a0_proj", D, D), ("x0_q", D, D), ("x0_kv", D, 2 * D),
                                 ("x0_proj", D, D), ("f_w1", D, FF0), ("f_w2", FF0, D),
                                 ("a1_v", D, D), ("a1_o", D, D), ("x1_q", D, D), ("x1_k", D, D), ("x1_v", D, D),
                                 ("x1_o", D, D), ("m_qkv", D, 3 * D), ("m_proj", D, D)):
            half, n = (0 if name[0] == "f" or name[1] == "0" else 1), rows // P * cols
            wt[name] = w_up[:, half, used[half]:used[half] + n].rearrange("p (t n) -> p t n", n=cols)
            used[half] += n
        wf = {s: w_up[:, 1, used[1] + 2 * KT * D * i:used[1] + 2 * KT * D * (i + 1)].rearrange("p (t n) -> p t n", t=KT)
              for i, s in enumerate("qk")}
        rows_of = {}
        for name in ("a0_b", "x0_b", "f_b2", "x1_bq", "x1_bk", "x1_bv", "x1_bo", "m_ln2_w", "m_ln2_b"):
            if name[:2] == "x1":
                rows_of[name] = w_up[:, 1, E * 2 * FFE - D * (1 + len(rows_of) % 4):][:, 0:D]
            else:
                rows_of[name] = sb("r_" + name, [P, D])
        f_b1 = sb("f_b1", [P, FF0 // P])
        fmb = {s: sb(f"fmb_{s}", [P, 1]) for s in "qk"}
        rmsw = sb("rmsw", [P, 1])
        ln1w = sb("ln1w", [P, KT])
        ln1b = sb("ln1b", [P, KT])
        convw = sb("convw", [P, KT, 3])
        routw = sb("routw", [P, E, D])

        two = range(2)
        xin = [sb(f"xin{j}", [P, TT, D]) for j in two]
        cin = [sb(f"cin{j}", [C, D]) for j in two]
        bkin = [sb(f"bkin{j}", [C, 1], U8) for j in two]
        fkin = [sb(f"fkin{j}", [P, TT, C]) for j in two]
        ctxT = [sb(f"ctxT{j}", [P, KT, C]) for j in two]
        bkneg = [sb(f"bkneg{j}", [C, 1]) for j in two]
        fk4 = [sb(f"fk4{j}", [P, TT, C]) for j in two]
        fk4T = [sb(f"fk4T{j}", [C, S]) for j in two]
        x = [sb(f"x{j}", [P, TT, D]) for j in two]
        xb = [sb(f"xb{j}", [P, TT, D]) for j in two]
        r = [sb(f"r{j}", [P, TT, D]) for j in two]
        xT = [sb(f"xT{j}", [P, KT, S]) for j in two]
        bn = [sb(f"bn{j}", [P, TT, 6]) for j in two]
        mv = [sb(f"mv{j}", [P, TT, 2]) for j in two]
        rstd = [sb(f"rstd{j}", [P, TT]) for j in two]
        mx = [sb(f"mx{j}", [P, TT, H]) for j in two]
        mn = [sb(f"mn{j}", [P, TT, P], BF16) for j in two]
        mT = [sb(f"mT{j}", [P, S], BF16) for j in two]
        oT = [sb(f"oT{j}", [P, 512]) for j in two]
        rden = [t[:, :, :].rearrange("p t n -> p (t n)") for t in r]
        vexp = [sb(f"vexp{j}", [P, TT, H * 32]) for j in two]
        big = [sb(f"big{j}", [P, 6144]) for j in two]
        qkT = [sb(f"qkT{j}", [P, 2, H, S], BF16) for j in two]
        lg = [sb(f"lg{j}", [P, TT * E]) for j in two]
        setup_dma = sem("weights_loaded")
        settled_wait = settler(sem)

        loads = []

        def queue(dst, src):
            loads.append((dst, src))

        rest = []

        def later(dst, src):
            rest.append((dst, src))

        FIRST = ("a0_qkv", "a0_proj", "a0_b", "x0_b", "f_b2")
        queue(cf[:, :], a["cf"])
        queue(cb[:, :], a["cb"])
        for name, t in wt.items():
            (queue if name in FIRST else later)(t[:, :, :], a[name].rearrange("(t p) n -> p t n", p=P))
        for name, t in rows_of.items():
            (queue if name in FIRST else later)(t[:, :], a[name].rearrange("(o n) -> o n", o=1).broadcast_to([P, D]))
        queue(f_b1[:, :], a["f_b1"])
        later(ln1w[:, :], a["m_ln1_w"])
        later(ln1b[:, :], a["m_ln1_b"])
        later(convw[:, :, :], a["m_conv"])
        for e in range(E):
            later(routw[:, e, :], a["m_router"][e:e + 1, :].broadcast_to([P, D]))
        raw_w = {s: big[0][:, 512 * i:512 * i + 512].rearrange("p (t n) -> p t n", t=KT) for i, s in enumerate("qk")}
        diag = {s: big[0][:, 1024 + P * i:1024 + P * i + P] for i, s in enumerate("qk")}
        for s in "qk":
            queue(raw_w[s], a[f"a1_{s}"].rearrange("(t p) n -> p t n", p=P))
            for g in range(4):
                queue(fmb[s][32 * g:32 * g + 32, :], a[f"a1_fm{s}_b"].rearrange("(n o) -> n o", o=1))
        for g in range(4):
            later(rmsw[32 * g:32 * g + 32, :], a["a1_rms"].rearrange("(n o) -> n o", o=1))
        diag_loads = [(diag[s][32 * g:32 * g + 32, 32 * g:32 * g + 32], a[f"a1_fm{s}T"])
                      for s in "qk" for g in range(4)]
        LOADED = 16 * (len(loads) + len(diag_loads))
        REST_LOADED = 16 * len(rest)

        block = one.enter_context(nc.Block())

        def tiles2(ap, n):
            return ap.rearrange("p (t n) -> p t n", n=n)

        def stack_view(j, which):
            o = which * 3136
            t = big[j][:, o // 2:o // 2 + TT * H * W // 2].bitcast(BF16)
            g = t.rearrange("p (g w) -> p g w", w=W)
            return g, g[:, :, 0:KS].rearrange("p g (a d) -> p g a d", d=HD)

        def qk32(j, which):
            o = 3136 + 512 * which
            return big[j][:, o:o + 512]

        def qk32_both(j):
            return big[j][:, 3136:3136 + 1024]

        def rope_tmp(j, i):
            o = 5184 if i == 0 else 4160
            return big[j][:, o:o + 512]

        def rem(j, which):
            o = 4160 + 512 * which
            return big[j][:, o:o + 512]

        def probs(j, kb):
            if kb == 0:
                return big[j][:, 0:4096].rearrange("p (h q) -> p h q", h=H)
            return big[j][:, 4096:6144].rearrange("p (h q) -> p h q", h=H)

        vview = [t[:, :, :].rearrange("p t (g w) -> p t g w", w=64) for t in vexp]
        onesexp = const("onesexp").rearrange("p (a w) -> p a w", a=2)

        ffn = [[big[j][:, 2048 * i:2048 * i + 2048] for i in range(3)]
               + [qkT[j][:, i, :, :].rearrange("p h s -> p (h s)").bitcast(F32) for i in range(2)] for j in two]
        qF = [big[j][:, 0:1024].rearrange("p (m s) -> p m s", m=4) for j in two]
        kF = [big[j][:, 1024:3072].rearrange("p (m a s) -> p m a s", m=4, a=2) for j in two]
        aT = [[big[j][:, 3072:5120].rearrange("p (h q) -> p h q", h=H1),
               big[j][:, 5120:6144].rearrange("p (h q) -> p h q", h=H1)] for j in two]
        v1 = [qkT[j][:, 0, :, :].rearrange("p h s -> p (h s)").bitcast(F32)[:, 0:512] for j in two]
        sq1 = [qkT[j][:, 0, :, :].rearrange("p h s -> p (h s)").bitcast(F32)[:, 512:1024] for j in two]
        qT0 = [big[j][:, 0:512].rearrange("p (t s) -> p t s", t=KT) for j in two]
        kT0 = [big[j][:, 512:1024].rearrange("p (t s) -> p t s", t=KT) for j in two]
        v0 = [big[j][:, 1024:1536].rearrange("p (t s) -> p t s", t=TT) for j in two]
        p0 = [big[j][:, 1536:2048].rearrange("p (t s) -> p t s", t=TT) for j in two]
        p0T = [big[j][:, 2048:2560].rearrange("p (t s) -> p t s", t=TT) for j in two]
        o0 = [big[j][:, 2560:3072].rearrange("p (t s) -> p t s", t=TT) for j in two]
        sm0 = [big[j][:, 3072:3080] for j in two]
        ms = [big[j][:, 0:H * C].rearrange("p (a b c) -> p a b c", a=4, b=4) for j in two]
        hpad = [big[j][:, 0:2 * (S + 2)].rearrange("p (t s) -> p t s", t=KT) for j in two]
        h1n = [big[j][:, 1024:1536].rearrange("p (t s) -> p t s", t=TT) for j in two]

        @block.tensor
        def _(pe):
            pe.wait_ge(setup_dma, LOADED)
            for i, s in enumerate("qk"):
                for t in range(KT):
                    for g in range(KT):
                        mm = pe.matmul(ps[0][:, 512 * i + 256 * t + P * g:512 * i + 256 * t + P * g + P],
                                       raw_w[s][:, g, P * t:P * t + P], diag[s], start=True, stop=True)
            mm.then_inc(sem("folded_maps"), 1)
            pe.wait_ge(sem("setup_act"), 1)
            pe.wait_ge(sem("setup_pool"), 1)

            def transposed(src, dst, signal):
                for kt in range(KT):
                    for tt in range(TT):
                        mm = pe.transpose(dst[:, kt * S + tt * P:kt * S + tt * P + P],
                                          src[:, tt, kt * P:kt * P + P], ident)
                mm.then_inc(signal, 1)

            def rows_product(dst, lhs, weight, cols, signal=None):
                n = cols.stop - cols.start
                for tt in range(TT):
                    for kt in range(KT):
                        mm = pe.matmul(dst[:, tt * n:tt * n + n], lhs[:, kt, tt * P:tt * P + P],
                                       weight[:, kt, cols], start=kt == 0, stop=kt == KT - 1)
                if signal is not None:
                    mm.then_inc(signal, 1)

            def start(j, n):
                pe.wait_ge(sem(f"inputs_loaded{j}"), n.loaded())
                transposed(xin[j], ps[j], sem("x_transposed", j))
                for kt in range(KT):
                    mm = pe.transpose(ps[j][:, 512 + kt * C:512 + kt * C + C], cin[j][:, kt * P:kt * P + P],
                                      ident[0:C, 0:C])
                mm.then_inc(sem("ctx_transposed", j), 1)

            def mask_transposes(j, n):
                pe.wait_ge(sem("fk4", j), n("fk4"))
                for tt in range(TT):
                    mm = pe.transpose(ps[j][0:C, 1024 + tt * P:1024 + tt * P + P], fk4[j][:, tt, :], ident)
                mm.then_inc(sem("fk4_transposed", j), 1)

            def a0_qkv(j, n):
                pe.wait_ge(sem("start_xT", j), n("start_xT"))
                pe.wait_ge(sem("start_ctxT", j), n("start_ctxT"))
                w = wt["a0_qkv"]
                for i in range(2):
                    for m in range(KT):
                        for kt in range(KT):
                            mm = pe.matmul(ps[j][:, 512 * i + S * m:512 * i + S * m + S],
                                           w[:, kt, D * i + P * m:D * i + P * m + P], xT[j][:, kt, :],
                                           start=kt == 0, stop=kt == KT - 1)
                rows_product(ps[j][:, 1024:1536], xT[j], w, slice(2 * D, 3 * D), sem("a0_qkv", j))

            def a0_scores(j, n):
                pe.wait_ge(sem("a0_qT", j), n("a0_qT"))
                pe.wait_ge(sem("a0_kT_v", j), n("a0_kT_v"))
                for tt in range(TT):
                    for kt in range(KT):
                        mm = pe.matmul(ps[j][:, tt * S:tt * S + S], qT0[j][:, kt, tt * P:tt * P + P],
                                       kT0[j][:, kt, :], start=kt == 0, stop=kt == KT - 1)
                mm.then_inc(sem("a0_scores", j), 1)

            def a0_pT(j, n):
                pe.wait_ge(sem("a0_exp", j), n("a0_exp"))
                transposed(p0[j], ps[j], sem("a0_p_transposed", j))

            def a0_pv(j, n):
                pe.wait_ge(sem("a0_pT", j), n("a0_pT"))
                rows_product(ps[j][:, 0:512], p0T[j], v0[j], slice(0, D), sem("a0_pv", j))

            def a0_proj(j, n):
                pe.wait_ge(sem("a0_o", j), n("a0_o"))
                rows_product(ps[j][:, 0:512], o0[j], wt["a0_proj"], slice(0, D), sem("a0_y", j))

            def x_transposes(s):
                def step(j, n):
                    pe.wait_ge(sem(f"{s}_normed", j), n(f"{s}_normed"))
                    transposed(x[j], ps[j], sem(f"{s}_transposed", j))
                return step

            def cross_qkv(s, wq, wk, wv, prev):
                def step(j, n):
                    if s == "x0":
                        pe.wait_ge(sem("rest_loaded"), REST_LOADED)
                    pe.wait_ge(sem(f"{prev}_xT", j), n(f"{prev}_xT"))
                    rows_product(ps[j][:, 0:512], xT[j], wq, slice(0, D))
                    if s == "x0":
                        pe.wait_ge(sem("fk4_T", j), n("fk4_T"))
                    for i, w in enumerate((wk, wv)):
                        for kt in range(KT):
                            mm = pe.matmul(ps[j][0:C, 512 + 512 * i:512 + 512 * i + D], ctxT[j][:, kt, :],
                                           w[:, kt, 0:D], start=kt == 0, stop=kt == KT - 1)
                    mm.then_inc(sem(f"{s}_qkv", j), 1)
                return step

            def causal_qkv(j, n):
                pe.wait_ge(sem("m_conv", j), n("m_conv"))
                rows_product(ps[j][:, 0:1024], xT[j], wt["m_qkv"], slice(0, 2 * D))
                rows_product(ps[j][:, 1024:1536], xT[j], wt["m_qkv"], slice(2 * D, 3 * D), sem("m_qkv", j))

            def q_transposes(s, rows):
                def step(j, n):
                    pe.wait_ge(sem(f"{s}_q_stack", j), n(f"{s}_q_stack"))
                    if s == "x0":
                        pe.wait_ge(sem("x0_rows", j), n("x0_rows"))
                    pe.wait_ge(sem(f"{s}_v", j), n(f"{s}_v"))
                    pe.wait_ge(sem(f"{s}_k_stack", j), n(f"{s}_k_stack"))
                    if s == "m":
                        pe.wait_ge(sem("m_k_part3", j), n("m_k_part3"))
                    g, _ = stack_view(j, 0)
                    for h in range(H):
                        for tt in range(TT):
                            mm = pe.transpose(psb[j][0:rows, h * S + tt * P:h * S + tt * P + P],
                                              g[:, tt * H + h, 0:rows], identb)
                    mm.then_inc(sem(f"{s}_q_transposed", j), 1)
                return step

            def k_transposes(s, rows, cross):
                def step(j, n):
                    pe.wait_ge(sem(f"{s}_qT_act", j), n(f"{s}_qT_act"))
                    pe.wait_ge(sem(f"{s}_qT_dve", j), n(f"{s}_qT_dve"))
                    g, _ = stack_view(j, 1)
                    for h in range(H):
                        if cross:
                            mm = pe.transpose(psb[j][0:rows, h * S:h * S + C], g[0:C, h, 0:rows],
                                              identb[0:C, 0:C])
                        else:
                            for tt in range(TT):
                                mm = pe.transpose(psb[j][0:rows, h * S + tt * P:h * S + tt * P + P],
                                                  g[:, tt * H + h, 0:rows], identb)
                    mm.then_inc(sem(f"{s}_k_transposed", j), 1)
                return step

            def cross_scores(s, rows, tt):
                def step(j, n):
                    if tt == 0:
                        pe.wait_ge(sem(f"{s}_kT_act", j), n(f"{s}_kT_act"))
                        pe.wait_ge(sem(f"{s}_kT_dve", j), n(f"{s}_kT_dve"))
                    else:
                        pe.wait_ge(sem(f"{s}_max0", j), n(f"{s}_max0"))
                    for h in range(H):
                        o = 512 * (h // 4) + C * (h % 4)
                        mm = pe.matmul(ps[j][:, o:o + C], qkT[j][0:rows, 0, h, tt * P:tt * P + P],
                                       qkT[j][0:rows, 1, h, 0:C], start=True, stop=True)
                    mm.then_inc(sem(f"{s}_scores{tt}", j), 1)
                return step

            def causal_scores(part):
                def step(j, n):
                    if part == 0:
                        pe.wait_ge(sem("m_kT_act", j), n("m_kT_act"))
                        pe.wait_ge(sem("m_kT_dve", j), n("m_kT_dve"))
                    else:
                        pe.wait_ge(sem(f"m_max{part - 1}", j), n(f"m_max{part - 1}"))
                    heads, tt, nk = (8, 1, S) if part < 2 else (16, 0, P)
                    per = 512 // nk
                    neg = neg_qk if part < 2 else neg_qk[:, P:S]
                    for bank in range(4):
                        bk = ps[j][:, 512 * bank:512 * bank + 512]
                        pe.matmul(bk.rearrange("p (a k) -> p a k", a=per), identb,
                                  neg.unsqueeze(1).broadcast_to([P, per, nk]), start=True, stop=False)
                        for i in range(per):
                            h = (8 * part if part < 2 else 0) + bank * per + i
                            mm = pe.matmul(bk[:, nk * i:nk * i + nk], qkT[j][0:KS, 0, h, tt * P:tt * P + P],
                                           qkT[j][0:KS, 1, h, 0:nk], start=False, stop=i == per - 1)
                    mm.then_inc(sem(f"m_scores{part}", j), 1)
                return step

            def max_transposes(s):
                def step(j, n):
                    pe.wait_ge(sem(f"{s}_minus_max", j), n(f"{s}_minus_max"))
                    for tt in range(TT):
                        mm = pe.transpose(psb[j][:, tt * P:tt * P + P], mn[j][:, tt, :], identb)
                    mm.then_inc(sem(f"{s}_max_transposed", j), 1)
                return step

            def cross_scores_t(s, rows, part):
                def step(j, n):
                    pe.wait_ge(sem(f"{s}_mT" if part == 0 else f"{s}_exp0", j), n(f"{s}_mT" if part == 0 else f"{s}_exp0"))
                    for i in range(8):
                        h = 8 * part + i
                        pe.matmul(ps[j][0:C, S * i:S * i + S], qkT[j][0:rows, 1, h, 0:C],
                                  qkT[j][0:rows, 0, h, :], start=True, stop=False)
                        mm = pe.matmul(ps[j][0:C, S * i:S * i + S], selh[:, h, 0:C], mT[j][:, :],
                                       start=False, stop=True)
                    mm.then_inc(sem(f"{s}_scores_t{part}", j), 1)
                return step

            def causal_scores_t(part):
                def step(j, n):
                    pe.wait_ge(sem("m_mT" if part == 0 else f"m_exp{part - 1}", j), n("m_mT" if part == 0 else f"m_exp{part - 1}"))
                    kb, q0 = (0, 0) if part < 2 else (1, P)
                    nq = S - q0
                    per = 512 // nq
                    for bank in range(4):
                        bk = ps[j][:, 512 * bank:512 * bank + 512]
                        pe.matmul(bk.rearrange("p (a k) -> p a k", a=per), identb,
                                  neg_kq[:, 0:nq].unsqueeze(1).broadcast_to([P, per, nq]), start=True, stop=False)
                        for i in range(per):
                            h = (8 * part if part < 2 else 0) + bank * per + i
                            o = bk[:, nq * i:nq * i + nq]
                            pe.matmul(o, qkT[j][0:KS, 1, h, kb * P:kb * P + P], qkT[j][0:KS, 0, h, q0:S],
                                      start=False, stop=False)
                            mm = pe.matmul(o, selh[:, h, :], mT[j][:, q0:S], start=False, stop=i == per - 1)
                    mm.then_inc(sem(f"m_scores_t{part}", j), 1)
                return step

            def weigh_values(s, cross):
                def step(j, n):
                    pe.wait_ge(sem(f"{s}_exp{1 if cross else 2}", j), n(f"{s}_exp{1 if cross else 2}"))
                    kbs = ((0, 0, C),) if cross else ((0, 0, P), (1, P, P))
                    for bank in range(2):
                        for half in range(2):
                            todo = [(par, kb) for kb in kbs for par in range(2)]
                            for i, (par, (kb, q0, nk)) in enumerate(todo):
                                for strip in range(4):
                                    h = 8 * half + 2 * strip + par
                                    lhs = (vexp[j][0:nk, kb, 32 * h:32 * h + 32] if bank == 0
                                           else onesexp[0:nk, par, :])
                                    mm = pe.matmul(
                                        ps[j][32 * strip:32 * strip + 32,
                                              512 * bank + S * half + q0:512 * bank + S * half + S],
                                        lhs, probs(j, kb)[0:nk, h, :], start=i == 0, stop=i == len(todo) - 1)
                    mm.then_inc(sem(f"{s}_pv", j), 1)
                return step

            def out_proj(s, w):
                def step(j, n):
                    pe.wait_ge(sem(f"{s}_oT", j), n(f"{s}_oT"))
                    rows_product(ps[j][:, 0:512], oT[j][:, :].rearrange("p (t s) -> p t s", t=2), w,
                                 slice(0, D), sem(f"{s}_y", j))
                return step

            def f_up(j, n):
                pe.wait_ge(sem("x0_xT", j), n("x0_xT"))
                for m in range(FF0 // P):
                    for kt in range(KT):
                        mm = pe.matmul(ps[j][:, S * m:S * m + S], wt["f_w1"][:, kt, P * m:P * m + P],
                                       xT[j][:, kt, :], start=kt == 0, stop=kt == KT - 1)
                    if m % 4 == 3:
                        mm.then_inc(sem("f_h0" if m < 4 else "f_h1", j), 1)

            def f_down(j, n):
                h = ffn[j][0].rearrange("p (m s) -> p m s", s=S)
                for half in range(2):
                    pe.wait_ge(sem(f"f_hT{half}", j), n(f"f_hT{half}"))
                    for tt in range(TT):
                        for m in range(4 * half, 4 * half + 4):
                            mm = pe.matmul(ps[j][:, tt * 512:tt * 512 + D], h[:, m, tt * P:tt * P + P],
                                           wt["f_w2"][:, m, :], start=m == 0, stop=m == FF0 // P - 1)
                mm.then_inc(sem("f_y", j), 1)

            def l_features(j, n):
                pe.wait_ge(sem("f_xT", j), n("f_xT"))
                for i, s in enumerate("qk"):
                    for m in range(4):
                        for kt in range(KT):
                            mm = pe.matmul(ps[j][:, 1024 * i + S * m:1024 * i + S * m + S],
                                           wf[s][:, kt, P * m:P * m + P], xT[j][:, kt, :],
                                           start=kt == 0, stop=kt == KT - 1)
                mm.then_inc(sem("l_maps", j), 1)

            def l_scores0(j, n):
                pe.wait_ge(sem("l_features", j), n("l_features"))
                for h in range(H1):
                    mm = pe.matmul(ps[j][:, S * h:S * h + S], kF[j][:, h // 2, h % 2, 0:P],
                                   qF[j][:, h // 2, :], start=True, stop=True)
                mm.then_inc(sem("l_scores0", j), 1)

            def l_scores1(j, n):
                pe.wait_ge(sem("l_masked0", j), n("l_masked0"))
                for h in range(H1):
                    mm = pe.matmul(ps[j][:, P * h:P * h + P], kF[j][:, h // 2, h % 2, P:S],
                                   qF[j][:, h // 2, P:S], start=True, stop=True)
                mm.then_inc(sem("l_scores1", j), 1)
                rows_product(ps[j][:, 1024:1536], xT[j], wt["a1_v"], slice(0, D), sem("l_v_product", j))

            def l_values(j, n):
                pe.wait_ge(sem("l_masked1", j), n("l_masked1"))
                pe.wait_ge(sem("l_v", j), n("l_v"))
                for half in range(2):
                    for kb, q0 in ((0, 0), (1, P)):
                        for strip in range(4):
                            h = 4 * half + strip
                            mm = pe.matmul(ps[j][32 * strip:32 * strip + 32, S * half + q0:S * half + S],
                                           v1[j][:, kb * D + 32 * h:kb * D + 32 * h + 32],
                                           aT[j][kb][:, h, :], start=kb == 0, stop=kb == 1)
                mm.then_inc(sem("l_o", j), 1)

            def l_squares(j, n):
                pe.wait_ge(sem("l_squared", j), n("l_squared"))
                pe.matmul(ps[j][:, 512:1024], const("block"), sq1[j], start=True, stop=True)\
                    .then_inc(sem("l_square_sums", j), 1)

            def m_transposes(j, n):
                pe.wait_ge(sem("m_h", j), n("m_h"))
                transposed(h1n[j], ps[j], sem("m_transposed", j))

            def guard(j, n):
                pe.wait_ge(sem("m_x", j), n("m_x"))

            def cross_steps(s, first, rows, wq, wk, wv, prev, wo):
                steps = [cross_qkv(s, wq, wk, wv, prev), q_transposes(s, rows), k_transposes(s, rows, True),
                         cross_scores(s, rows, 0), cross_scores(s, rows, 1), max_transposes(s),
                         cross_scores_t(s, rows, 0), cross_scores_t(s, rows, 1), weigh_values(s, True),
                         out_proj(s, wo)]
                return list(enumerate(steps, first))

            schedule = Schedule(
                list(enumerate([start, a0_qkv, a0_scores, a0_pT, a0_pv, a0_proj, x_transposes("a0")], A0))
                + [(A0 + 6.2, mask_transposes)]
                + cross_steps("x0", X0, KS + 1, wt["x0_q"], wt["x0_kv"], wt["x0_kv"][:, :, D:2 * D], "a0",
                              wt["x0_proj"])
                + [(X0 + 10, x_transposes("x0")), (F, f_up), (L - 2, f_down), (L - 1, x_transposes("f"))]
                + list(enumerate([l_features, l_scores0, l_scores1, l_values, l_squares, out_proj("l", wt["a1_o"]),
                                  x_transposes("l")], L))
                + cross_steps("x1", X1, KS, wt["x1_q"], wt["x1_k"], wt["x1_v"], "l", wt["x1_o"])
                + list(enumerate([m_transposes, causal_qkv, q_transposes("m", KS), k_transposes("m", KS, False),
                                  causal_scores(0), causal_scores(1), causal_scores(2), max_transposes("m"),
                                  causal_scores_t(0), causal_scores_t(1), causal_scores_t(2),
                                  weigh_values("m", False), out_proj("m", wt["m_proj"]), guard], M)))
            schedule.first(Count(pe, 0))
            with pe.Fori(0, ROUNDS - 1) as i:
                schedule.round(Count(pe, i))
            schedule.round(Count(pe, ROUNDS - 1), last=True)

        @block.scalar
        def _(act):
            act.wait_ge(sem("folded_maps"), 1)
            for i, s in enumerate("qk"):
                for t in range(KT):
                    for dup in range(2):
                        src = ps[0][:, 512 * i + 256 * t:512 * i + 256 * t + 256].rearrange("p (h e) -> p h e", e=32)
                        dst = wf[s][:, t, :].rearrange("p (h a e) -> p h a e", a=2, e=32)[:, :, dup, :]
                        last = act.activation(dst, src, ACT.Copy)
            last.then_inc(sem("setup_act"), 1)
            act.wait_ge(sem("setup_pool"), 1)

            def copy_xT(s, signal):
                def step(j, n):
                    act.wait_ge(sem(f"{s}_transposed", j), n(f"{s}_transposed"))
                    act.activation(xT[j][:, :, :].rearrange("p t s -> p (t s)"), ps[j][:, 0:512], ACT.Copy)\
                        .then_inc(sem(signal, j), 1)
                return step

            def a0_qT(j, n):
                act.wait_ge(sem("a0_qkv", j), n("a0_qkv"))
                act.activation(big[j][:, 0:512], ps[j][:, 0:512], ACT.Copy).then_inc(sem("a0_qT", j), 1)

            def a0_exp(j, n):
                act.wait_ge(sem("a0_minus_max", j), n("a0_minus_max"))
                for tt in range(TT):
                    last = act.activation(p0[j][:, tt, :], ps[j][:, tt * S:tt * S + S], ACT.Exp,
                                          bias=sm0[j][:, tt:tt + 1], scale=HD ** -0.5,
                                          accum_out=sm0[j][:, 2 + tt:3 + tt])
                last.then_inc(sem("a0_exp", j), 1)

            def a0_pT(j, n):
                act.wait_ge(sem("a0_p_transposed", j), n("a0_p_transposed"))
                act.activation(big[j][:, 2048:2560], ps[j][:, 0:512], ACT.Copy).then_inc(sem("a0_pT", j), 1)

            def first_parts(s, cross):
                def step(j, n):
                    for which, c in ((0, "q"), (1, "k")):
                        rows = C if cross and which else P
                        g = H if cross and which else TT * H
                        _, st = stack_view(j, which)
                        src = qk32(j, which).rearrange("p (g d) -> p g d", d=HD)
                        act.wait_ge(sem(f"{s}_{c}32", j), n(f"{s}_{c}32"))
                        act.activation(st[0:rows, 0:g, 0, :], src[0:rows, 0:g, :], ACT.Copy)\
                            .then_inc(sem(f"{s}_{c}_part1", j), 1)
                return step

            def values(s, cross):
                def step(j, n):
                    act.wait_ge(sem(f"{s}_qkv", j), n(f"{s}_qkv"))
                    rows = C if cross else P
                    nt = 1 if cross else TT
                    vp = ps[j][0:rows, 1024:1024 + nt * D].rearrange("p (t g a d) -> p t g a d", t=nt, a=2, d=HD)
                    if s == "x1":
                        act.wait_ge(sem("x1_v32", j), n("x1_v32"))
                        vp = rden[j][0:rows, 0:D].rearrange("p (t g a d) -> p t g a d", t=nt, a=2, d=HD)
                    for t in range(nt):
                        act.activation(vview[j][0:rows, t, :, 0:16], vp[:, t, :, 0, :], ACT.Copy)
                        last = act.activation(vview[j][0:rows, t, :, 48:64], vp[:, t, :, 1, :], ACT.Copy)
                    last.then_inc(sem(f"{s}_v", j), 1)
                return step

            def second_parts(s, cross):
                def step(j, n):
                    for which, c in ((0, "q"), (1, "k")):
                        rows = C if cross and which else P
                        g = H if cross and which else TT * H
                        _, st = stack_view(j, which)
                        second = SECOND[which]
                        act.wait_ge(sem(f"{s}_{c}_rest", j), n(f"{s}_{c}_rest"))
                        src = rem(j, which).rearrange("p (g d) -> p g d", d=HD)
                        act.activation(st[0:rows, 0:g, second, :], src[0:rows, 0:g, :], ACT.Copy)\
                            .then_inc(sem(f"{s}_{c}_part2", j), 1)
                return step

            def qT_copy(s, rows):
                def step(j, n):
                    act.wait_ge(sem(f"{s}_q_transposed", j), n(f"{s}_q_transposed"))
                    act.activation(qkT[j][0:rows, 0, 0:8, :].rearrange("p h s -> p (h s)"),
                                   psb[j][0:rows, 0:2048], ACT.Copy).then_inc(sem(f"{s}_qT_act", j), 1)
                return step

            def kT_copy(s, rows, cross):
                def step(j, n):
                    act.wait_ge(sem(f"{s}_k_transposed", j), n(f"{s}_k_transposed"))
                    nk = C if cross else S
                    act.activation(qkT[j][0:rows, 1, 0:8, 0:nk],
                                   psb[j][0:rows, 0:2048].rearrange("p (h s) -> p h s", s=S)[:, :, 0:nk],
                                   ACT.Copy).then_inc(sem(f"{s}_kT_act", j), 1)
                return step

            def x0_exp(part):
                def step(j, n):
                    act.wait_ge(sem(f"x0_scores_t{part}", j), n(f"x0_scores_t{part}"))
                    act.activation(probs(j, 0)[0:C, 8 * part:8 * part + 8, :].rearrange("p h q -> p (h q)"),
                                   ps[j][0:C, :], ACT.Exp, scale=HD ** -0.5).then_inc(sem(f"x0_exp{part}", j), 1)
                return step

            def x1_exp(part):
                def step(j, n):
                    act.wait_ge(sem(f"x1_masked_t{part}", j), n(f"x1_masked_t{part}"))
                    p = probs(j, 0)[0:C, 8 * part:8 * part + 8, :].rearrange("p h q -> p (h q)")
                    act.activation(p, p, ACT.Exp, scale=HD ** -0.5).then_inc(sem(f"x1_exp{part}", j), 1)
                return step

            def m_exp(part):
                def step(j, n):
                    act.wait_ge(sem(f"m_scores_t{part}", j), n(f"m_scores_t{part}"))
                    act.activation(big[j][:, 2048 * part:2048 * part + 2048], ps[j][:, :], ACT.Exp,
                                   scale=HD ** -0.5).then_inc(sem(f"m_exp{part}", j), 1)
                return step

            def inverse(s):
                def step(j, n):
                    act.wait_ge(sem(f"{s}_pv", j), n(f"{s}_pv"))
                    act.activation(rden[j], ps[j][:, 512:1024], ACT.Ln).then_inc(sem(f"{s}_ln", j), 1)
                    act.wait_ge(sem(f"{s}_ln", j), n(f"{s}_ln"))
                    act.activation(rden[j], rden[j], ACT.Exp, scale=-1.0).then_inc(sem(f"{s}_inverse", j), 1)
                return step

            def f_bias(j, n):
                for m in range(FF0 // P):
                    if m % 4 == 0:
                        act.wait_ge(sem("f_h0" if m < 4 else "f_h1", j), n("f_h0" if m < 4 else "f_h1"))
                    last = act.activation(ffn[j][0][:, S * m:S * m + S], ps[j][:, S * m:S * m + S],
                                          ACT.Identity, bias=f_b1[:, m:m + 1], scale=256.0)
                last.then_inc(sem("f_h256", j), 1)

            def f_gelu(j, n):
                act.wait_ge(sem("f_index", j), n("f_index"))
                act.activation(ffn[j][3], ffn[j][1], ACT.Gelu, bias=const("left"), scale=1.0 / 256).then_inc(sem("f_left", j), 1)
                act.activation(ffn[j][4], ffn[j][1], ACT.Gelu, bias=const("right"), scale=1.0 / 256)\
                    .then_inc(sem("f_right", j), 1)

            def l_features(j, n):
                act.wait_ge(sem("l_maps", j), n("l_maps"))
                act.activation(big[j][:, 0:1024], ps[j][:, 0:1024], ACT.Exp, bias=fmb["q"][:, :],
                               scale=const("pm"))
                act.wait_ge(sem("l_zeros", j), n("l_zeros"))
                for s in range(2):
                    rows = slice(64 * s, 64 * s + 64)
                    last = act.activation(kF[j][rows, :, s, :],
                                          ps[j][rows, 1024:2048].rearrange("p (m s) -> p m s", s=S), ACT.Exp,
                                          bias=fmb["k"][rows, :], scale=const("pm")[rows, :])
                last.then_inc(sem("l_features", j), 1)

            def l_v(j, n):
                act.wait_ge(sem("l_v_product", j), n("l_v_product"))
                act.activation(v1[j], ps[j][:, 1024:1536], ACT.Copy).then_inc(sem("l_v", j), 1)

            def l_square(j, n):
                act.wait_ge(sem("l_o", j), n("l_o"))
                act.activation(sq1[j], ps[j][:, 0:512], ACT.Square).then_inc(sem("l_squared", j), 1)

            def l_ln(j, n):
                act.wait_ge(sem("l_mean_square", j), n("l_mean_square"))
                act.activation(rden[j][:, :], rden[j][:, :], ACT.Ln).then_inc(sem("l_ln", j), 1)

            def l_rms(j, n):
                act.wait_ge(sem("l_ln", j), n("l_ln"))
                act.activation(rden[j][:, :], rden[j][:, :], ACT.Exp, scale=-0.5).then_inc(sem("l_rms", j), 1)

            def m_affine(j, n):
                act.wait_ge(sem("m_transposed", j), n("m_transposed"))
                act.wait_ge(sem("m_pad", j), n("m_pad"))
                for kt in range(KT):
                    last = act.activation(hpad[j][:, kt, 2:S + 2], ps[j][:, kt * S:kt * S + S], ACT.Identity,
                                          bias=ln1b[:, kt:kt + 1], scale=ln1w[:, kt:kt + 1])
                last.then_inc(sem("m_affine", j), 1)

            def start_ctx(j, n):
                act.wait_ge(sem("x_transposed", j), n("x_transposed"))
                act.activation(xT[j][:, :, :].rearrange("p t s -> p (t s)"), ps[j][:, 0:512], ACT.Copy)\
                    .then_inc(sem("start_xT", j), 1)
                act.wait_ge(sem("ctx_transposed", j), n("ctx_transposed"))
                act.activation(ctxT[j][:, :, :].rearrange("p t s -> p (t s)"), ps[j][:, 512:512 + KT * C], ACT.Copy)\
                    .then_inc(sem("start_ctxT", j), 1)

            def mask_copy(j, n):
                act.wait_ge(sem("fk4_transposed", j), n("fk4_transposed"))
                act.activation(fk4T[j][:, :], ps[j][0:C, 1024:1024 + S], ACT.Copy).then_inc(sem("fk4_T", j), 1)

            schedule = Schedule([
                (A0, start_ctx), (A0 + 1, a0_qT), (A0 + 2, a0_exp), (A0 + 3, a0_pT), (A0 + 6, copy_xT("a0", "a0_xT")), (A0 + 6.4, mask_copy),
                (X0 + 0.3, first_parts("x0", True)), (X0 + 0.4, values("x0", True)),
                (X0 + 0.6, second_parts("x0", True)), (X0 + 1, qT_copy("x0", KS + 1)), (X0 + 2, kT_copy("x0", KS + 1, True)),
                (X0 + 6, x0_exp(0)), (X0 + 7, x0_exp(1)), (X0 + 8, inverse("x0")), (X0 + 10, copy_xT("x0", "x0_xT")),
                (F + 0.1, f_bias), (F + 0.4, f_gelu), (L - 1, copy_xT("f", "f_xT")),
                (L, l_features), (L + 2, l_v), (L + 3, l_square), (L + 4.2, l_ln), (L + 4.6, l_rms), (L + 6, copy_xT("l", "l_xT")),
                (X1 + 0.3, first_parts("x1", True)), (X1 + 0.4, values("x1", True)),
                (X1 + 0.6, second_parts("x1", True)), (X1 + 1, qT_copy("x1", KS)), (X1 + 2, kT_copy("x1", KS, True)),
                (X1 + 6, x1_exp(0)), (X1 + 7, x1_exp(1)), (X1 + 8, inverse("x1")),
                (M, m_affine), (M + 1 + 0.3, first_parts("m", False)), (M + 1 + 0.4, values("m", False)),
                (M + 1 + 0.6, second_parts("m", False)), (M + 2, qT_copy("m", KS)),
                (M + 3, kT_copy("m", KS, False)), (M + 8, m_exp(0)), (M + 9, m_exp(1)), (M + 10, m_exp(2)), (M + 11, inverse("m"))])
            schedule.first(Count(act, 0))
            with act.Fori(0, ROUNDS - 1) as i:
                schedule.round(Count(act, i))
            schedule.round(Count(act, ROUNDS - 1), last=True)

        @block.vector
        def _(dve):
            dve.wait_ge(setup_dma, LOADED)
            for j in two:
                dve.memset(vexp[j][:, :, :], 0.0)
                dve.memset(mn[j][:, :, :], 0.0)
            dve.tensor_scalar(f_b1[:, :], f_b1[:, :], 256.0, None, ALU.mult)
            for s in "qk":
                dve.tensor_scalar(fmb[s][:, :], fmb[s][:, :], const("pm"), None, ALU.mult)
            dve.tensor_scalar(rows_of["f_b2"][:, :], rows_of["f_b2"][:, :], 256.0, None, ALU.mult)\
                .then_inc(sem("setup_dve"), 1)
            dve.wait_ge(sem("setup_dve"), 1)
            dve.wait_ge(sem("setup_act"), 1)
            dve.wait_ge(sem("setup_pool"), 1)

            chain = {"base": None, "n": 0}

            def link(ins, held=False):
                chain["n"] += 1
                ins.then_inc(sem("dve_chain"), 1)
                if held:
                    settled_wait(dve, sem("dve_chain"), chain["base"] + chain["n"])
                else:
                    dve.wait_ge(sem("dve_chain"), chain["base"] + chain["n"])

            def moments(s, j):
                for tt in range(TT):
                    ins = dve.bn_stats(bn[j][:, tt, :], r[j][:, tt, :])
                link(ins, True)
                for tt in range(TT):
                    ins = dve.bn_aggr(mv[j][:, tt, :], bn[j][:, tt, :])
                ins.then_inc(sem(f"{s}_moments", j), 1)

            def normalised(s, j, n, dst, signal):
                dve.wait_ge(sem(f"{s}_rstd", j), n(f"{s}_rstd"))
                for tt in range(TT):
                    ins = dve.tensor_scalar(dst[:, tt, :], r[j][:, tt, :], mv[j][:, tt, 0:1], rstd[j][:, tt:tt + 1],
                                            ALU.subtract, ALU.mult)
                ins.then_inc(sem(signal, j), 1)

            def flat(t):
                return t[:, :, :].rearrange("p t n -> p (t n)")

            def add_norm(s, residual_signal, residual):
                def step(j, n):
                    dve.wait_ge(sem(f"{s}_y", j), n(f"{s}_y"))
                    if residual_signal:
                        dve.wait_ge(sem(residual_signal, j), n(residual_signal))
                    link(dve.tensor_tensor(flat(r[j]), ps[j][:, 0:512], flat(residual[j]), ALU.add))
                    moments(s, j)
                    normalised(s, j, n, x[j], f"{s}_normed")
                return step

            def a0_kv(j, n):
                dve.wait_ge(sem("a0_qkv", j), n("a0_qkv"))
                dve.tensor_copy(big[j][:, 512:1536], ps[j][:, 512:1536]).then_inc(sem("a0_kT_v", j), 1)

            def a0_max(j, n):
                dve.wait_ge(sem("a0_scores", j), n("a0_scores"))
                link(dve.tensor_reduce(sm0[j][:, 4:6], tiles2(ps[j][:, 0:512], S), AX, ALU.max))
                dve.tensor_scalar(sm0[j][:, 0:2], sm0[j][:, 4:6], -HD ** -0.5, None, ALU.mult)\
                    .then_inc(sem("a0_minus_max", j), 1)

            def a0_o(j, n):
                dve.wait_ge(sem("a0_pv", j), n("a0_pv"))
                link(dve.reciprocal(sm0[j][:, 6:8], sm0[j][:, 2:4]))
                for tt in range(TT):
                    ins = dve.tensor_scalar(o0[j][:, tt, :], ps[j][:, tt * S:tt * S + S], sm0[j][:, 6 + tt:7 + tt],
                                            None, ALU.mult)
                ins.then_inc(sem("a0_o", j), 1)

            def cross_qk32(s):
                def step(j, n):
                    dve.wait_ge(sem(f"{s}_qkv", j), n(f"{s}_qkv"))
                    if s == "x0":
                        dve.tensor_copy(qk32(j, 0), ps[j][:, 0:512]).then_inc(sem("x0_q32", j), 1)
                        dve.tensor_copy(qk32(j, 1)[0:C, 0:D], ps[j][0:C, 512:512 + D]).then_inc(sem("x0_k32", j), 1)
                    else:
                        bq = rows_of["x1_bq"][:, :].unsqueeze(1).broadcast_to([P, TT, D])
                        dve.tensor_tensor(tiles2(qk32(j, 0), D), tiles2(ps[j][:, 0:512], D), bq, ALU.add)\
                            .then_inc(sem("x1_q32", j), 1)
                        dve.tensor_tensor(qk32(j, 1)[0:C, 0:D], ps[j][0:C, 512:512 + D],
                                          rows_of["x1_bk"][0:C, :], ALU.add).then_inc(sem("x1_k32", j), 1)
                        dve.tensor_tensor(rden[j][0:C, 0:D], ps[j][0:C, 1024:1024 + D],
                                          rows_of["x1_bv"][0:C, :], ALU.add).then_inc(sem("x1_v32", j), 1)
                return step

            def rope(j, n):
                dve.wait_ge(sem("m_qkv", j), n("m_qkv"))
                co = const("cos").rearrange("p (t d) -> p t d", t=TT).unsqueeze(2).broadcast_to([P, TT, H, HD])
                si = const("sin").rearrange("p (t d) -> p t d", t=TT).unsqueeze(2).broadcast_to([P, TT, H, HD])
                hd = HD // 2
                heads = lambda t: t.rearrange("p (t g d) -> p t g d", t=TT, d=HD)
                for which, c in ((0, "q"), (1, "k")):
                    src = ps[j][:, 0:1024].rearrange("p (t w g d) -> p t w g d", t=TT, w=2, d=HD)[:, :, which]
                    straight, turned = heads(rope_tmp(j, which)), heads((oT, rden)[which][j][:, :])
                    dve.tensor_tensor(straight, src, co, ALU.mult)
                    dve.tensor_tensor(turned[:, :, :, 0:hd], src[:, :, :, hd:HD], si[:, :, :, 0:hd], ALU.mult)
                    link(dve.tensor_tensor(turned[:, :, :, hd:HD], src[:, :, :, 0:hd], si[:, :, :, hd:HD], ALU.mult))
                    dve.tensor_tensor(heads(qk32(j, which)), straight, turned, ALU.add)\
                        .then_inc(sem(f"m_{c}32", j), 1)

            def repeat(j, cross, which, part, places):
                rows = C if cross and which else P
                g = H if cross and which else TT * H
                _, st = stack_view(j, which)
                for place in places:
                    dve.tensor_copy(st[0:rows, 0:g, place, :], st[0:rows, 0:g, part, :])

            def rests(s, cross):
                def step(j, n):
                    if s == "m":
                        dve.wait_ge(sem("m_k32", j), n("m_k32"))
                    for which, c in ((0, "q"), (1, "k"))[:1 if s == "m" else 2]:
                        rows = C if cross and which else P
                        g = H if cross and which else TT * H
                        _, st = stack_view(j, which)
                        src = qk32(j, which).rearrange("p (g d) -> p g d", d=HD)[0:rows, 0:g, :]
                        rest = rem(j, which).rearrange("p (g d) -> p g d", d=HD)[0:rows, 0:g, :]
                        dve.wait_ge(sem(f"{s}_{c}_part1", j), n(f"{s}_{c}_part1"))
                        dve.tensor_tensor(rest, src, st[0:rows, 0:g, 0, :], ALU.subtract)\
                            .then_inc(sem(f"{s}_{c}_rest", j), 1)
                    for which, c in ((0, "q"), (1, "k")):
                        dve.wait_ge(sem(f"{s}_{c}_part1", j), n(f"{s}_{c}_part1"))
                        repeat(j, cross, which, 0, FIRST_AGAIN[which])
                return step

            def third_parts(s, cross):
                def step(j, n):
                    for which, c in ((0, "q"), (1, "k")):
                        rows = C if cross and which else P
                        g = H if cross and which else TT * H
                        _, st = stack_view(j, which)
                        rest = rem(j, which).rearrange("p (g d) -> p g d", d=HD)[0:rows, 0:g, :]
                        second = SECOND[which]
                        dve.wait_ge(sem(f"{s}_{c}_part2", j), n(f"{s}_{c}_part2"))
                        if s == "m" and which:
                            dve.tensor_copy(st[0:rows, 0:g, 4, :], st[0:rows, 0:g, second, :])\
                                .then_inc(sem("m_k_stack", j), 1)
                            continue
                        repeat(j, cross, which, second, (4,))
                        dve.tensor_tensor(st[0:rows, 0:g, THIRD[which], :], rest, st[0:rows, 0:g, second, :],
                                          ALU.subtract).then_inc(sem(f"{s}_{c}_stack", j), 1)
                return step

            def qT_copy(s, rows):
                def step(j, n):
                    dve.wait_ge(sem(f"{s}_q_transposed", j), n(f"{s}_q_transposed"))
                    dve.tensor_copy(qkT[j][0:rows, 0, 8:16, :].rearrange("p h s -> p (h s)"),
                                    psb[j][0:rows, 2048:4096]).then_inc(sem(f"{s}_qT_dve", j), 1)
                return step

            def kT_copy(s, rows, cross):
                def step(j, n):
                    dve.wait_ge(sem(f"{s}_k_transposed", j), n(f"{s}_k_transposed"))
                    nk = C if cross else S
                    dve.tensor_copy(qkT[j][0:rows, 1, 8:16, 0:nk],
                                    psb[j][0:rows, 2048:4096].rearrange("p (h s) -> p h s", s=S)[:, :, 0:nk])\
                        .then_inc(sem(f"{s}_kT_dve", j), 1)
                return step

            def minus_max(s, j, n):
                dve.wait_ge(sem(f"{s}_max{1 if s != 'm' else 2}", j), n(f"{s}_max{1 if s != 'm' else 2}"))
                link(dve.tensor_scalar(mn[j][:, :, 0:H], mx[j][:, :, :], -1.0, None, ALU.mult))
                dve.scalar_tensor_tensor(out=mn[j][:, :, H:2 * H], in0=mx[j][:, :, :], scalar=-1.0,
                                         in1=mn[j][:, :, 0:H], op0=ALU.mult, op1=ALU.subtract)\
                    .then_inc(sem(f"{s}_minus_max", j), 1)

            def cross_max(s, tt):
                def step(j, n):
                    dve.wait_ge(sem(f"{s}_scores{tt}", j), n(f"{s}_scores{tt}"))
                    sc = ps[j][:, :].rearrange("p (a k) -> p a k", a=4)[:, :, 0:4 * C]\
                        .rearrange("p a (b c) -> p a b c", c=C)
                    if s == "x1":
                        mask = fk4[j][:, tt, :].unsqueeze(1).unsqueeze(1).broadcast_to([P, 4, 4, C])
                        link(dve.tensor_tensor(ms[j], sc, mask, ALU.add))
                        sc = ms[j]
                    dve.tensor_reduce(mx[j][:, tt, :].rearrange("p (a b) -> p a b", a=4), sc, AX, ALU.max)\
                        .then_inc(sem(f"{s}_max{tt}", j), 1)
                    if tt == 1:
                        minus_max(s, j, n)
                return step

            def causal_max(part):
                def step(j, n):
                    dve.wait_ge(sem(f"m_scores{part}", j), n(f"m_scores{part}"))
                    dst = mx[j][:, 1, 8 * part:8 * part + 8] if part < 2 else mx[j][:, 0, :]
                    dve.tensor_reduce(dst, tiles2(ps[j][:, :], S if part < 2 else P), AX, ALU.max)\
                        .then_inc(sem(f"m_max{part}", j), 1)
                    if part == 2:
                        minus_max("m", j, n)
                return step

            def mT_copy(s):
                def step(j, n):
                    dve.wait_ge(sem(f"{s}_max_transposed", j), n(f"{s}_max_transposed"))
                    dve.tensor_copy(mT[j][:, :], psb[j][:, 0:S]).then_inc(sem(f"{s}_mT", j), 1)
                return step

            def x1_mask(part):
                def step(j, n):
                    dve.wait_ge(sem(f"x1_scores_t{part}", j), n(f"x1_scores_t{part}"))
                    mask = fk4T[j][:, :].unsqueeze(1).broadcast_to([C, 8, S])
                    dve.tensor_tensor(probs(j, 0)[0:C, 8 * part:8 * part + 8, :],
                                      ps[j][0:C, :].rearrange("p (h q) -> p h q", q=S), mask, ALU.add)\
                        .then_inc(sem(f"x1_masked_t{part}", j), 1)
                return step

            def divided(s):
                def step(j, n):
                    dve.wait_ge(sem(f"{s}_pv", j), n(f"{s}_pv"))
                    dve.wait_ge(sem(f"{s}_inverse", j), n(f"{s}_inverse"))
                    dve.tensor_tensor(oT[j][:, :], ps[j][:, 0:512], rden[j][:, :], ALU.mult)\
                        .then_inc(sem(f"{s}_oT", j), 1)
                return step

            def f_round(j, n):
                k, idx, t = ffn[j][0], ffn[j][1], ffn[j][2]
                dve.wait_ge(sem("f_h256", j), n("f_h256"))
                dve.tensor_scalar(k, k, MAGIC, MAGIC, ALU.add, ALU.subtract).then_inc(sem("f_k", j), 1)
                dve.wait_ge(sem("f_k", j), n("f_k"))
                dve.tensor_scalar(t, k, -1024.0, 1024.0, ALU.max, ALU.min).then_inc(sem("f_clipped", j), 1)

            def f_index(j, n):
                idx, t = ffn[j][1], ffn[j][2]
                dve.wait_ge(sem("f_clipped", j), n("f_clipped"))
                dve.tensor_scalar(idx, t, 31.5, MAGIC64, ALU.subtract, ALU.add).then_inc(sem("f_index", j), 1)

            def f_fraction(j, n):
                k, idx, t = ffn[j][0], ffn[j][1], ffn[j][2]
                dve.wait_ge(sem("f_index", j), n("f_index"))
                dve.scalar_tensor_tensor(out=t, in0=idx, scalar=MAGIC64, in1=t, op0=ALU.subtract,
                                          op1=ALU.subtract).then_inc(sem("f_fraction", j), 1)

            def f_hidden(half):
                def step(j, n):
                    k, idx, t, left, right = (v[:, 1024 * half:1024 * half + 1024] for v in ffn[j])
                    dve.wait_ge(sem("f_right", j), n("f_right"))
                    dve.tensor_tensor(right, left, right, ALU.subtract).then_inc(sem(f"f_slope{half}", j), 1)
                    dve.wait_ge(sem(f"f_slope{half}", j), n(f"f_slope{half}"))
                    dve.tensor_tensor(right, right, t, ALU.mult).then_inc(sem(f"f_rise{half}", j), 1)
                    dve.wait_ge(sem(f"f_rise{half}", j), n(f"f_rise{half}"))
                    dve.scalar_tensor_tensor(out=right, in0=right, scalar=1.0 / 64, in1=left, op0=ALU.mult,
                                             op1=ALU.add).then_inc(sem(f"f_value{half}", j), 1)
                    dve.wait_ge(sem(f"f_value{half}", j), n(f"f_value{half}"))
                    dve.tensor_scalar(right, right, 256.0, MAGIC, ALU.mult, ALU.add)\
                        .then_inc(sem(f"f_rounded{half}", j), 1)
                    dve.wait_ge(sem(f"f_rounded{half}", j), n(f"f_rounded{half}"))
                    dve.wait_ge(sem("f_over", j), n("f_over"))
                    dve.scalar_tensor_tensor(out=k, in0=right, scalar=MAGIC, in1=k, op0=ALU.subtract, op1=ALU.add)\
                        .then_inc(sem(f"f_hT{half}", j), 1)
                return step

            def f_norm(j, n):
                dve.wait_ge(sem("f_y", j), n("f_y"))
                b2 = rows_of["f_b2"][:, :].unsqueeze(1).broadcast_to([P, TT, D])
                link(dve.tensor_tensor(r[j][:, :, :], tiles2(ps[j][:, 0:1024], 512)[:, :, 0:D], b2, ALU.add))
                link(dve.tensor_scalar(flat(r[j]), flat(r[j]), MAGIC, MAGIC, ALU.add, ALU.subtract))
                link(dve.scalar_tensor_tensor(out=flat(r[j]), in0=flat(r[j]), scalar=1.0 / 256, in1=flat(x[j]),
                                              op0=ALU.mult, op1=ALU.add))
                moments("f", j)
                normalised("f", j, n, x[j], "f_normed")

            def l_mask(kb):
                def step(j, n):
                    dve.wait_ge(sem(f"l_scores{kb}", j), n(f"l_scores{kb}"))
                    nq = S if kb == 0 else P
                    allow = const("allow")[:, 0:nq].unsqueeze(1).broadcast_to([P, H1, nq])
                    src = ps[j][:, 0:H1 * nq].rearrange("p (h q) -> p h q", q=nq)
                    dve.scalar_tensor_tensor(out=aT[j][kb], in0=src, scalar=FLT_MAX, in1=allow, op0=ALU.min,
                                             op1=ALU.mult).then_inc(sem(f"l_masked{kb}", j), 1)
                return step

            def l_mean(j, n):
                dve.wait_ge(sem("l_square_sums", j), n("l_square_sums"))
                dve.tensor_scalar(rden[j][:, :], ps[j][:, 512:1024], 1.0 / HD1, EPS, ALU.mult, ALU.add)\
                    .then_inc(sem("l_mean_square", j), 1)

            def l_scale(j, n):
                dve.wait_ge(sem("l_rms", j), n("l_rms"))
                dve.scalar_tensor_tensor(out=oT[j][:, :], in0=ps[j][:, 0:512], scalar=rmsw[:, :], in1=rden[j][:, :],
                                         op0=ALU.mult, op1=ALU.mult).then_inc(sem("l_oT", j), 1)

            def m_norm1(j, n):
                dve.wait_ge(sem("x1_normed", j), n("x1_normed"))
                for tt in range(TT):
                    ins = dve.bn_stats(bn[j][:, tt, :], x[j][:, tt, :])
                link(ins, True)
                for tt in range(TT):
                    ins = dve.bn_aggr(mv[j][:, tt, :], bn[j][:, tt, :])
                ins.then_inc(sem("n1_moments", j), 1)
                dve.wait_ge(sem("n1_rstd", j), n("n1_rstd"))
                for tt in range(TT):
                    ins = dve.tensor_scalar(h1n[j][:, tt, :], x[j][:, tt, :], mv[j][:, tt, 0:1],
                                            rstd[j][:, tt:tt + 1], ALU.subtract, ALU.mult)
                ins.then_inc(sem("m_h", j), 1)

            def m_conv(j, n):
                dve.wait_ge(sem("m_affine", j), n("m_affine"))
                for kt in range(KT):
                    ins = dve.tensor_scalar(xT[j][:, kt, :], hpad[j][:, kt, 2:S + 2], convw[:, kt, 2:3], None, ALU.mult)
                link(ins)
                for tap in (1, 0):
                    for kt in range(KT):
                        ins = dve.scalar_tensor_tensor(out=xT[j][:, kt, :], in0=hpad[j][:, kt, tap:S + tap],
                                                       scalar=convw[:, kt, tap:tap + 1], in1=xT[j][:, kt, :],
                                                       op0=ALU.mult, op1=ALU.add)
                    if tap:
                        link(ins)
                ins.then_inc(sem("m_conv", j), 1)

            def m_add(j, n):
                dve.wait_ge(sem("m_y", j), n("m_y"))
                dve.tensor_tensor(flat(r[j]), ps[j][:, 0:512], flat(x[j]), ALU.add).then_inc(sem("m_x", j), 1)

            def m_moments(j, n):
                dve.wait_ge(sem("m_x", j), n("m_x"))
                moments("n2", j)

            def m_norm2(j, n):
                dve.wait_ge(sem("n2_rstd", j), n("n2_rstd"))
                for tt in range(TT):
                    ins = dve.tensor_scalar(xb[j][:, tt, :], r[j][:, tt, :], mv[j][:, tt, 0:1],
                                            rstd[j][:, tt:tt + 1], ALU.subtract, ALU.mult)
                link(ins)
                w = rows_of["m_ln2_w"][:, :].unsqueeze(1).broadcast_to([P, TT, D])
                b = rows_of["m_ln2_b"][:, :].unsqueeze(1).broadcast_to([P, TT, D])
                link(dve.tensor_tensor(xb[j][:, :, :], xb[j][:, :, :], w, ALU.mult))
                dve.tensor_tensor(xb[j][:, :, :], xb[j][:, :, :], b, ALU.add).then_inc(sem("m_h2", j), 1)

            def m_router(j, n):
                dve.wait_ge(sem("m_h2", j), n("m_h2"))
                for tt in range(TT):
                    for e in range(E):
                        ins = dve.tensor_tensor_reduce(
                            out=oT[j][:, e % 2 * D:e % 2 * D + D], in0=xb[j][:, tt, :], in1=routw[:, e, :], scale=1.0,
                            scalar=0.0, op0=ALU.mult, op1=ALU.add, accum_out=lg[j][:, tt * E + e:tt * E + e + 1])
                        if e % 2:
                            link(ins)
                dve.tensor_copy(logits[:, bass.ds(n.of(4, TT * j), TT), :], lg[j][:, :].rearrange("p (t e) -> p t e", e=E))\
                    .then_inc(sem("m_logits", j), 1)

            def guard(j, n):
                dve.wait_ge(sem(f"rows_stored{j}"), n.stored())

            schedule = Schedule([
                (A0 + 1, a0_kv), (A0 + 2, a0_max), (A0 + 4, a0_o), (A0 + 5, add_norm("a0", "a0_residual", xb)),
                (X0, cross_qk32("x0")), (X0 + 0.5, rests("x0", True)), (X0 + 0.8, third_parts("x0", True)), (X0 + 1, qT_copy("x0", KS + 1)),
                (X0 + 2, kT_copy("x0", KS + 1, True)), (X0 + 3, cross_max("x0", 0)), (X0 + 4, cross_max("x0", 1)),
                (X0 + 5, mT_copy("x0")), (X0 + 8, divided("x0")), (X0 + 9, add_norm("x0", "x0_residual", xb)),
                (F + 0.25, f_round), (F + 0.35, f_index), 
                (F + 0.45, f_fraction), (F + 0.6, f_hidden(0)), (F + 0.6, f_hidden(1)), (L - 2, f_norm),
                (L + 1, l_mask(0)), (L + 2, l_mask(1)), (L + 4, l_mean), (L + 4.8, l_scale),
                (L + 5, add_norm("l", None, x)),
                (X1, cross_qk32("x1")), (X1 + 0.5, rests("x1", True)), (X1 + 0.8, third_parts("x1", True)), (X1 + 1, qT_copy("x1", KS)),
                (X1 + 2, kT_copy("x1", KS, True)), (X1 + 3, cross_max("x1", 0)), (X1 + 4, cross_max("x1", 1)),
                (X1 + 5, mT_copy("x1")), (X1 + 6, x1_mask(0)), (X1 + 7, x1_mask(1)), (X1 + 8, divided("x1")),
                (X1 + 9, add_norm("x1", "x1_residual", xb)), (X1 + 9, m_norm1),
                (M, m_conv), (M + 1, rope), (M + 1 + 0.5, rests("m", False)), (M + 1 + 0.8, third_parts("m", False)), (M + 2, qT_copy("m", KS)),
                (M + 3, kT_copy("m", KS, False)), (M + 4, causal_max(0)), (M + 5, causal_max(1)),
                (M + 6, causal_max(2)), (M + 7, mT_copy("m")), (M + 11, divided("m")), (M + 12, m_add), (M + 12.15, m_moments), (M + 12.3, m_norm2),
                (M + 12.5, m_router),
                (M + 13, guard)])
            chain["base"] = 0
            schedule.first(Count(dve, 0))
            first_links = chain["n"]
            with dve.Fori(0, ROUNDS - 1) as i:
                chain["n"] = first_links
                chain["base"] = dve.snap(i * DVE_LINKS)
                schedule.round(Count(dve, i))
            assert chain["n"] - first_links == DVE_LINKS, chain["n"] - first_links
            chain["n"] = first_links
            chain["base"] = (ROUNDS - 1) * DVE_LINKS
            schedule.round(Count(dve, ROUNDS - 1), last=True)

        @block.gpsimd
        def _(pool):
            for s in "qk":
                last = pool.memset(diag[s], 0.0)
            last.then_inc(sem("diag_zero"), 1)
            pool.wait_ge(setup_dma, LOADED)
            pool.wait_ge(sem("setup_act"), 1)
            pool.wait_ge(sem("setup_dve"), 1)
            pool.engine_nop().then_inc(sem("setup_pool"), 1)

            def start(j, n):
                settled_wait(pool, sem(f"inputs_loaded{j}"), n.loaded())
                pool.tensor_scalar(fk4[j][:, :, :], fkin[j][:, :, :], -4e6, None, ALU.mult).then_inc(sem("fk4", j), 1)
                pool.tensor_scalar(bkneg[j][:, :], bkin[j][:, :], NEG, None, ALU.mult)
                ab = rows_of["a0_b"][:, :].unsqueeze(1).broadcast_to([P, TT, D])
                pool.tensor_tensor(xb[j][:, :, :], xin[j][:, :, :], ab, ALU.add).then_inc(sem("a0_residual", j), 1)

            def heads(ap):
                return ap.rearrange("p (g d) -> p g d", d=HD)

            def rstd_of(s):
                def step(j, n):
                    settled_wait(pool, sem(f"{s}_moments", j), n(f"{s}_moments"))
                    pool.tensor_scalar(rstd[j][:, :], mv[j][:, :, 1], EPS, None, ALU.add)\
                        .then_inc(sem(f"{s}_variance", j), 1)
                    pool.wait_ge(sem(f"{s}_variance", j), n(f"{s}_variance"))
                    pool.tensor_tensor(rstd[j][:, :], rstd[j][:, :], const("half")[:, 0:TT], ALU.pow)\
                        .then_inc(sem(f"{s}_rstd", j), 1)
                return step

            def residual(s, prev, bias):
                def step(j, n):
                    settled_wait(pool, sem(f"{prev}_normed", j), n(f"{prev}_normed"))
                    bb = rows_of[bias][:, :].unsqueeze(1).broadcast_to([P, TT, D])
                    pool.tensor_tensor(xb[j][:, :, :], x[j][:, :, :], bb, ALU.add).then_inc(sem(f"{s}_residual", j), 1)
                return step

            def f_over(j, n):
                k = ffn[j][0]
                settled_wait(pool, sem("f_clipped", j), n("f_clipped"))
                pool.tensor_scalar(k, k, 1024.0, 0.0, ALU.subtract, ALU.max).then_inc(sem("f_over", j), 1)

            def m_k_rest(j, n):
                settled_wait(pool, sem("m_k_part1", j), n("m_k_part1"))
                pool.tensor_tensor(heads(rem(j, 1)), heads(qk32(j, 1)), stack_view(j, 1)[1][:, :, 0, :],
                                   ALU.subtract).then_inc(sem("m_k_rest", j), 1)

            def m_k_part3(j, n):
                settled_wait(pool, sem("m_k_part2", j), n("m_k_part2"))
                pool.tensor_tensor(stack_view(j, 1)[1][:, :, THIRD[1], :], heads(rem(j, 1)),
                                   stack_view(j, 1)[1][:, :, SECOND[1], :], ALU.subtract)\
                    .then_inc(sem("m_k_part3", j), 1)

            def mask_rows(j, n):
                settled_wait(pool, sem("x0_k_part1", j), n("x0_k_part1"))
                pool.memset(stack_view(j, 0)[0][:, 0:TT * H, KS:KS + 1], 1.0)
                pool.tensor_scalar(stack_view(j, 1)[0][0:C, 0:H, KS:KS + 1],
                                   cf[0:C, CF["ones"][0]:CF["ones"][0] + H].unsqueeze(2), bkneg[j][:, :], None,
                                   ALU.mult).then_inc(sem("x0_rows", j), 1)

            def l_zeros(j, n):
                settled_wait(pool, sem("f_normed", j), n("f_normed"))
                pool.memset(kF[j], 0.0).then_inc(sem("l_zeros", j), 1)

            def m_residual(j, n):
                pool.wait_ge(sem("m_x", j), n("m_x"))
                pool.tensor_tensor(x[j][:, :, :], x[j][:, :, :], r[j][:, :, :], ALU.add)\
                    .then_inc(sem("m_residual", j), 1)

            def m_pad(j, n):
                settled_wait(pool, sem("x1_normed", j), n("x1_normed"))
                pool.memset(hpad[j][:, :, 0:2], 0.0).then_inc(sem("m_pad", j), 1)

            def guard(j, n):
                settled_wait(pool, sem(f"rows_stored{j}"), n.stored())
                settled_wait(pool, sem("m_logits", j), n("m_logits"))

            schedule = Schedule([
                (A0, start), (A0 + 5, rstd_of("a0")), (A0 + 5, residual("x0", "a0", "x0_b")), (X0 + 0.5, mask_rows),
                (X0 + 9, rstd_of("x0")), (F + 0.3, f_over), (L - 2, rstd_of("f")), (L - 1, l_zeros),
                (L + 5, rstd_of("l")), (L + 5, residual("x1", "l", "x1_bo")),
                (X1 + 9, rstd_of("x1")), (X1 + 9, m_pad), (X1 + 9, rstd_of("n1")),
                (M + 1.5, m_k_rest), (M + 1.8, m_k_part3), (M + 12.2, rstd_of("n2")), (M + 12.4, m_residual), (M + 13, guard)])
            schedule.first(Count(pool, 0))
            with pool.Fori(0, ROUNDS - 1) as i:
                schedule.round(Count(pool, i))
            schedule.round(Count(pool, ROUNDS - 1), last=True)

        @block.sync
        def _(sp):
            for dst, src in loads:
                sp.dma_start(dst, src).then_inc(setup_dma, 16)
            sp.wait_ge(sem("diag_zero"), 1)
            for dst, src in diag_loads:
                sp.dma_start(dst, src).then_inc(setup_dma, 16)

            mask_bytes = a["bk"].bitcast(U8).rearrange("(b p) -> b p", p=C)

            def load(j, b):
                q = sem(f"inputs_loaded{j}")
                sp.dma_start(xin[j][:, :, :], a["x"][bass.ds(b, 1)].rearrange("b (t p) n -> p (b t) n", p=P))\
                    .then_inc(q, 16)
                sp.dma_start(cin[j][:, :], a["ctx"][bass.ds(b, 1)].rearrange("b p n -> p (b n)")).then_inc(q, 16)
                sp.dma_start(bkin[j][:, :], mask_bytes[bass.ds(b, 1)].rearrange("b p -> p b")).then_inc(q, 16)
                sp.dma_start(fkin[j][:, :, :], a["fk"][bass.ds(b, 1)].rearrange("b o (t p) n -> p (b o t) n", p=P))\
                    .then_inc(q, 16)

            def load_next(j, n):
                settled_wait(sp, sem("ctx_transposed", j), n("ctx_transposed"))
                settled_wait(sp, sem("a0_residual", j), n("a0_residual"))
                load(j, n.of(2, 2 + j))

            def store(j, n):
                q = sem(f"rows_stored{j}")
                rows = bass.ds(S * n.of(2, j), S)
                sp.wait_ge(sem("m_residual", j), n("m_residual"))
                sp.dma_start(residual_dram[rows, :].rearrange("(t p) n -> p t n", p=P), x[j][:, :, :]).then_inc(q, 16)
                sp.wait_ge(sem("m_h2", j), n("m_h2"))
                sp.dma_start(h2_dram[rows, :].rearrange("(t p) n -> p t n", p=P), xb[j][:, :, :]).then_inc(q, 16)

            for j in two:
                load(j, j)
            for dst, src in rest:
                sp.dma_start(dst, src).then_inc(sem("rest_loaded"), 16)
            schedule = Schedule([(X1, load_next), (M + 12.5, store)])
            with sp.Fori(0, ROUNDS - 1) as i:
                schedule.round(Count(sp, i))
            def load_experts(j, n):
                if j == 1:
                    sp.wait_ge(sem("f_y", 0), n.at(0)("f_y"))
                    sp.wait_ge(sem("f_y", 1), n("f_y"))
                    for e in range(E):
                        c = 2 * FFE
                        sp.dma_start(w_up[:, 0, e * c:e * c + c], a["e_up"][e][0:P, :])\
                            .then_inc(sem("experts_half"), 16)

            Schedule([(X1, load_experts), (M + 12.5, store)]).round(Count(sp, ROUNDS - 1), last=True)


def part_two(nc, a, ctx, sb, sem, ps, w_up, const, ident, logits, residual_dram, h2_dram, token_dram, out):
    w_down = sb("w_down", [P, FFE // P, E * D])
    top = sb("top", [P, NT])
    oh = sb("oh", [P, NT, E])
    free = sb("free", [P, NT])
    before = sb("before", [P, NT + 1, E])
    fills = sb("fills", [P, E, NT])
    ntile = sb("ntile", [P, E])
    base = sb("base", [P, E])
    place = sb("place", [P, NT, E])
    row = sb("row", [P, NT])
    row_i = sb("row_i", [P, NT], I32)
    token_i = sb("token_i", [P, NT], I32)
    nobody = sb("nobody", [P, TILES], I32)
    expert = sb("expert", [P, TILES])
    expert_i = sb("expert_i", [P, TILES], I32)
    tokens_i = sb("tokens_i", [TILES, P], I32)
    tokens = sb("tokens", [TILES, P])
    target = sb("target", [P, TILES], I32)
    source = sb("source", [P, TILES], I32)
    idx_h = sb("idx_h", [P, 1], I32)
    idx_x = sb("idx_x", [P, 1], I32)
    idx_o = sb("idx_o", [P, 1], I32)
    hg = sb("hg", [P, D])
    xg = sb("xg", [P, D])
    hT = sb("hT", [P, KT, P])
    silu = sb("silu", [P, FFE])
    hid = sb("hid", [P, FFE])
    hidT = sb("hidT", [P, FFE])
    total = sb("total", [P, D])
    bn2 = sb("bn2", [P, 6])
    mv2 = sb("mv2", [P, 2])
    rs2 = sb("rs2", [P, 1])
    result = sb("result", [P, D])

    settled_wait = settler(sem)
    block = ctx.enter_context(nc.Block())

    def load_experts(engine, experts, signal):
        engine.wait_ge(sem("cleared"), 16)
        done = 0
        for e in experts:
            c = 2 * FFE
            for dst, src in ((w_up[:, 1, e * c:e * c + c], a["e_up"][e][P:D, :]),
                             (w_down[:, :, e * D:e * D + D],
                              a["e_down"][e].rearrange("(t p) n -> p t n", p=P))):
                if done:
                    engine.wait_ge(sem(signal), done)
                engine.dma_start(dst, src).then_inc(sem(signal), 16)
                done += 16

    @block.sync
    def _(sp):
        load_experts(sp, range(0, E, 2), "even_experts")

    @block.tensor
    def _(pe):
        pe.wait_ge(sem("one_expert"), 1)
        flat = oh[:, :, :].rearrange("p t e -> p (t e)")
        pe.matmul(ps[0][:, 0:NT * E], const("upper"), flat, start=True, stop=True)
        pe.matmul(ps[1][:, 0:NT * E], const("ones"), flat, start=True, stop=True).then_inc(sem("counts"), 1)
        pe.wait_ge(sem("rows_known"), 1)
        pe.wait_ge(sem("tokens_float"), 1)
        pe.transpose(ps[0][:, 0:TILES], tokens[:, :], ident[0:TILES, 0:TILES]).then_inc(sem("tokens_by_tile"), 1)
        pe.wait_ge(sem("sources"), 1)
        pe.wait_ge(sem("experts_half"), 16 * E)
        pe.wait_ge(sem("even_experts"), 16 * E)
        pe.wait_ge(sem("odd_experts"), 16 * E)

        def turn(n16):
            pe.wait_ge(sem("h_gathered"), n16)
            for kt in range(KT):
                mm = pe.transpose(ps[1][:, P * kt:P * kt + P], hg[:, P * kt:P * kt + P], ident)
            mm.then_inc(sem("h_turned"), 1)

        def turn_hidden(n):
            pe.wait_ge(sem("expert_hidden"), n)
            for m in range(FFE // P):
                mm = pe.transpose(ps[1][:, 512 + P * m:512 + P * m + P], hid[:, P * m:P * m + P], ident)
            mm.then_inc(sem("hidden_turned"), 1)

        def up(n, e):
            pe.wait_ge(sem("hT"), n)
            for c in range(4):
                for kt in range(KT):
                    mm = pe.matmul(ps[0][:, 512 * c:512 * c + 512], hT[:, kt, :],
                                   w_up[:, kt, bass.ds(e * (2 * FFE) + 512 * c, 512)],
                                   start=kt == 0, stop=kt == KT - 1)
            mm.then_inc(sem("up"), 1)

        def down(n, e):
            pe.wait_ge(sem("hidT_act"), n)
            pe.wait_ge(sem("hidT_dve"), n)
            for m in range(FFE // P):
                mm = pe.matmul(ps[1][:, 1536:1536 + D], hidT[:, P * m:P * m + P],
                               w_down[:, m, bass.ds(e * D, D)], start=m == 0, stop=m == FFE // P - 1)
            mm.then_inc(sem("expert_y"), 1)

        def expert_of(t):
            return pe.value_load(expert_i[0:1, t], min_val=0, max_val=E - 1)

        turn(16)
        up(1, expert_of(slice(0, 1)))
        with pe.Fori(1, TILES) as t:
            n, prev = pe.snap(t + 1), t
            turn(pe.snap(16 * t + 16))
            turn_hidden(prev)
            up(n, expert_of(bass.ds(t, 1)))
            down(prev, expert_of(bass.ds(t - 1, 1)))
        turn_hidden(TILES)
        down(TILES, expert_of(slice(TILES - 1, TILES)))

    @block.scalar
    def _(act):
        load_experts(act, range(1, E, 2), "odd_experts")

        def copy_hT(n):
            act.wait_ge(sem("h_turned"), n)
            act.activation(hT[:, :, :].rearrange("p t s -> p (t s)"), ps[1][:, 0:D], ACT.Copy)\
                .then_inc(sem("hT"), 1)

        def copy_hidT(n):
            act.wait_ge(sem("hidden_turned"), n)
            act.activation(hidT[:, 0:512], ps[1][:, 512:1024], ACT.Copy).then_inc(sem("hidT_act"), 1)

        def gate(n):
            act.wait_ge(sem("up"), n)
            act.activation(silu[:, :], ps[0][:, 0:FFE], ACT.Silu).then_inc(sem("silu"), 1)

        copy_hT(1)
        gate(1)
        with act.Fori(1, TILES) as t:
            n = act.snap(t + 1)
            copy_hT(n)
            copy_hidT(t)
            gate(n)
        copy_hidT(TILES)

    @block.vector
    def _(dve):
        done = {"n": 0}

        def link(ins):
            done["n"] += 1
            ins.then_inc(sem("routing_chain"), 1)
            dve.wait_ge(sem("routing_chain"), done["n"])

        dve.memset(nobody[:, :], N).then_inc(sem("ids"), 1)
        link(dve.tensor_reduce(top[:, :], logits[:, :, :], AX, ALU.max))
        link(dve.tensor_tensor(oh[:, :, :], logits[:, :, :], top[:, :].unsqueeze(2).broadcast_to([P, NT, E]),
                               ALU.is_ge))
        link(dve.tensor_scalar(free[:, :], oh[:, :, 0], -1.0, 1.0, ALU.mult, ALU.add))
        for e in range(1, E - 1):
            link(dve.tensor_tensor(oh[:, :, e], oh[:, :, e], free[:, :], ALU.mult))
            link(dve.tensor_tensor(free[:, :], free[:, :], oh[:, :, e], ALU.subtract))
        dve.tensor_copy(oh[:, :, E - 1], free[:, :]).then_inc(sem("one_expert"), 1)
        dve.tensor_copy(token_i[:, :], const("token"))
        dve.memset(before[:, 0, :], 0.0)
        link(dve.memset(base[:, :], 0.0))
        dve.wait_ge(sem("counts"), 1)
        tot = ps[1][:, 0:NT * E].rearrange("p (t e) -> p t e", e=E)
        for t in range(NT):
            link(dve.tensor_tensor(before[:, t + 1, :], tot[:, t, :], before[:, t, :], ALU.add))
        link(dve.tensor_tensor(fills[:, :, :], before[:, NT, :].unsqueeze(2).broadcast_to([P, E, NT]),
                               const("kth").unsqueeze(1).broadcast_to([P, E, NT]), ALU.is_gt))
        link(dve.tensor_reduce(ntile[:, :], fills[:, :, :], AX, ALU.add))
        for e in range(1, E):
            link(dve.tensor_tensor(base[:, e:e + 1], base[:, e - 1:e], ntile[:, e - 1:e], ALU.add))
        link(dve.tensor_tensor(place[:, :, :], ps[0][:, 0:NT * E].rearrange("p (t e) -> p t e", e=E),
                               before[:, 0:NT, :], ALU.add))
        link(dve.scalar_tensor_tensor(out=place[:, :, :], in0=base[:, :].unsqueeze(1).broadcast_to([P, NT, E]),
                                      scalar=float(P), in1=place[:, :, :], op0=ALU.mult, op1=ALU.add))
        link(dve.tensor_tensor(place[:, :, :], place[:, :, :], oh[:, :, :], ALU.mult))
        link(dve.tensor_reduce(row[:, :], place[:, :, :], AX, ALU.add))
        dve.tensor_copy(row_i[:, :], row[:, :]).then_inc(sem("row_of_token"), 1)
        link(dve.tensor_scalar(expert[:, :], const("tile"), base[:, 1:2], None, ALU.is_ge))
        for e in range(2, E):
            link(dve.scalar_tensor_tensor(out=expert[:, :], in0=const("tile"), scalar=base[:, e:e + 1],
                                          in1=expert[:, :], op0=ALU.is_ge, op1=ALU.add))
        dve.tensor_copy(expert_i[:, :], expert[:, :]).then_inc(sem("rows_known"), 1)
        dve.wait_ge(sem("tokens_read"), 16)
        dve.tensor_copy(tokens[:, :], tokens_i[:, :]).then_inc(sem("tokens_float"), 1)
        dve.wait_ge(sem("tokens_by_tile"), 1)
        dve.tensor_copy(target[:, :], ps[0][:, 0:TILES])
        dve.tensor_scalar(source[:, :], ps[0][:, 0:TILES], float(N - 1), None, ALU.min).then_inc(sem("sources"), 1)

        def copy_hidT(n):
            dve.wait_ge(sem("hidden_turned"), n)
            dve.tensor_copy(hidT[:, 512:1024], ps[1][:, 1024:1536]).then_inc(sem("hidT_dve"), 1)

        def gated(n, prev):
            dve.wait_ge(sem("silu"), n)
            if prev is not None:
                dve.wait_ge(sem("hidden_turned"), prev)
            dve.tensor_tensor(hid[:, :], ps[0][:, FFE:2 * FFE], silu[:, :], ALU.mult).then_inc(sem("expert_hidden"), 1)

        def finish(n, n16):
            dve.wait_ge(sem("expert_y"), n)
            dve.wait_ge(sem("x_gathered"), n16)
            dve.tensor_tensor(total[:, :], ps[1][:, 1536:1536 + D], xg[:, :], ALU.add).then_inc(sem("total"), 1)
            dve.wait_ge(sem("total"), n)
            dve.bn_stats(bn2[:, :], total[:, :]).then_inc(sem("stats"), 1)
            settled_wait(dve, sem("stats"), n)
            dve.bn_aggr(mv2[:, :], bn2[:, :]).then_inc(sem("last_moments"), 1)
            dve.wait_ge(sem("last_rstd"), n)

        def write_result(scattered):
            if scattered is not None:
                dve.wait_ge(sem("scattered"), scattered)
            dve.tensor_scalar(result[:, :], total[:, :], mv2[:, 0:1], rs2[:, 0:1], ALU.subtract, ALU.mult)\
                .then_inc(sem("result"), 1)

        gated(1, None)
        copy_hidT(1)
        gated(2, 1)
        finish(1, 16)
        write_result(None)
        with dve.Fori(2, TILES) as t:
            n, n16 = dve.snap(t + 1), dve.snap(16 * t)
            copy_hidT(t)
            gated(n, t)
            finish(t, n16)
            write_result(dve.snap(16 * t - 16))
        copy_hidT(TILES)
        finish(TILES, 16 * TILES)
        write_result(16 * TILES - 16)

    @block.gpsimd
    def _(pool):
        pool.wait_ge(sem("ids"), 1)
        pool.dma_start(token_dram.rearrange("(p t) o -> p (t o)", p=P), nobody[:, :]).then_inc(sem("cleared"), 16)
        pool.wait_ge(sem("cleared"), 16)
        pool.wait_ge(sem("row_of_token"), 1)
        for t in range(NT):
            pool.indirect_dma_start(out=token_dram, out_offset=bass.IndirectOffsetOnAxis(ap=row_i[:, t:t + 1], axis=0),
                                    in_=token_i[:, t:t + 1], in_offset=None, bounds_check=ROWS - 1,
                                    oob_is_err=True).then_inc(sem("tokens_written"), 16)
        pool.wait_ge(sem("tokens_written"), 16 * NT)
        pool.dma_start(tokens_i[:, :], token_dram.rearrange("(t p) o -> t (p o)", p=P)).then_inc(sem("tokens_read"), 16)
        pool.wait_ge(sem("sources"), 1)

        def gather(dst, table, idx, t, signal, copied, n):
            pool.tensor_copy(idx[:, :], source[:, t]).then_inc(sem(copied), 1)
            settled_wait(pool, sem(copied), n)
            pool.indirect_dma_start(out=dst[:, :], out_offset=None, in_=table,
                                    in_offset=bass.IndirectOffsetOnAxis(ap=idx[:, :], axis=0),
                                    bounds_check=N - 1, oob_is_err=True).then_inc(sem(signal), 16)

        def rstd(n):
            settled_wait(pool, sem("last_moments"), n)
            pool.tensor_scalar(rs2[:, :], mv2[:, 1:2], EPS, None, ALU.add).then_inc(sem("last_variance"), 1)
            pool.wait_ge(sem("last_variance"), n)
            pool.tensor_tensor(rs2[:, :], rs2[:, :], const("half")[:, 0:1], ALU.pow).then_inc(sem("last_rstd"), 1)

        def scatter(t, n):
            pool.tensor_copy(idx_o[:, :], target[:, t]).then_inc(sem("o_index"), 1)
            pool.wait_ge(sem("o_index"), n)
            settled_wait(pool, sem("result"), n)
            pool.indirect_dma_start(out=out, out_offset=bass.IndirectOffsetOnAxis(ap=idx_o[:, :], axis=0),
                                    in_=result[:, :], in_offset=None, bounds_check=N - 1, oob_is_err=False)\
                .then_inc(sem("scattered"), 16)

        gather(hg, h2_dram, idx_h, slice(0, 1), "h_gathered", "h_index", 1)
        gather(xg, residual_dram, idx_x, slice(0, 1), "x_gathered", "x_index", 1)
        pool.wait_ge(sem("h_turned"), 1)
        gather(hg, h2_dram, idx_h, slice(1, 2), "h_gathered", "h_index", 2)
        pool.wait_ge(sem("h_turned"), 2)
        gather(hg, h2_dram, idx_h, slice(2, 3), "h_gathered", "h_index", 3)
        rstd(1)
        scatter(slice(0, 1), 1)
        gather(xg, residual_dram, idx_x, slice(1, 2), "x_gathered", "x_index", 2)
        with pool.Fori(2, TILES - 1) as t:
            n = pool.snap(t + 1)
            settled_wait(pool, sem("h_turned"), n)
            gather(hg, h2_dram, idx_h, bass.ds(t + 1, 1), "h_gathered", "h_index", pool.snap(t + 2))
            rstd(t)
            settled_wait(pool, sem("scattered"), 16 * t - 16)
            scatter(bass.ds(t - 1, 1), t)
            gather(xg, residual_dram, idx_x, bass.ds(t, 1), "x_gathered", "x_index", n)
        rstd(TILES - 1)
        pool.wait_ge(sem("scattered"), 16 * TILES - 32)
        scatter(slice(TILES - 2, TILES - 1), TILES - 1)
        gather(xg, residual_dram, idx_x, slice(TILES - 1, TILES), "x_gathered", "x_index", TILES)
        rstd(TILES)
        pool.wait_ge(sem("scattered"), 16 * TILES - 16)
        scatter(slice(TILES - 1, TILES), TILES)
        pool.wait_ge(sem("scattered"), 16 * TILES)


def kernel(**inputs):
    import numpy as _np
    import concourse.bacc as _bacc
    from concourse import mybir as _mybir
    from concourse.bass_utils import run_bass_kernel_spmd as _run

    g = {k: _np.asarray(v) for k, v in inputs.items()}
    cf, cb = shape_constants()
    host = {
        "x": g["x"], "ctx": g["ctx_1024"], "bk": _np.ascontiguousarray(g["mask_BxS2_bk0"]).reshape(-1).view(_np.int32), "fk": g["mask_Bx1xSxS2_fk0"],
        "cf": cf, "cb": cb,
        "a0_qkv": g["L0_attn_w_qkv"].T, "a0_proj": g["L0_attn_w_proj"].T, "a0_b": g["L0_attn_b_proj"],
        "x0_q": g["L0_xattn_Wq"], "x0_kv": g["L0_xattn_Wkv"], "x0_proj": g["L0_xattn_Wproj"],
        "x0_b": g["L0_xattn_bproj"],
        "f_w1": g["L0_ffn_w1"], "f_b1": g["L0_ffn_b1"].reshape(FF0 // P, P).T, "f_w2": g["L0_ffn_w2"], "f_b2": g["L0_ffn_b2"],
        "a1_q": g["L1_attn_Wq"], "a1_k": g["L1_attn_Wk"], "a1_v": g["L1_attn_Wv"].T, "a1_o": g["L1_attn_Wo"].T,
        "a1_fmqT": g["L1_attn_fmq_w"].T, "a1_fmq_b": g["L1_attn_fmq_b"],
        "a1_fmkT": g["L1_attn_fmk_w"].T, "a1_fmk_b": g["L1_attn_fmk_b"], "a1_rms": g["L1_attn_rms_w"],
        "x1_q": g["L1_xattn_Wq"].T, "x1_bq": g["L1_xattn_bq"], "x1_k": g["L1_xattn_Wk"].T,
        "x1_bk": g["L1_xattn_bk"], "x1_v": g["L1_xattn_Wv"].T, "x1_bv": g["L1_xattn_bv"],
        "x1_o": g["L1_xattn_Wo"].T, "x1_bo": g["L1_xattn_bo"],
        "m_ln1_w": g["L1_ffn_ln1_w"].reshape(KT, P).T, "m_ln1_b": g["L1_ffn_ln1_b"].reshape(KT, P).T, "m_ln2_w": g["L1_ffn_ln2_w"],
        "m_ln2_b": g["L1_ffn_ln2_b"], "m_conv": g["L1_ffn_conv_w"].reshape(KT, P, 3).transpose(1, 0, 2), "m_qkv": g["L1_ffn_attn_w"],
        "m_proj": g["L1_ffn_proj_w"], "m_router": g["L1_ffn_router_w"].T,
        "e_up": g["L1_ffn_expert_wv"], "e_down": g["L1_ffn_expert_proj"],
    }
    nc = _bacc.Bacc("TRN2", target_bir_lowering=False, num_devices=1)
    arrays, aps = {}, {}
    for name, v in host.items():
        v = _np.ascontiguousarray(v)
        arrays[f"in_{name}"] = v
        aps[name] = nc.dram_tensor(f"in_{name}", v.shape, _mybir.dt.from_np(v.dtype), kind="ExternalInput").ap()
    out = nc.dram_tensor("out_rows", (N, D), F32, kind="ExternalOutput").ap()
    decoder(nc, aps, out)
    r = _run(nc, [arrays], core_ids=[0])
    return r.results[0]["out_rows"].reshape(B, S, D)
```
